# Optimizing a Trainium2 kernel written in Bass

```python
import numpy as np
import jax
import jax.numpy as jnp

def _softmax(x, axis=-1):
    return jax.nn.softmax(x, axis=axis)

def _gelu(x):
    return jax.nn.gelu(x, approximate=True)

def _silu(x):
    return jax.nn.silu(x)

def _sigmoid(x):
    return jax.nn.sigmoid(x)

def _layernorm(x, axis=-1, eps=1e-05):
    m = jnp.mean(x, axis=axis, keepdims=True)
    v = jnp.var(x, axis=axis, keepdims=True)
    return (x - m) / jnp.sqrt(v + eps)

def _scatter_add(tgt, idx, src, axis=0):
    return tgt.at[idx].add(src)

def _segment_sum(src, seg, n):
    return jax.ops.segment_sum(src, seg, n)
kernel_name = 'mk_vit_tower_d1_tok_img768_r4_592249'

def setup_inputs(seed: int=0):
    np.random.seed(seed)
    _w = jnp.asarray

    def _rec_inputs():
        import jax
        import jax.numpy as jnp
        _rk = jax.random.key(seed)
        x = -0.000596345 + 1.00056 * jax.random.normal(jax.random.fold_in(_rk, 1), (8, 3, 64, 64), jnp.float32)
        return x
    x = _rec_inputs()

    def _L0_tok_setup():
        import jax, jax.numpy as jnp
        import numpy as np
        B = 16
        IMG = 64
        CH = 3
        EMBED = 64
        GP = 16
        PRE = [1, 2, 4]
        N_LEVELS = 3
        FUSED = EMBED * N_LEVELS

        def hilbert_flat_indices(n):
            t = np.arange(n * n, dtype=np.int64)
            x = np.zeros(n * n, dtype=np.int64)
            y = np.zeros(n * n, dtype=np.int64)
            s = 1
            while s < n:
                rx = 1 & t // 2
                ry = 1 & (t ^ rx)
                swap = ry == 0
                flip = swap & (rx == 1)
                x = np.where(flip, s - 1 - x, x)
                y = np.where(flip, s - 1 - y, y)
                x2 = np.where(swap, y, x)
                y2 = np.where(swap, x, y)
                x, y = (x2, y2)
                x = x + s * rx
                y = y + s * ry
                t = t // 4
                s *= 2
            return y * n + x

        def _level(x, idx, W, b, p, gp):
            Bsz, C, H, _ = x.shape
            h = H // p
            t = x.reshape(Bsz, C, h, p, h, p).transpose(0, 2, 4, 3, 5, 1).reshape(Bsz, h * h, p * p * C)
            t = t[:, idx]
            t = t.reshape(Bsz, h * h // gp, gp * p * p * C)
            return t @ W.T + b

        def _interp_linear(x, n_out):
            L = x.shape[1]
            pos = (jnp.arange(n_out, dtype=jnp.float32) + 0.5) * (L / n_out) - 0.5
            pos = jnp.clip(pos, 0.0, L - 1)
            i0 = jnp.floor(pos).astype(jnp.int32)
            i1 = jnp.minimum(i0 + 1, L - 1)
            w = (pos - i0).astype(x.dtype)
            return x[:, i0] * (1.0 - w)[None, :, None] + x[:, i1] * w[None, :, None]
        key = jax.random.key(seed)
        ks = jax.random.split(key, 9)
        inp = {'x': jax.random.normal(ks[0], (B, CH, IMG, IMG), jnp.float32)}
        for i, p in enumerate(PRE):
            din = CH * p * p * GP
            inp[f'W{i}'] = jax.random.normal(ks[1 + 2 * i], (EMBED, din), jnp.float32) * din ** (-0.5)
            inp[f'b{i}'] = jax.random.normal(ks[2 + 2 * i], (EMBED,), jnp.float32) * 0.02
        inp['Wf'] = jax.random.normal(ks[7], (FUSED, FUSED), jnp.float32) * FUSED ** (-0.5)
        inp['bf'] = jax.random.normal(ks[8], (FUSED,), jnp.float32) * 0.02
        for i, p in enumerate(PRE):
            inp[f'idx{i}'] = jnp.asarray(hilbert_flat_indices(IMG // p), jnp.int32)
        return inp
    _L0_tok_all = _L0_tok_setup()
    _L0_tok_in = {k: v for k, v in _L0_tok_all.items() if k in ('W0', 'b0', 'W1', 'b1', 'W2', 'b2', 'Wf', 'bf', 'idx0', 'idx1', 'idx2')}
    del _L0_tok_all

    def _L0_attn_setup():
        import jax, jax.numpy as jnp
        import numpy as np
        EPS = 1e-06
        H = 12

        def _phi(x):
            return jax.nn.elu(x) + 1.0
        key = jax.random.key(seed)
        k1, k2, k3 = jax.random.split(key, 3)
        B, N, D = (32, 256, 192)
        x = jax.random.normal(k1, (B, N, D), dtype=jnp.float32)
        W_qkv = jax.random.normal(k2, (D, 3 * D), dtype=jnp.float32) * D ** (-0.5)
        W_out = jax.random.normal(k3, (D, D), dtype=jnp.float32) * D ** (-0.5)
        b_out = jnp.zeros((D,), dtype=jnp.float32)
        return {'x': x, 'W_qkv': W_qkv, 'W_out': W_out, 'b_out': b_out}
    _L0_attn_all = _L0_attn_setup()
    _L0_attn_in = {k: v for k, v in _L0_attn_all.items() if k in ('W_qkv', 'W_out', 'b_out')}
    del _L0_attn_all

    def _L0_ffn_setup():
        import jax, jax.numpy as jnp
        import numpy as np
        E = 16
        K = 4
        H = 192
        I = 384
        LIMIT = 7.0
        ALPHA = 1.702
        EPS = 1e-05

        def rmsnorm(x, scale):
            xf = x.astype(jnp.float32)
            inv = jax.lax.rsqrt(jnp.mean(xf * xf, axis=-1, keepdims=True) + EPS)
            return (xf * inv).astype(x.dtype) * scale

        def swiglu(x, limit=LIMIT, alpha=ALPHA):
            x_glu = x[..., ::2]
            x_lin = x[..., 1::2]
            x_glu = jnp.minimum(x_glu, limit)
            x_lin = jnp.clip(x_lin, -limit, limit)
            return x_glu * jax.nn.sigmoid(alpha * x_glu) * (x_lin + 1.0)
        key = jax.random.key(seed)
        ks = jax.random.split(key, 7)
        s = 0.02
        return {'x': jax.random.normal(ks[0], (2, 256, H), dtype=jnp.float32), 'norm_scale': jnp.ones((H,), dtype=jnp.float32), 'gate_w': jax.random.normal(ks[1], (E, H), dtype=jnp.float32) * s, 'gate_b': jnp.zeros((E,), dtype=jnp.float32), 'mlp1_w': jax.random.normal(ks[2], (E, 2 * I, H), dtype=jnp.float32) * s, 'mlp1_b': jax.random.normal(ks[3], (E, 2 * I), dtype=jnp.float32) * s, 'mlp2_w': jax.random.normal(ks[4], (E, H, I), dtype=jnp.float32) * s, 'mlp2_b': jax.random.normal(ks[5], (E, H), dtype=jnp.float32) * s}
    _L0_ffn_all = _L0_ffn_setup()
    _L0_ffn_in = {k: v for k, v in _L0_ffn_all.items() if k in ('norm_scale', 'gate_w', 'gate_b', 'mlp1_w', 'mlp1_b', 'mlp2_w', 'mlp2_b')}
    del _L0_ffn_all
    return {'x': x, 'L0_tok_W0': _L0_tok_in['W0'], 'L0_tok_b0': _L0_tok_in['b0'], 'L0_tok_W1': _L0_tok_in['W1'], 'L0_tok_b1': _L0_tok_in['b1'], 'L0_tok_W2': _L0_tok_in['W2'], 'L0_tok_b2': _L0_tok_in['b2'], 'L0_tok_Wf': _L0_tok_in['Wf'], 'L0_tok_bf': _L0_tok_in['bf'], 'L0_tok_idx0': _L0_tok_in['idx0'], 'L0_tok_idx1': _L0_tok_in['idx1'], 'L0_tok_idx2': _L0_tok_in['idx2'], 'L0_attn_W_qkv': _L0_attn_in['W_qkv'], 'L0_attn_W_out': _L0_attn_in['W_out'], 'L0_attn_b_out': _L0_attn_in['b_out'], 'L0_ffn_norm_scale': _L0_ffn_in['norm_scale'], 'L0_ffn_gate_w': _L0_ffn_in['gate_w'], 'L0_ffn_gate_b': _L0_ffn_in['gate_b'], 'L0_ffn_mlp1_w': _L0_ffn_in['mlp1_w'], 'L0_ffn_mlp1_b': _L0_ffn_in['mlp1_b'], 'L0_ffn_mlp2_w': _L0_ffn_in['mlp2_w'], 'L0_ffn_mlp2_b': _L0_ffn_in['mlp2_b']}

def reference(x, L0_tok_W0, L0_tok_b0, L0_tok_W1, L0_tok_b1, L0_tok_W2, L0_tok_b2, L0_tok_Wf, L0_tok_bf, L0_tok_idx0, L0_tok_idx1, L0_tok_idx2, L0_attn_W_qkv, L0_attn_W_out, L0_attn_b_out, L0_ffn_norm_scale, L0_ffn_gate_w, L0_ffn_gate_b, L0_ffn_mlp1_w, L0_ffn_mlp1_b, L0_ffn_mlp2_w, L0_ffn_mlp2_b):
    import jax
    import jax.numpy as jnp

    def _L0_tok_ref(x, W0, b0, W1, b1, W2, b2, Wf, bf, idx0, idx1, idx2):
        import jax, jax.numpy as jnp
        import numpy as np
        B = 16
        IMG = 64
        CH = 3
        EMBED = 64
        GP = 16
        PRE = [1, 2, 4]
        N_LEVELS = 3
        FUSED = EMBED * N_LEVELS

        def hilbert_flat_indices(n):
            t = np.arange(n * n, dtype=np.int64)
            x = np.zeros(n * n, dtype=np.int64)
            y = np.zeros(n * n, dtype=np.int64)
            s = 1
            while s < n:
                rx = 1 & t // 2
                ry = 1 & (t ^ rx)
                swap = ry == 0
                flip = swap & (rx == 1)
                x = np.where(flip, s - 1 - x, x)
                y = np.where(flip, s - 1 - y, y)
                x2 = np.where(swap, y, x)
                y2 = np.where(swap, x, y)
                x, y = (x2, y2)
                x = x + s * rx
                y = y + s * ry
                t = t // 4
                s *= 2
            return y * n + x

        def _level(x, idx, W, b, p, gp):
            Bsz, C, H, _ = x.shape
            h = H // p
            t = x.reshape(Bsz, C, h, p, h, p).transpose(0, 2, 4, 3, 5, 1).reshape(Bsz, h * h, p * p * C)
            t = t[:, idx]
            t = t.reshape(Bsz, h * h // gp, gp * p * p * C)
            return t @ W.T + b

        def _interp_linear(x, n_out):
            L = x.shape[1]
            pos = (jnp.arange(n_out, dtype=jnp.float32) + 0.5) * (L / n_out) - 0.5
            pos = jnp.clip(pos, 0.0, L - 1)
            i0 = jnp.floor(pos).astype(jnp.int32)
            i1 = jnp.minimum(i0 + 1, L - 1)
            w = (pos - i0).astype(x.dtype)
            return x[:, i0] * (1.0 - w)[None, :, None] + x[:, i1] * w[None, :, None]
        Ws = [(idx0, W0, b0, PRE[0]), (idx1, W1, b1, PRE[1]), (idx2, W2, b2, PRE[2])]
        outs = [_level(x, idx, W, b, p, GP) for idx, W, b, p in Ws]
        n_tokens = outs[0].shape[1]
        outs = [outs[0]] + [_interp_linear(o, n_tokens) for o in outs[1:]]
        y = jnp.concatenate(outs, axis=-1)
        return y @ Wf.T + bf

    def _L0_attn_ref(x, W_qkv, W_out, b_out):
        import jax, jax.numpy as jnp
        import numpy as np
        EPS = 1e-06
        H = 12

        def _phi(x):
            return jax.nn.elu(x) + 1.0
        B, N, D = x.shape
        d = D // H
        x_ = jnp.pad(x, ((0, 0), (0, 1), (0, 0)))
        qkv = x_ @ W_qkv
        q, k, v = jnp.split(qkv, 3, axis=-1)
        q = q.reshape(B, N + 1, H, d)
        k = k.reshape(B, N + 1, H, d)
        v = v.reshape(B, N + 1, H, d)
        q = _phi(q)
        k = _phi(k)
        kv = jnp.einsum('bshd,bshm->bhdm', k, v)
        z = 1.0 / (jnp.einsum('blhd,bhd->blh', q, k.sum(axis=1)) + EPS)
        out = jnp.einsum('blhd,bhdm,blh->blhm', q, kv, z)
        out = out.reshape(B, N + 1, D)
        out = out @ W_out + b_out
        return out[:, :-1, :]

    def _L0_ffn_ref(x, norm_scale, gate_w, gate_b, mlp1_w, mlp1_b, mlp2_w, mlp2_b):
        import jax, jax.numpy as jnp
        import numpy as np
        E = 16
        K = 4
        H = 192
        I = 384
        LIMIT = 7.0
        ALPHA = 1.702
        EPS = 1e-05

        def rmsnorm(x, scale):
            xf = x.astype(jnp.float32)
            inv = jax.lax.rsqrt(jnp.mean(xf * xf, axis=-1, keepdims=True) + EPS)
            return (xf * inv).astype(x.dtype) * scale

        def swiglu(x, limit=LIMIT, alpha=ALPHA):
            x_glu = x[..., ::2]
            x_lin = x[..., 1::2]
            x_glu = jnp.minimum(x_glu, limit)
            x_lin = jnp.clip(x_lin, -limit, limit)
            return x_glu * jax.nn.sigmoid(alpha * x_glu) * (x_lin + 1.0)
        B, T, _ = x.shape
        t = rmsnorm(x, norm_scale)
        g = jnp.einsum('bth,eh->bte', t, gate_w) + gate_b
        top_vals, top_idx = jax.lax.top_k(g, K)
        route_w = jax.nn.softmax(top_vals, axis=-1)
        t_flat = t.reshape(B * T, H)
        idx_flat = top_idx.reshape(B * T, K)
        w_flat = route_w.reshape(B * T, K)
        onehot = jax.nn.one_hot(idx_flat, E, dtype=t_flat.dtype)
        comb = jnp.einsum('nke,nk->ne', onehot, w_flat)
        h = jnp.einsum('nh,ech->nec', t_flat, mlp1_w) + mlp1_b
        a = swiglu(h)
        y = jnp.einsum('nec,ehc->neh', a, mlp2_w) + mlp2_b
        out_flat = jnp.einsum('neh,ne->nh', y, comb)
        return x + out_flat.reshape(B, T, H)
    h = _L0_tok_ref(x, L0_tok_W0, L0_tok_b0, L0_tok_W1, L0_tok_b1, L0_tok_W2, L0_tok_b2, L0_tok_Wf, L0_tok_bf, L0_tok_idx0, L0_tok_idx1, L0_tok_idx2)
    h = h + _L0_attn_ref(_layernorm(h, axis=-1), L0_attn_W_qkv, L0_attn_W_out, L0_attn_b_out)
    h = h + _L0_ffn_ref(_layernorm(h, axis=-1), L0_ffn_norm_scale, L0_ffn_gate_w, L0_ffn_gate_b, L0_ffn_mlp1_w, L0_ffn_mlp1_b, L0_ffn_mlp2_w, L0_ffn_mlp2_b)
    return h

_drawn_inputs = setup_inputs


def setup_inputs(seed=0):
    import zlib

    import numpy as np

    out = dict(_drawn_inputs(seed))
    spreads = {'L0_attn_b_out': (0.0, 0.1), 'L0_ffn_norm_scale': (1.0, 0.6), 'L0_ffn_gate_b': (0.0, 0.8)}
    factors = {'L0_tok_b0': 2.902,
     'L0_tok_b1': 3.075,
     'L0_tok_b2': 2.955,
     'L0_ffn_gate_w': 3.867,
     'L0_ffn_mlp1_w': 3.491,
     'L0_ffn_mlp1_b': 8.0,
     'L0_ffn_mlp2_w': 3.403,
     'L0_ffn_mlp2_b': 8.0}
    for name, (base, spread) in spreads.items():
        noise = np.random.default_rng([zlib.crc32(name.encode()), seed]).standard_normal(out[name].shape)
        drawn = base * np.exp(spread * noise) if base else spread * noise
        out[name] = jnp.asarray(drawn.astype(out[name].dtype))
    for name, factor in factors.items():
        out[name] = (out[name] * factor).astype(out[name].dtype)
    return out
```

```python
import numpy as np
import concourse.bass as bass
from concourse import mybir
from contextlib import ExitStack

F32 = mybir.dt.float32
F16 = mybir.dt.float16
I32 = mybir.dt.int32
U32 = mybir.dt.uint32
ALU = mybir.AluOpType
ACT = mybir.ActivationFunctionType
AX = mybir.AxisListType

P = 128
NB, NTOK, D = 8, 256, 192
NT = NB * NTOK // P
ROWS = NB * NTOK
D1 = D - P
EMB, GP, CH = 64, 16, 3
HD = 16
NE, TOPK, HID = 16, 4, 384
QT = ROWS // P
TILES = ROWS * TOPK // P + NE - 1
STEPS = 80
RING = 8
AHEAD = 5
TAB = STEPS + RING
HC = HID // P
ROWT = D + D + 2 * NE
S1 = 2.0 ** 9
S2 = 2.0 ** 9
SA = 2.0 ** 9
LN_EPS, RMS_EPS, ATT_EPS = 1e-5, 1e-5, 1e-6
LIMIT, ALPHA = 7.0, 1.702
SIGMAX = float(1.0 / (1.0 + np.exp(-np.float64(LIMIT * ALPHA))))
MAGIC = 1597463007.0


def build(nc, x0, x1, x2, idx, w0t, w1t, w2t, wft, bcol, wq, wk, wo, gw, m1a, m1b, b1, m2, b2, sraw,
          c32, c16, p1, p2, pat, out):
    with ExitStack() as ctx:
        def sb(name, shape, dt=F32):
            return ctx.enter_context(nc.sbuf_tensor(name, shape, dt))

        def sem(name):
            return ctx.enter_context(nc.semaphore(name))

        t_dram = nc.dram_tensor("t_dram", [ROWS + P, ROWT // 2], F32, kind="Internal").ap()
        acc_odd = nc.dram_tensor("acc_odd", [ROWS + P, D], F32, kind="Internal").ap()

        W1s = sb("W1s", [P, NE, 4, 2 * HID], F16)
        W2s = sb("W2s", [P, NE, 2, HC * D], F16)
        C32 = sb("C32", [P, 128 + 128 + 16 + 3])
        C16 = sb("C16", [P, 128 * 3 + 256], F16)
        srow_raw = sb("srow_raw", [P, 4])
        srow = sb("srow", [P, 4])
        ident, bmask = C32[:, 0:128], C32[:, 128:256]
        iota16, pcol, pcol_pad = C32[:, 256:272], C32[:, 272:273], C32[:, 273:274]
        ident16, ustrict, ones16, iota256 = C16[:, 0:128], C16[:, 128:256], C16[:, 256:384], C16[:, 384:640]
        idx_sb = sb("idx_sb", [P, 42], I32)
        WF0 = sb("WF0", [P, D])
        WF1 = sb("WF1", [D1 + 1, D])
        BC = sb("BC", [P, 2])
        WA = sb("WA", [P, 8 * D])
        WQ = WA[:, 0:2 * D].rearrange("p (k n) -> p k n", k=2)
        WK = WA[:, 2 * D:6 * D].rearrange("p (k n) -> p k n", k=2)
        WO = WA[:, 6 * D:8 * D].rearrange("p (k n) -> p k n", k=2)
        GW = sb("GW", [P, 2, NE])
        GS = sb("GS", [P, 2, NE])
        B2 = sb("B2", [NE, D])
        lz = sb("lz", [P, 208])
        h_all = sb("h_all", [P, NT, D])

        RW = 12736
        R = sb("R", [P, RW])
        mark = [0]

        def carve(shape, dt=F32, parts=P):
            n = 1
            for k in shape:
                n *= k
            words = n if dt != F16 else n // 2
            a = mark[0]
            mark[0] += words
            assert mark[0] <= RW, mark[0]
            v = R[0:parts, a:a + words]
            if dt != F32:
                v = v.bitcast(dt)
            if len(shape) == 1:
                return v
            names = "abcde"[:len(shape)]
            return v.rearrange("p (" + " ".join(names) + ") -> p " + " ".join(names),
                               **{names[k]: shape[k] for k in range(len(shape))})

        hw = h_all[:, :, :].rearrange("p t n -> p (t n)")
        stA = hw[:, 0:4 * HID].rearrange("p (s n) -> p s n", s=2)
        stC = hw[0:67, 4 * HID:8 * HID].rearrange("p (s n) -> p s n", s=2)
        stB = WA[:, 0:4 * HID].rearrange("p (s n) -> p s n", s=2)
        hC = carve([2, 2 * HID], F16, parts=67)
        stD = carve([2, HC * D])
        G0w, G1w, G2w = carve([32 * 24]), carve([8 * 96]), carve([2 * 384])
        G0 = G0w.rearrange("p (k j b c) -> p k j b c", k=2, j=16, b=8)
        G1 = G1w.rearrange("p (j b f) -> p j b f", j=8, b=8)
        G2 = G2w.rearrange("p (j b f) -> p j b f", j=2, b=8)
        XT1 = carve([2, 8, 64], parts=96)
        x2w = mark[0]
        XT2 = carve([8, 8, 16], parts=96)
        X0T = R[0:48, x2w:x2w + 1024].rearrange("p (q n) -> p q n", q=2)
        o1 = carve([4, 64])
        o2 = carve([64])
        W0T = carve([64], parts=48)
        W1T = carve([2, 64], parts=96)
        W2T = carve([8, 64], parts=96)
        P1 = carve([256])
        P2 = carve([512])
        CT0 = carve([ROWS])
        CT1 = carve([ROWS], parts=D1 + 1)

        B2r = CT0[:, 0:768].rearrange("p (b n) -> p b n", b=8)
        B1r = CT0[:, 768:1536].rearrange("p (b n) -> p b n", b=8)
        B0r = G2w.rearrange("p (k b n) -> p k b n", k=2, b=8)

        mark[0] = 0
        rows = carve([2, 2, 2 * D], F16)
        rows32 = R[:, 0:4 * D].rearrange("p (s t n) -> p s t n", s=2, t=2)
        comb = carve([NT, NE])
        bst, mv, mv2 = carve([NT, 6]), carve([NT, 2]), carve([NT, 2])
        rs1, ve1 = carve([NT]), carve([NT])
        nw = carve([3, NT])
        vv, rr = carve([2, 2, 2]), carve([2, 2, 2])
        nw2 = carve([2, 3, 4])
        hn, hnT = carve([2, 2, D]), carve([2, 2, 256])
        ek, rk, phk = carve([2, D]), carve([2, D]), carve([2, 2, D])
        vx = carve([2, 2, 129 + 65])
        eq, rq, phq = carve([2, 256]), carve([2, 256]), carve([2, 2, 256])
        kvm = carve([2, 4, 128])
        dn = carve([2, 512])
        attT = carve([2, 2, 256])
        tp, tpT = carve([2, 2, D]), carve([2, 2, 256])
        g_all = carve([NT, NE])

        mark[0] = NT * NE + 4 * D
        oh, ohw = carve([NT, TOPK, NE]), carve([NT, TOPK, NE])
        rank = carve([NT, NE])
        mx8 = carve([NT, 8])
        ix8 = carve([NT, 8], U32)
        ixf, ew, es = carve([NT, TOPK]), carve([NT, TOPK]), carve([NT])
        Mx = carve([NT, NE], F16)
        rkk, rkr, rkq, idv = carve([NT, TOPK]), carve([NT, TOPK]), carve([NT, TOPK]), carve([NT])
        rki = carve([2, NT, TOPK], I32)
        Aoh, Boh = carve([8, 256], F16), carve([8, 128], F16)
        lpad = carve([256])
        cnt_i, cnt, tt_e = carve([NE], I32), carve([4, NE]), carve([4])
        cT = carve([4, 512], parts=NE)
        mark[0] = NT * NE + 4 * D
        Ct, Cb = carve([2, 3, P], F16), carve([2, P], F16, parts=67)
        sg, lin, uu, av = (carve([2, HID]) for _ in range(4))
        ah, al = carve([2, HID], F16), carve([2, HID], F16)
        yv = carve([4, D])
        Li = sb("Li", [P, 257], I32)
        tab = sb("tab", [1, 2 * P], I32)
        ixr = sb("ixr", [P, RING], I32)
        Grw = carve([RING * ROWT // 2])
        Gr = Grw.bitcast(F16).rearrange("p (s n) -> p s n", s=RING)
        Gr32 = Grw.rearrange("p (s n) -> p s n", s=RING)

        bank = [ctx.enter_context(nc.psum_tensor(f"bank{k}", [P, 512], F32)) for k in range(8)]

        l1bank = [(bank[5], bank[6]), (bank[7], bank[4])]
        trs = [bank[0][:, 0:256].bitcast(F16), bank[7][:, 0:256].bitcast(F16)]

        s_c = sem("s_consts_loaded"); s_idx = sem("s_idx_loaded"); s_lw = sem("s_level_weights_loaded")
        s_aw = sem("s_attention_weights_loaded")
        s_st = [sem(f"s_stage_loaded{k}") for k in range(2)]
        s_pat = sem("s_pattern_loaded")
        s_sr = sem("s_scales_ready"); s_hi = sem("s_high_parts"); s_lo = sem("s_low_parts"); s_ah0 = sem("s_act_hold")
        s_g2 = sem("s_level2_gathered"); s_g1 = sem("s_level1_gathered"); s_g0 = [sem(f"s_level0_gathered{k}") for k in range(2)]
        s_by = sem("s_by_batch"); s_x = sem("s_level_matmul"); s_xe = sem("s_level_copied")
        s_ms = sem("s_constants_set")
        s_h = sem("s_h_matmul"); s_he = sem("s_h_copied")
        s_dv = sem("s_vector_chain")
        s_hn = sem("s_hn"); s_hnt = sem("s_hn_transposed"); s_hnte = sem("s_hnT_copied")
        s_kv = sem("s_kv"); s_q = sem("s_q"); s_ke = sem("s_k_parts"); s_qe = sem("s_q_parts")
        s_phk = sem("s_phi_k"); s_phq = sem("s_phi_q")
        s_stt = sem("s_state"); s_kvm = sem("s_state_masked"); s_nd = sem("s_num_den"); s_dn = sem("s_den_eps")
        s_att = sem("s_att"); s_o = sem("s_attention_out"); s_h2 = sem("s_h2")
        s_tp = sem("s_tp"); s_th = sem("s_high_rows"); s_tpt = sem("s_tp_transposed"); s_tpte = sem("s_tpT_copied")
        s_ga = sem("s_gate"); s_row = sem("s_rows_ready"); s_rowd = [sem(f"s_rows_stored{k}") for k in range(2)]
        s_z = sem("s_zero_rows"); s_zd = sem("s_zeros_stored")
        s_gs = sem("s_gate_weights_scaled")
        s_nx = sem("s_top_negated"); s_ex = sem("s_top_exp"); s_cb = sem("s_comb_ready"); s_cbd = sem("s_comb_stored")
        s_mr = sem("s_members"); s_rp = sem("s_rank"); s_oha = sem("s_onehot"); s_ohu = sem("s_onehot_used")
        s_ct = sem("s_comb_transposed"); s_cte = sem("s_combT_copied"); s_b2 = sem("s_bias2")
        s_base = sem("s_base"); s_based = sem("s_base_stored")
        s_tabt = sem("s_table_columns"); s_tabp = sem("s_table_row"); s_tab = sem("s_table_ready")
        s_ixc = sem("s_index_copied")
        s_gr = [sem(f"s_tile_gathered{k}") for k in range(RING)]
        s_tr = sem("s_tile_transposed"); s_tc = sem("s_tile_copied"); s_l1 = sem("s_hidden"); s_sg = sem("s_sigmoid")
        s_lin = sem("s_linear_clipped"); s_u = sem("s_gated"); s_a = sem("s_a"); s_ahi = sem("s_a_high"); s_alo = sem("s_a_low")
        s_l2 = sem("s_y"); s_y = sem("s_y_weighted"); s_sc = [sem(f"s_scattered{k}") for k in range(2)]
        s_hold = sem("s_hold"); s_clear = sem("s_accumulator_free"); s_fin = sem("s_final")

        block = ctx.enter_context(nc.Block())

        def wait(eng, s, v):
            if v > 0:
                eng.wait_ge(s, v)

        NCONST = 3 * 16

        @block.sync
        def _(sp):
            sp.dma_start(idx_sb[:, :], idx).then_inc(s_idx, 16)
            sp.dma_start(C32[:, :], c32).then_inc(s_c, 16)
            sp.dma_start(C16[:, :], c16).then_inc(s_c, 16)
            sp.dma_start(srow_raw[:, :], sraw).then_inc(s_c, 16)
            for k in range(2):
                sp.dma_start(stC[66:67, k, :], pat).then_inc(s_pat, 16)
            sp.dma_start(W2T, w2t.rearrange("(h p) e -> p h e", p=96)).then_inc(s_lw, 16)
            sp.dma_start(W1T, w1t.rearrange("(h p) e -> p h e", p=96)).then_inc(s_lw, 16)
            sp.dma_start(W0T, w0t).then_inc(s_lw, 16)
            sp.dma_start(P1, p1).then_inc(s_lw, 16)
            sp.dma_start(P2, p2).then_inc(s_lw, 16)
            sp.dma_start(BC[:, :], bcol).then_inc(s_lw, 16)
            sp.dma_start(WF0[:, :], wft[0:P, :]).then_inc(s_lw, 16)
            sp.dma_start(WF1[:, :], wft[P:D + 1, :]).then_inc(s_lw, 16)
            with sp.Fori(0, NE // 2) as i:
                for u in range(2):
                    sp.wait_ge(s_hi, i * 2 + (u + 1))
                    sp.wait_ge(s_lo, i * 2 + (u + 1))
                    e = i * 2 + u
                    sp.dma_start(stA[:, u, :], m1a[bass.ds(e, 1), :, :].rearrange("e p n -> (e p) n")).then_inc(s_st[u], 16)
                    for k in range(2):
                        sp.dma_start(stB[k * D1:(k + 1) * D1, u, :], m1b[bass.ds(e, 1), :, :].rearrange("e p n -> (e p) n")).then_inc(s_st[u], 16)
                    sp.dma_start(stC[0:D1, u, :], m1b[bass.ds(e, 1), :, :].rearrange("e p n -> (e p) n")).then_inc(s_st[u], 16)
                    for k in range(2):
                        sp.dma_start(stC[D1 + k:D1 + k + 1, u, :], b1[bass.ds(e, 1), :]).then_inc(s_st[u], 16)
                    sp.dma_start(stD[:, u, :], m2[bass.ds(e, 1), :, :].rearrange("e p n -> (e p) n")).then_inc(s_st[u], 16)
            sp.wait_ge(s_hi, NE + 2)
            sp.wait_ge(s_lo, NE + 2)
            for dst, src in ((WQ, wq), (WK, wk), (WO, wo), (GW, gw)):
                sp.dma_start(dst[:, 0, :], src[0:P, :]).then_inc(s_aw, 16)
                n = src.shape[0] - P
                sp.dma_start(dst[0:n, 1, :], src[P:P + n, :]).then_inc(s_aw, 16)
            sp.dma_start(B2[:, :], b2).then_inc(s_aw, 16)
            sp.wait_ge(s_z, 1)
            for t in range(NT + 1):
                sp.dma_start(acc_odd[t * P:(t + 1) * P, :], lz[:, 0:D]).then_inc(s_zd, 16)
            sp.dma_start(out[ROWS:ROWS + P, :], lz[:, 0:D]).then_inc(s_zd, 16)
            sp.dma_start(t_dram[ROWS:ROWS + P, :], lz[:, 0:ROWT // 2]).then_inc(s_zd, 16)
            tv = t_dram[0:ROWS, :].rearrange("(t p) n -> p t n", p=P)
            for b in range(NB):
                sp.wait_ge(s_row, b + 1)
                sp.dma_start(tv[:, 2 * b:2 * b + 2, 0:D], rows32[:, b % 2, :, :]).then_inc(s_rowd[b % 2], 16)
            sp.wait_ge(s_cb, 1)
            sp.dma_start(tv[:, :, D:D + NE], comb).then_inc(s_cbd, 16)
            ov = out[0:ROWS, :].rearrange("(t p) n -> p t n", p=P)
            for b in range(NB):
                sp.wait_ge(s_base, b + 1)
                sp.dma_start(ov[:, 2 * b:2 * b + 2, :], h_all[:, 2 * b:2 * b + 2, :]).then_inc(s_based, 16)

        @block.gpsimd
        def _(po):
            po.memset(lz[:, :], 0.0).then_inc(s_z, 1)
            po.wait_ge(s_z, 1)
            po.memset(CT1[D1:D1 + 1, :], 1.0).then_inc(s_ms, 1)
            po.wait_ge(s_ms, 1)
            po.wait_ge(s_idx, 16)

            def take(dst, src, col, s):
                po.indirect_dma_start(out=dst, out_offset=None, in_=src,
                                      in_offset=bass.IndirectOffsetOnAxis(ap=idx_sb[:, col:col + 1], axis=0)).then_inc(s, 16)
            for j in range(2):
                take(G2w[:, 384 * j:384 * (j + 1)], x2, 40 + j, s_g2)
            for j in range(8):
                take(G1w[:, 96 * j:96 * (j + 1)], x1, 32 + j, s_g1)
            for k in range(2):
                for j in range(16):
                    q = 16 * k + j
                    take(G0w[:, 24 * q:24 * (q + 1)], x0, q, s_g0[k])

            po.wait_ge(s_he, NB)
            po.memset(vx[:, :, :, :], 1.0).then_inc(s_ms, 1)
            po.wait_ge(s_ms, 2)
            po.memset(tpT[D1:D1 + 1, :, 1, :], 1.0).then_inc(s_ms, 1)
            po.wait_ge(s_ms, 3)
            po.memset(attT[D1:D1 + 1, :, 1, :], 1.0).then_inc(s_ms, 1)
            po.wait_ge(s_base, NB)
            po.memset(Cb[D1:67, :, :], 1.0).then_inc(s_ms, 1)
            po.wait_ge(s_ms, 5)

            po.wait_ge(s_tab, 1)
            po.wait_ge(s_rowd[0], 16 * NB // 2)
            po.wait_ge(s_rowd[1], 16 * NB // 2)
            po.wait_ge(s_cbd, 16)
            po.wait_ge(s_zd, 16 * (NT + 3))
            po.wait_ge(s_based, 16 * NB)

            def index(tile, slot, done):
                c = po.value_load(tab[0:1, tile], min_val=0, max_val=NE * QT)
                po.tensor_copy(ixr[:, slot:slot + 1], Li[:, bass.ds(c, 1)]).then_inc(s_ixc, 1)
                po.wait_ge(s_ixc, done)

            def gather(slot):
                po.indirect_dma_start(out=Gr32[:, slot, :], out_offset=None, in_=t_dram,
                                      in_offset=bass.IndirectOffsetOnAxis(ap=ixr[:, slot:slot + 1], axis=0)).then_inc(s_gr[slot], 16)
            for t in range(AHEAD):
                index(slice(t, t + 1), t, t + 1)
                gather(t)
            with po.Fori(0, STEPS // RING) as i:
                for u in range(RING):
                    po.wait_ge(s_y, i * RING + (u + 3))
                    po.sem_inc(s_hold, 1)
                    if u >= 2:
                        po.wait_ge(s_sc[u % 2], i * (RING // 2 * 16) + 16 * (u // 2))
                    po.sem_inc(s_clear, 1)
                    po.indirect_dma_start(out=(out, acc_odd)[u % 2],
                                          out_offset=bass.IndirectOffsetOnAxis(ap=ixr[:, u:u + 1], axis=0),
                                          in_=yv[:, u % 4, :], in_offset=None, compute_op=ALU.add).then_inc(s_sc[u % 2], 16)
                    v = (u + AHEAD) % RING
                    c = po.value_load(tab[0:1, bass.ds(i * RING + (u + AHEAD), 1)], min_val=0, max_val=NE * QT)
                    po.tensor_copy(ixr[:, v:v + 1], Li[:, bass.ds(c, 1)]).then_inc(s_ixc, 1)
                    po.wait_ge(s_ixc, i * RING + (u + 1 + AHEAD))
                    po.sem_inc(s_hold, 1)
                    gather(v)
                for k in range(2):
                    po.wait_ge(s_sc[k], i * (RING // 2 * 16) + RING // 2 * 16)
                    po.sem_inc(s_hold, 1)
            for k in range(RING):
                po.wait_ge(s_gr[k], 16 * (STEPS // RING + (1 if k < AHEAD else 0)))
            po.dma_start(out[0:ROWS, :], acc_odd[0:ROWS, :], accum_op=ALU.add, max_dma_last_dim=4096).then_inc(s_fin, 16)
            po.wait_ge(s_fin, 16)

        chain = {}

        def link(eng, ins):
            chain["n"] = chain.get("n", 0) + 1
            ins.then_inc(s_dv, 1)
            eng.wait_ge(s_dv, chain["n"])

        @block.vector
        def _(ve):
            ve.wait_ge(s_c, NCONST)
            ve.tensor_scalar(srow[:, :], srow_raw[:, :], S1, None, ALU.mult).then_inc(s_sr, 1)
            ve.wait_ge(s_sr, 1)
            ve.sem_inc(s_lo, 2)
            with ve.Fori(0, NE // 2) as i:
                for u in range(2):
                    e = i * 2 + u
                    ve.wait_ge(s_hi, i * 2 + (u + 3))
                    ve.scalar_tensor_tensor(out=W1s[:, bass.ds(e, 1), 1, :], in0=stA[:, u, :], scalar=srow[:, 0:1],
                                            in1=W1s[:, bass.ds(e, 1), 0, :], op0=ALU.mult, op1=ALU.subtract)
                    ve.scalar_tensor_tensor(out=W1s[0:67, bass.ds(e, 1), 3, :], in0=stC[:, u, :], scalar=srow[0:67, 2:3],
                                            in1=hC[:, u, :], op0=ALU.mult, op1=ALU.subtract)
                    ve.scalar_tensor_tensor(out=W2s[:, bass.ds(e, 1), 1, :], in0=stD[:, u, :], scalar=S2,
                                            in1=W2s[:, bass.ds(e, 1), 0, :], op0=ALU.mult, op1=ALU.subtract).then_inc(s_lo, 1)
            ve.wait_ge(s_g2, 32)
            ve.tensor_copy(B2r.rearrange("p b (j f) -> p j b f", j=2), G2).then_inc(s_by, 1)
            ve.wait_ge(s_g1, 16 * 8)
            ve.tensor_copy(B1r.rearrange("p b (j f) -> p j b f", j=8), G1).then_inc(s_by, 1)
            for k in range(2):
                ve.wait_ge(s_x, 1 + k)
                ve.tensor_copy(XT2[:, :, 4 * k:4 * k + 4, :],
                               bank[k][0:96, :].rearrange("p (b h g) -> p h b g", b=4, h=8)).then_inc(s_xe, 1)
            ve.wait_ge(s_x, 3)
            ve.tensor_copy(o2, bank[2][:, 0:64]).then_inc(s_xe, 1)
            for k in range(2):
                ve.wait_ge(s_x, 4 + k)
                ve.tensor_copy(XT1[:, :, 4 * k:4 * k + 4, :],
                               bank[k][0:96, :].rearrange("p (b h g) -> p h b g", b=4, h=2)).then_inc(s_xe, 1)
            ve.wait_ge(s_x, 6)
            ve.tensor_copy(o1, bank[2][:, 0:256].rearrange("p (b e) -> p b e", b=4)).then_inc(s_xe, 1)
            for k in range(4):
                ve.wait_ge(s_x, 7 + k)
                ve.tensor_scalar(CT1[0:EMB, 512 * k:512 * k + 512], bank[3 + k % 2][0:EMB, :], BC[0:EMB, 1:2], None,
                                 ALU.add).then_inc(s_xe, 1)
            for k in range(4):
                ve.wait_ge(s_x, 11 + k)
                for j in range(2):
                    ins = ve.tensor_scalar(CT0[EMB:P, 512 * k + 256 * j:512 * k + 256 * (j + 1)],
                                           l1bank[k % 2][j][EMB:P, 0:256], BC[EMB:P, 0:1], None, ALU.add)
                ins.then_inc(s_xe, 1)
            CT0v = CT0.rearrange("p (b k t) -> p b k t", b=8, k=2)
            n = 14
            for k in range(2):
                ve.wait_ge(s_by, 1)
                ve.wait_ge(s_g0[k], 16 * 16)
                ve.tensor_copy(B0r[:, k].rearrange("p b (j c) -> p j b c", j=16), G0[:, k]).then_inc(s_by, 1)
                for q in range(2):
                    ve.wait_ge(s_x, n + 1)
                    ve.tensor_copy(X0T[:, q, :], bank[q][0:48, :]).then_inc(s_xe, 1)
                    ve.wait_ge(s_x, n + 2)
                    ve.tensor_scalar(CT0v[0:EMB, 4 * q:4 * q + 4, k, :],
                                     bank[2 + q][0:EMB, :].rearrange("p (b t) -> p b t", b=4), BC[0:EMB, 0:1], None,
                                     ALU.add).then_inc(s_xe, 1)
                    n += 2
            ve.wait_ge(s_aw, 16 * 9)
            ve.tensor_scalar(GS[:, 0, :], GW[:, 0, :], srow_raw[:, 0:1], None, ALU.mult)
            ve.tensor_scalar(GS[0:D1 + 1, 1, :], GW[0:D1 + 1, 1, :], srow_raw[0:D1 + 1, 2:3], None, ALU.mult).then_inc(s_gs, 1)

            def rsqrt(y, v, s0, s1, s2):
                link(ve, ve.tensor_scalar(y.bitcast(I32), v.bitcast(I32), -0.5, MAGIC, ALU.mult, ALU.add))
                for _ in range(4):
                    link(ve, ve.tensor_tensor(s0, y, y, ALU.mult))
                    link(ve, ve.tensor_tensor(s1, s0, v, ALU.mult))
                    link(ve, ve.tensor_scalar(s2, s1, -0.5, 1.5, ALU.mult, ALU.add))
                    link(ve, ve.tensor_tensor(y, y, s2, ALU.mult))

            for t in range(NT):
                ve.wait_ge(s_he, t // 2 + 1)
                ins = ve.bn_stats(bst[:, t, :], h_all[:, t, :])
            link(ve, ins)
            for t in range(NT):
                ins = ve.bn_aggr(mv[:, t, :], bst[:, t, :])
            link(ve, ins)
            link(ve, ve.tensor_scalar(ve1, mv[:, :, 1], LN_EPS, None, ALU.add))
            rsqrt(rs1, ve1, nw[:, 0, :], nw[:, 1, :], nw[:, 2, :])

            def normalise(b):
                p = b % 2
                wait(ve, s_hnt, b - 1)
                for j in range(2):
                    t = 2 * b + j
                    ins = ve.tensor_scalar(hn[:, p, j, :], h_all[:, t, :], mv[:, t, 0:1], rs1[:, t:t + 1],
                                           ALU.subtract, ALU.mult)
                ins.then_inc(s_hn, 1)

            def phi(b):
                p = b % 2
                ve.wait_ge(s_ke, b + 1)
                wait(ve, s_stt, b - 1)
                ve.scalar_tensor_tensor(out=phk[:, p, :, :], in0=ek, scalar=1.0, in1=rk,
                                        op0=ALU.min, op1=ALU.add).then_inc(s_phk, 1)
                ve.wait_ge(s_qe, b + 1)
                wait(ve, s_nd, b - 1)
                ve.scalar_tensor_tensor(out=phq[:, p, 0, :], in0=eq[:, 0, :], scalar=1.0, in1=rq[:, 0, :],
                                        op0=ALU.min, op1=ALU.add)
                ve.scalar_tensor_tensor(out=phq[0:D1, p, 1, :], in0=eq[0:D1, 1, :], scalar=1.0,
                                        in1=rq[0:D1, 1, :], op0=ALU.min, op1=ALU.add).then_inc(s_phq, 1)

            def mask_state(b):
                p = b % 2
                ve.wait_ge(s_stt, b + 1)
                wait(ve, s_nd, b - 1)
                ve.tensor_tensor(kvm[:, p, 0, :], bank[4][:, 0:128], bmask, ALU.mult)
                ve.scalar_tensor_tensor(out=kvm[:, p, 1, :], in0=bmask, scalar=bank[4][:, 128:129], in1=bmask,
                                        op0=ALU.mult, op1=ALU.add)
                ve.tensor_tensor(kvm[0:D1, p, 2, 0:D1], bank[4][0:D1, 256:256 + D1], bmask[0:D1, 0:D1], ALU.mult)
                ve.scalar_tensor_tensor(out=kvm[0:D1, p, 3, 0:D1], in0=bmask[0:D1, 0:D1],
                                        scalar=bank[4][0:D1, 320:321], in1=bmask[0:D1, 0:D1],
                                        op0=ALU.mult, op1=ALU.add).then_inc(s_kvm, 1)

            def divide(b):
                p = b % 2
                ve.wait_ge(s_dn, b + 1)
                ve.reciprocal(dn[:, p, 0:256], dn[:, p, 0:256])
                link(ve, ve.reciprocal(dn[0:D1, p, 256:512], dn[0:D1, p, 256:512]))
                wait(ve, s_o, b - 1)
                ve.tensor_tensor(attT[:, p, 0, :], bank[5][:, 0:256], dn[:, p, 0:256], ALU.mult)
                ve.tensor_tensor(attT[0:D1, p, 1, :], bank[5][0:D1, 256:512], dn[0:D1, p, 256:512],
                                 ALU.mult).then_inc(s_att, 1)

            def second_norm(b):
                p = b % 2
                h2 = h_all[:, 2 * b:2 * b + 2, :]
                ve.wait_ge(s_o, b + 1)
                link(ve, ve.tensor_tensor(h2, h2, bank[4][:, 0:2 * D].rearrange("p (t n) -> p t n", t=2), ALU.add))
                for j in range(2):
                    ins = ve.bn_stats(bst[:, 2 * b + j, :], h_all[:, 2 * b + j, :])
                ins.then_inc(s_h2, 1)
                ve.wait_ge(s_h2, b + 1)
                for j in range(2):
                    ins = ve.bn_aggr(mv2[:, 2 * b + j, :], bst[:, 2 * b + j, :])
                link(ve, ins)
                var = mv2[:, 2 * b:2 * b + 2, 1]
                link(ve, ve.tensor_scalar(vv[:, p, 0, :], var, LN_EPS, None, ALU.add))
                link(ve, ve.scalar_tensor_tensor(out=vv[:, p, 1, :], in0=vv[:, p, 0, :], scalar=RMS_EPS, in1=var,
                                                 op0=ALU.mult, op1=ALU.add))
                f = "p a t -> p (a t)"
                rsqrt(rr[:, p, :, :].rearrange(f), vv[:, p, :, :].rearrange(f), nw2[:, p, 0, :], nw2[:, p, 1, :],
                      nw2[:, p, 2, :])
                wait(ve, s_tpt, b - 1)
                wait(ve, s_th, b - 1)
                for j in range(2):
                    ins = ve.tensor_scalar(tp[:, p, j, :], h_all[:, 2 * b + j, :], mv2[:, 2 * b + j, 0:1],
                                           rr[:, p, 1, j:j + 1], ALU.subtract, ALU.mult)
                ins.then_inc(s_tp, 1)
                link(ve, ve.tensor_tensor(nw2[:, p, 0, 0:2], mv2[:, 2 * b:2 * b + 2, 0], rr[:, p, 0, :], ALU.mult))
                ve.tensor_scalar(nw2[:, p, 1, 0:2], nw2[:, p, 0, 0:2], -1.0, None, ALU.mult)
                link(ve, ve.tensor_scalar(nw2[:, p, 2, 0:2], rr[:, p, 0, :], 1.0, None, ALU.add))
                for j in range(2):
                    t = 2 * b + j
                    ve.tensor_scalar(h_all[:, t, :], h_all[:, t, :], nw2[:, p, 2, j:j + 1], nw2[:, p, 1, j:j + 1],
                                     ALU.mult, ALU.add)
                ve.wait_ge(s_th, b + 1)
                tt2 = tp[:, p, :, :]
                r2 = rows[:, p, :, :]
                ve.tensor_tensor(r2[:, :, D:D + D1], tt2[:, :, P:D], r2[:, :, P:D], ALU.subtract)
                ve.tensor_tensor(r2[:, :, D + D1:2 * D], tt2[:, :, 0:P], r2[:, :, 0:P], ALU.subtract).then_inc(s_row, 1)

            def gates(b):
                ve.wait_ge(s_ga, b + 1)
                ve.tensor_copy(g_all[:, 2 * b:2 * b + 2, :], bank[7][:, 0:32].rearrange("p (t e) -> p t e", t=2))\
                  .then_inc(s_gs, 1)

            for s in range(NB + 3):
                if s < NB:
                    normalise(s)
                if 0 <= s - 2 < NB:
                    second_norm(s - 2)
                if 0 <= s - 1 < NB:
                    mask_state(s - 1)
                if s < NB:
                    phi(s)
                if 0 <= s - 1 < NB:
                    divide(s - 1)
                if 0 <= s - 3 < NB:
                    gates(s - 3)

            ve.wait_ge(s_gs, NB + 1)
            for t in range(NT):
                ins = ve.max(mx8[:, t, :], g_all[:, t, :])
            link(ve, ins)
            for t in range(NT):
                ins = ve.max_index(ix8[:, t, :], mx8[:, t, :], g_all[:, t, :])
            top = mx8[:, :, 0:TOPK]
            ve.tensor_tensor(ew[:, :, :], top, mx8[:, :, 0:1].broadcast_to([P, NT, TOPK]), ALU.subtract).then_inc(s_nx, 1)
            link(ve, ins)
            link(ve, ve.tensor_copy(ixf[:, :, :], ix8[:, :, 0:TOPK]))
            full = [P, NT, TOPK, NE]
            link(ve, ve.tensor_tensor(oh, iota16.rearrange("p (a k e) -> p a k e", a=1, k=1).broadcast_to(full),
                                      ixf[:, :, :].rearrange("p t (k e) -> p t k e", e=1).broadcast_to(full), ALU.is_equal))
            with nc.allow_low_precision(reason="sums of zeros and one one are exact"):
                ve.tensor_reduce(Mx, oh.rearrange("p t k e -> p t e k"), AX.X, ALU.add).then_inc(s_mr, 1)
            ve.wait_ge(s_ex, 1)
            link(ve, ve.tensor_reduce(es, ew[:, :, :], AX.X, ALU.add))
            link(ve, ve.reciprocal(es, es))
            link(ve, ve.tensor_tensor(ew[:, :, :], ew[:, :, :],
                                      es.rearrange("p (t k) -> p t k", k=1).broadcast_to([P, NT, TOPK]), ALU.mult))
            link(ve, ve.tensor_tensor(ohw, oh, ew[:, :, :].rearrange("p t (k e) -> p t k e", e=1).broadcast_to(full), ALU.mult))
            ve.tensor_reduce(comb, ohw.rearrange("p t k e -> p t e k"), AX.X, ALU.add).then_inc(s_cb, 1)
            ve.wait_ge(s_rp, 1)
            ve.wait_ge(s_cb, 1)
            link(ve, ve.tensor_copy(rank[:, :, :], bank[0][:, 0:NT * NE].rearrange("p (t e) -> p t e", t=NT)))
            link(ve, ve.tensor_tensor(ohw, oh, rank[:, :, :].rearrange("p t (k e) -> p t k e", k=1).broadcast_to(full), ALU.mult))
            link(ve, ve.tensor_reduce(rkk[:, :, :], ohw, AX.X, ALU.add))
            link(ve, ve.tensor_copy(rki[:, 0, :, :], rkk[:, :, :]))
            link(ve, ve.tensor_single_scalar(rki[:, 1, :, :], rki[:, 0, :, :], 7, ALU.logical_shift_right))
            link(ve, ve.tensor_copy(rkq[:, :, :], rki[:, 1, :, :]))
            link(ve, ve.scalar_tensor_tensor(out=rkr[:, :, :], in0=rkq[:, :, :], scalar=-128.0, in1=rkk[:, :, :],
                                             op0=ALU.mult, op1=ALU.add))
            link(ve, ve.scalar_tensor_tensor(out=rkq[:, :, :], in0=ixf[:, :, :], scalar=float(QT), in1=rkq[:, :, :],
                                             op0=ALU.mult, op1=ALU.add))
            for k in range(4):
                ve.wait_ge(s_ct, k + 1)
                ve.tensor_copy(cT[:, k, :], bank[3][0:NE, :]).then_inc(s_cte, 1)
            for t in range(NT):
                ins = ve.tensor_scalar(idv[:, t:t + 1], pcol, float(P * t + 1), None, ALU.add)
            link(ve, ins)
            for n in range(NT * TOPK):
                t, k = divmod(n, TOPK)
                wait(ve, s_ohu, n - 7)
                ve.tensor_scalar(Aoh[:, n % 8, :], iota256, rkq[:, t, k:k + 1], idv[:, t:t + 1], ALU.is_equal, ALU.mult)
                ve.tensor_scalar(Boh[:, n % 8, :], iota256[:, 0:128], rkr[:, t, k:k + 1], None,
                                 ALU.is_equal).then_inc(s_oha, 1)
            link(ve, ve.tensor_scalar(cnt[:, 0, :], bank[0][:, 256:256 + NE], 127.0, None, ALU.add))
            link(ve, ve.tensor_copy(cnt_i, cnt[:, 0, :]))
            link(ve, ve.tensor_single_scalar(cnt_i, cnt_i, 7, ALU.logical_shift_right))
            link(ve, ve.tensor_copy(cnt[:, 1, :], cnt_i))
            link(ve, ve.tensor_tensor_scan(cnt[:, 2, :], ones16[:, 0:NE], cnt[:, 1, :], 0.0, ALU.mult, ALU.add))
            link(ve, ve.tensor_scalar(cnt[:, 3, :], cnt[:, 2, :], pcol, None, ALU.is_le))
            link(ve, ve.tensor_reduce(tt_e[:, 0:1], cnt[:, 3, :], AX.X, ALU.add))
            link(ve, ve.tensor_tensor(cnt[:, 3, :], cnt[:, 3, :], cnt[:, 1, :], ALU.mult))
            link(ve, ve.tensor_reduce(tt_e[:, 1:2], cnt[:, 3, :], AX.X, ALU.add))
            link(ve, ve.tensor_tensor(tt_e[:, 1:2], pcol, tt_e[:, 1:2], ALU.subtract))
            link(ve, ve.scalar_tensor_tensor(out=tt_e[:, 2:3], in0=tt_e[:, 0:1], scalar=float(QT), in1=tt_e[:, 1:2],
                                             op0=ALU.mult, op1=ALU.add))
            ve.tensor_scalar(tt_e[:, 2:3], tt_e[:, 2:3], float(NE * QT), None, ALU.min)
            ve.tensor_scalar(tt_e[:, 3:4], tt_e[:, 0:1], float(NE - 1), None, ALU.min).then_inc(s_tabt, 1)
            ve.wait_ge(s_ohu, NT * TOPK)
            link(ve, ve.tensor_scalar(lpad, bank[1][:, 0:256], 0.0, pcol_pad, ALU.is_equal, ALU.mult))
            ve.scalar_tensor_tensor(out=Li[:, 0:256], in0=bank[1][:, 0:256], scalar=-1.0, in1=lpad,
                                    op0=ALU.add, op1=ALU.add)
            ve.tensor_scalar(Li[:, 256:257], pcol_pad, -1.0, None, ALU.add)
            ve.wait_ge(s_tabp, 1)
            ve.tensor_copy(tab[:, :], bank[2][0:1, 0:2 * P]).then_inc(s_tab, 1)
            for b in range(NB):
                ve.wait_ge(s_b2, b + 1)
                h2 = h_all[:, 2 * b:2 * b + 2, :]
                ve.tensor_tensor(h2, h2, bank[4 + b % 2][:, 0:2 * D].rearrange("p (t n) -> p t n", t=2), ALU.add)\
                  .then_inc(s_base, 1)

            ve.sem_inc(s_u, 1)
            ve.sem_inc(s_y, 2)
            ve.sem_inc(s_clear, 2)

            def swiglu(p, n):
                ve.wait_ge(s_l1, n)
                ve.tensor_scalar(lin[:, p, :], bank[2 + 2 * p][:, 0:HID], (LIMIT + 1) * S1, (1 - LIMIT) * S1,
                                 ALU.min, ALU.max).then_inc(s_lin, 1)
                ve.wait_ge(s_sg, n + 1)
                ve.wait_ge(s_lin, n)
                ve.scalar_tensor_tensor(out=uu[:, p, :], in0=bank[1 + 2 * p][:, 0:HID], scalar=LIMIT * S1,
                                        in1=lin[:, p, :], op0=ALU.min, op1=ALU.mult).then_inc(s_u, 1)
                ve.wait_ge(s_u, n + 1)
                ve.scalar_tensor_tensor(out=av[:, p, :], in0=sg[:, p, :], scalar=SIGMAX, in1=uu[:, p, :],
                                        op0=ALU.min, op1=ALU.mult).then_inc(s_a, 1)
                ve.wait_ge(s_ahi, n)
                ve.scalar_tensor_tensor(out=al[:, p, :], in0=av[:, p, :], scalar=SA / (S1 * S1), in1=ah[:, p, :],
                                        op0=ALU.mult, op1=ALU.subtract).then_inc(s_alo, 1)
            swiglu(0, 1)
            with ve.Fori(0, STEPS // RING) as i:
                for u in range(RING):
                    swiglu((u + 1) % 2, i * RING + (u + 2))
                    e = ve.value_load(tab[0:1, bass.ds(i * RING + (P + u), 1)], min_val=0, max_val=NE - 1)
                    ve.wait_ge(s_l2, i * RING + (u + 2))
                    ve.wait_ge(s_clear, i * RING + (u + 1))
                    ve.tensor_scalar(yv[:, u % 4, :], bank[5 + u % 2][:, 0:D], Gr32[:, u, bass.ds(e + D, 1)],
                                     1.0 / (SA * S2), ALU.mult, ALU.mult).then_inc(s_y, 1)

        @block.scalar
        def _(ac):
            ac.wait_ge(s_sr, 1)
            ac.wait_ge(s_pat, 32)
            ac.sem_inc(s_hi, 2)
            with ac.Fori(0, NE // 2) as i:
                for u in range(2):
                    e = i * 2 + u
                    ac.wait_ge(s_st[u], i * (7 * 16) + 7 * 16)
                    ac.sem_inc(s_ah0, 1)
                    ac.activation(W1s[:, bass.ds(e, 1), 0, :], stA[:, u, :], ACT.Copy, scale=srow[:, 0:1])
                    ac.activation(W1s[:, bass.ds(e, 1), 2, :], stB[:, u, :], ACT.Copy, scale=srow[:, 1:2])
                    ac.wait_ge(s_lo, i * 2 + (u + 1))
                    ac.activation(hC[:, u, :], stC[:, u, :], ACT.Copy, scale=srow[0:67, 3:4])
                    ac.activation(W2s[:, bass.ds(e, 1), 0, :], stD[:, u, :], ACT.Copy, scale=S2).then_inc(s_hi, 1)
            ac.wait_ge(s_lo, NE + 2)
            for b in range(NB):
                ac.wait_ge(s_h, b + 1)
                ac.activation(h_all[:, 2 * b:2 * b + 2, :], bank[4 + b % 4][:, 0:2 * D].rearrange("p (t n) -> p t n", t=2),
                              ACT.Copy).then_inc(s_he, 1)
            ac.wait_ge(s_ms, 4)

            def copy_hnT(b):
                p = b % 2
                ac.wait_ge(s_hnt, b + 1)
                wait(ac, s_q, b - 1)
                ac.activation(hnT[:, p, 0, :], bank[0][:, 0:256], ACT.Copy)
                ac.activation(hnT[0:D1, p, 1, :], bank[0][0:D1, 256:512], ACT.Copy).then_inc(s_hnte, 1)

            def kv_parts(b):
                p = b % 2
                wait(ac, s_phk, b)
                wait(ac, s_stt, b - 1)
                for j in range(2):
                    ac.wait_ge(s_kv, 2 * b + j + 1)
                    ac.activation(ek[:, j, :], bank[1 + j][:, 0:D], ACT.Exp)
                    ac.activation(rk[:, j, :], bank[1 + j][:, 0:D], ACT.Relu)
                    ac.activation(vx[:, p, j, 0:P], bank[1 + j][:, D:D + P], ACT.Copy)
                    ins = ac.activation(vx[:, p, j, P + 1:D + 1], bank[1 + j][:, D + P:2 * D], ACT.Copy)
                ins.then_inc(s_ke, 1)

            def q_parts(b):
                p = b % 2
                ac.wait_ge(s_q, b + 1)
                wait(ac, s_phq, b)
                for f, dst in ((ACT.Exp, eq), (ACT.Relu, rq)):
                    ac.activation(dst[:, 0, :], bank[3][:, 0:256], f)
                    ins = ac.activation(dst[0:D1, 1, :], bank[3][0:D1, 256:512], f)
                ins.then_inc(s_qe, 1)

            def den(b):
                p = b % 2
                ac.wait_ge(s_nd, b + 1)
                wait(ac, s_att, b - 1)
                ac.activation(dn[:, p, 0:256], bank[6][:, 0:256], ACT.Copy, bias=ATT_EPS)
                ac.activation(dn[0:D1, p, 256:512], bank[6][0:D1, 256:512], ACT.Copy, bias=ATT_EPS).then_inc(s_dn, 1)

            def high_rows(b):
                p = b % 2
                ac.wait_ge(s_tp, b + 1)
                wait(ac, s_rowd[p], 16 * (b // 2))
                ac.activation(rows[:, p, :, 0:D], tp[:, p, :, :], ACT.Copy).then_inc(s_th, 1)

            def copy_tpT(b):
                p = b % 2
                ac.wait_ge(s_tpt, b + 1)
                wait(ac, s_ga, b - 1)
                ac.activation(tpT[:, p, 0, :], bank[0][:, 0:256], ACT.Copy)
                ac.activation(tpT[0:D1, p, 1, :], bank[0][0:D1, 256:512], ACT.Copy).then_inc(s_tpte, 1)

            for s in range(NB + 3):
                if s < NB:
                    copy_hnT(s)
                if 0 <= s - 2 < NB:
                    high_rows(s - 2)
                if s < NB:
                    kv_parts(s)
                    q_parts(s)
                if 0 <= s - 2 < NB:
                    copy_tpT(s - 2)
                if 0 <= s - 1 < NB:
                    den(s - 1)
            ac.wait_ge(s_nx, 1)
            ac.activation(ew[:, :, :], ew[:, :, :], ACT.Exp).then_inc(s_ex, 1)

            ac.wait_ge(s_ms, 5)
            ac.sem_inc(s_sg, 1)

            def copy_tile(p, n):
                ac.wait_ge(s_tr, n)
                ac.activation(Ct[:, p, :, :], trs[p][:, 0:384].rearrange("p (c t) -> p c t", c=3), ACT.Copy)
                ac.activation(Cb[0:D1, p, :], trs[p][0:D1, 128:256], ACT.Copy).then_inc(s_tc, 1)

            def sigmoid(p, n):
                ac.wait_ge(s_l1, n)
                ac.activation(sg[:, p, :], bank[1 + 2 * p][:, 0:HID], ACT.Sigmoid, scale=ALPHA / S1).then_inc(s_sg, 1)

            def high_half(p, n):
                ac.wait_ge(s_a, n)
                ac.activation(ah[:, p, :], av[:, p, :], ACT.Copy, scale=SA / (S1 * S1)).then_inc(s_ahi, 1)
            copy_tile(0, 1)
            copy_tile(1, 2)
            sigmoid(0, 1)
            high_half(0, 1)
            with ac.Fori(0, STEPS // RING) as i:
                for u in range(RING):
                    ac.wait_ge(s_l1, i * RING + (u + 1))
                    copy_tile(u % 2, i * RING + (u + 3))
                    sigmoid((u + 1) % 2, i * RING + (u + 2))
                    ac.wait_ge(s_l2, i * RING + (u + 1))
                    high_half((u + 1) % 2, i * RING + (u + 2))

        @block.tensor
        def _(pe):
            mm = pe.matmul
            pe.wait_ge(s_c, NCONST)
            pe.wait_ge(s_lw, 16 * 8)
            pe.wait_ge(s_by, 1)
            for k in range(2):
                for j in range(4):
                    ins = pe.transpose(bank[k][0:96, P * j:P * (j + 1)], B2r[:, 4 * k + j, :], ident)
                ins.then_inc(s_x, 1)
            pe.wait_ge(s_xe, 2)
            for h in range(8):
                ins = mm(bank[2][:, 0:64], XT2[:, h, :, :], W2T[:, h, :], start=h == 0, stop=h == 7)
            ins.then_inc(s_x, 1)
            pe.wait_ge(s_by, 2)
            for k in range(2):
                for j in range(4):
                    ins = pe.transpose(bank[k][0:96, P * j:P * (j + 1)], B1r[:, 4 * k + j, :], ident)
                ins.then_inc(s_x, 1)
            pe.wait_ge(s_xe, 5)
            for b in range(4):
                for h in range(2):
                    ins = mm(bank[2][:, 64 * b:64 * (b + 1)], XT1[:, h, 2 * b:2 * b + 2, :], W1T[:, h, :],
                             start=h == 0, stop=h == 1)
            ins.then_inc(s_x, 1)
            for k in range(4):
                if k >= 2:
                    pe.wait_ge(s_xe, 7 + k - 2)
                g = slice(32 * k, 32 * k + 32)
                mm(bank[3 + k % 2][0:EMB, :], o2[g, :], P2[g, :], start=True, stop=True).then_inc(s_x, 1)
            pe.wait_ge(s_xe, 10)
            for k in range(4):
                if k >= 2:
                    pe.wait_ge(s_xe, 11 + k - 2)
                for j in range(2):
                    g = slice(64 * j, 64 * j + 64)
                    ins = mm(l1bank[k % 2][j][EMB:P, 0:256], o1[g, k, :], P1[g, :], start=True, stop=True)
                ins.then_inc(s_x, 1)
            n = 14
            pe.wait_ge(s_xe, 10)
            for k in range(2):
                pe.wait_ge(s_by, 3 + k)
                for q in range(2):
                    pe.wait_ge(s_xe, n - 3 if k else 10)
                    for j in range(4):
                        ins = pe.transpose(bank[q][0:48, P * j:P * (j + 1)], B0r[:, k, 4 * q + j, :], ident)
                    ins.then_inc(s_x, 1)
                    pe.wait_ge(s_xe, n + 1)
                    mm(bank[2 + q][0:EMB, :], W0T, X0T[:, q, :], start=True, stop=True).then_inc(s_x, 1)
                    n += 2
            pe.wait_ge(s_xe, 22)
            for b in range(NB):
                wait(pe, s_he, b - 3)
                for j in range(2):
                    t = slice(P * (2 * b + j), P * (2 * b + j + 1))
                    o = bank[4 + b % 4][:, D * j:D * (j + 1)]
                    mm(o, CT0[:, t], WF0[:, :], start=True, stop=False)
                    ins = mm(o, CT1[:, t], WF1[:, :], start=False, stop=True)
                ins.then_inc(s_h, 1)

            pe.wait_ge(s_aw, 16 * 9)
            pe.wait_ge(s_he, NB)
            pe.wait_ge(s_ms, 4)

            def transposes(src, b, s):
                p = b % 2
                for j in range(2):
                    pe.transpose(bank[0][:, P * j:P * (j + 1)], src[:, p, j, 0:P], ident)
                    ins = pe.transpose(bank[0][0:D1, 256 + P * j:256 + P * (j + 1)], src[:, p, j, P:D], ident)
                ins.then_inc(s, 1)

            def kv(b):
                p = b % 2
                pe.wait_ge(s_hnte, b + 1)
                wait(pe, s_ke, b)
                for j in range(2):
                    t = slice(P * j, P * (j + 1))
                    mm(bank[1 + j][:, 0:2 * D], hnT[:, p, 0, t], WK[:, 0, :], start=True, stop=False)
                    mm(bank[1 + j][:, 0:2 * D], hnT[0:D1, p, 1, t], WK[0:D1, 1, :], start=False, stop=True).then_inc(s_kv, 1)

            def query(b):
                p = b % 2
                wait(pe, s_qe, b)
                mm(bank[3][:, 0:256], WQ[:, 0, 0:P], hnT[:, p, 0, :], start=True, stop=False)
                mm(bank[3][:, 0:256], WQ[0:D1, 1, 0:P], hnT[0:D1, p, 1, :], start=False, stop=True)
                mm(bank[3][0:D1, 256:512], WQ[:, 0, P:D], hnT[:, p, 0, :], start=True, stop=False)
                mm(bank[3][0:D1, 256:512], WQ[0:D1, 1, P:D], hnT[0:D1, p, 1, :], start=False, stop=True).then_inc(s_q, 1)

            def state(b):
                p = b % 2
                pe.wait_ge(s_phk, b + 1)
                wait(pe, s_h2, b)
                for j in range(2):
                    mm(bank[4][:, 0:129], phk[:, p, j, 0:P], vx[:, p, j, 0:129], start=j == 0, stop=j == 1)
                for j in range(2):
                    ins = mm(bank[4][0:D1, 256:321], phk[:, p, j, P:D], vx[:, p, j, 129:194], start=j == 0, stop=j == 1)
                ins.then_inc(s_stt, 1)

            def num_den(b):
                p = b % 2
                pe.wait_ge(s_kvm, b + 1)
                pe.wait_ge(s_phq, b + 1)
                wait(pe, s_att, b)
                for k in range(2):
                    mm(bank[5 + k][:, 0:256], kvm[:, p, k, :], phq[:, p, 0, :], start=True, stop=True)
                    ins = mm(bank[5 + k][0:D1, 256:512], kvm[0:D1, p, 2 + k, 0:D1], phq[0:D1, p, 1, :], start=True, stop=True)
                ins.then_inc(s_nd, 1)

            def project(b):
                p = b % 2
                pe.wait_ge(s_att, b + 1)
                for j in range(2):
                    t = slice(P * j, P * (j + 1))
                    o = bank[4][:, D * j:D * (j + 1)]
                    mm(o, attT[:, p, 0, t], WO[:, 0, :], start=True, stop=False)
                    ins = mm(o, attT[0:D1 + 1, p, 1, t], WO[0:D1 + 1, 1, :], start=False, stop=True)
                ins.then_inc(s_o, 1)

            def gate(b):
                p = b % 2
                pe.wait_ge(s_tpte, b + 1)
                pe.wait_ge(s_gs, b + 1)
                for j in range(2):
                    t = slice(P * j, P * (j + 1))
                    o = bank[7][:, NE * j:NE * (j + 1)]
                    mm(o, tpT[:, p, 0, t], GS[:, 0, :], start=True, stop=False)
                    ins = mm(o, tpT[0:D1 + 1, p, 1, t], GS[0:D1 + 1, 1, :], start=False, stop=True)
                ins.then_inc(s_ga, 1)

            for s in range(NB + 3):
                if s < NB:
                    wait(pe, s_tpte, s - 2)
                    pe.wait_ge(s_hn, s + 1)
                    transposes(hn, s, s_hnt)
                    kv(s)
                if 0 <= s - 1 < NB:
                    state(s - 1)
                if s < NB:
                    query(s)
                if 0 <= s - 2 < NB:
                    pe.wait_ge(s_tp, s - 1)
                    pe.wait_ge(s_hnte, min(s + 1, NB))
                    transposes(tp, s - 2, s_tpt)
                if 0 <= s - 1 < NB:
                    num_den(s - 1)
                if 0 <= s - 2 < NB:
                    gate(s - 2)
                if 0 <= s - 1 < NB:
                    project(s - 1)

            pe.wait_ge(s_mr, 1)
            R0 = bank[0][:, 0:NT * NE]
            mm(R0, ustrict, Mx.rearrange("p t e -> p (t e)"), start=True, stop=False)
            for j in range(NT - 1):
                mm(bank[0][:, NE * (j + 1):NE * NT].rearrange("p (t e) -> p t e", e=NE), ones16,
                   Mx[:, j:j + 1, :].broadcast_to([P, NT - 1 - j, NE]), start=False, stop=j == NT - 2)
            for j in range(NT):
                ins = mm(bank[0][:, 256:256 + NE], ones16, Mx[:, j, :], start=j == 0, stop=j == NT - 1)
            ins.then_inc(s_rp, 1)
            pe.wait_ge(s_cb, 1)
            for k in range(4):
                wait(pe, s_cte, k)
                for j in range(4):
                    ins = pe.transpose(bank[3][0:NE, P * j:P * (j + 1)], comb[:, 4 * k + j, :], ident)
                ins.then_inc(s_ct, 1)
            for n in range(NT * TOPK):
                pe.wait_ge(s_oha, n + 1)
                ins = mm(bank[1][:, 0:256], Boh[:, n % 8, :], Aoh[:, n % 8, :], start=n == 0, stop=n == NT * TOPK - 1)
                ins.then_inc(s_ohu, 1)
            pe.wait_ge(s_tabt, 1)
            for k in range(2):
                ins = mm(bank[2][0:1, P * k:P * (k + 1)], tt_e[:, 2 + k:3 + k], ident, start=True, stop=True)
            ins.then_inc(s_tabp, 1)
            for b in range(NB):
                pe.wait_ge(s_cte, b // 2 + 1)
                wait(pe, s_base, b - 1)
                for j in range(2):
                    t = 2 * b + j
                    ins = mm(bank[4 + b % 2][:, D * j:D * (j + 1)], cT[:, t // 4, P * (t % 4):P * (t % 4 + 1)],
                             B2[:, :], start=True, stop=True)
                ins.then_inc(s_b2, 1)

            pe.wait_ge(s_tab, 1)
            pe.wait_ge(s_base, NB)
            pe.sem_inc(s_l2, 1)

            def tile_transposes(slot, p, n):
                pe.wait_ge(s_gr[slot], n)
                for c in range(3):
                    ins = pe.transpose(trs[p][:, P * c:P * (c + 1)], Gr[:, slot, P * c:P * (c + 1)], ident16)
                ins.then_inc(s_tr, 1)

            def hidden(p, e):
                for m in range(2 * HC):
                    o = bank[(1 if m < HC else 2) + 2 * p][:, P * (m % HC):P * (m % HC + 1)]
                    c = slice(P * m, P * (m + 1))
                    mm(o, W1s[:, e, 0, c], Ct[:, p, 0, :], start=True, stop=False)
                    mm(o, W1s[:, e, 1, c], Ct[:, p, 0, :], start=False, stop=False)
                    mm(o, W1s[:, e, 0, c], Ct[:, p, 2, :], start=False, stop=False)
                    mm(o, W1s[:, e, 2, c], Ct[:, p, 1, :], start=False, stop=False)
                    ins = mm(o, W1s[0:67, e, 3, c], Cb[0:67, p, :], start=False, stop=True)
                ins.then_inc(s_l1, 1)

            def down(p, e):
                for k, (a, w) in enumerate(((ah, 0), (ah, 1), (al, 0))):
                    for m in range(HC):
                        ins = mm(bank[5 + p][:, 0:D], a[:, p, P * m:P * (m + 1)], W2s[:, e, w, D * m:D * (m + 1)],
                                 start=k == 0 and m == 0, stop=k == 2 and m == HC - 1)
                ins.then_inc(s_l2, 1)

            def expert(at):
                return bass.ds(pe.value_load(tab[0:1, at], min_val=0, max_val=NE - 1), 1)
            tile_transposes(0, 0, 16)
            pe.wait_ge(s_tc, 1)
            hidden(0, expert(slice(P, P + 1)))
            tile_transposes(1, 1, 16)
            with pe.Fori(0, STEPS // RING) as i:
                for u in range(RING):
                    e1 = expert(bass.ds(i * RING + (P + u + 1), 1))
                    pe.wait_ge(s_tc, i * RING + (u + 2))
                    pe.sem_inc(s_hold, 1)
                    pe.wait_ge(s_sg, i * RING + (u + 1))
                    pe.sem_inc(s_hold, 1)
                    pe.wait_ge(s_u, i * RING + (u + 1))
                    pe.sem_inc(s_hold, 1)
                    hidden((u + 1) % 2, e1)
                    pe.wait_ge(s_tc, i * RING + (u + 1))
                    v = (u + 2) % RING
                    tile_transposes(v, u % 2, i * 16 + (16 if u + 2 < RING else 32))
                    e0 = expert(bass.ds(i * RING + (P + u), 1))
                    pe.wait_ge(s_alo, i * RING + (u + 1))
                    pe.wait_ge(s_y, i * RING + (u + 1))
                    down(u % 2, e0)


    return nc


def kernel(x, L0_tok_W0, L0_tok_b0, L0_tok_W1, L0_tok_b1, L0_tok_W2, L0_tok_b2, L0_tok_Wf, L0_tok_bf,
           L0_tok_idx0, L0_tok_idx1, L0_tok_idx2, L0_attn_W_qkv, L0_attn_W_out, L0_attn_b_out, L0_ffn_norm_scale,
           L0_ffn_gate_w, L0_ffn_gate_b, L0_ffn_mlp1_w, L0_ffn_mlp1_b, L0_ffn_mlp2_w, L0_ffn_mlp2_b):
    import numpy as _np
    import concourse.bacc as _bacc
    from concourse import mybir as _mybir
    from concourse.bass_utils import run_bass_kernel_spmd as _run
    f32 = _np.float32
    A = _np.asarray
    x = A(x)
    x0 = x.transpose(2, 3, 0, 1).reshape(4096, 24)
    x1 = x.reshape(8, 3, 32, 2, 32, 2).transpose(2, 4, 0, 3, 5, 1).reshape(1024, 96)
    x2 = x.reshape(8, 3, 16, 4, 16, 4).transpose(2, 4, 0, 3, 5, 1).reshape(256, 384)
    i0 = A(L0_tok_idx0).reshape(2, 128, 16).transpose(1, 0, 2).reshape(128, 32)
    i1 = A(L0_tok_idx1).reshape(64, 2, 8).transpose(1, 0, 2).reshape(128, 8)
    i2 = A(L0_tok_idx2).reshape(16, 8, 2).transpose(1, 0, 2).reshape(128, 2)
    idx = _np.concatenate([i0, i1, i2], axis=1)
    wft = _np.concatenate([A(L0_tok_Wf).T, A(L0_tok_bf)[None]], axis=0)
    b0, b1_, b2_ = A(L0_tok_b0), A(L0_tok_b1), A(L0_tok_b2)
    bcol = _np.stack([_np.concatenate([b0, b1_]), _np.concatenate([b2_, b2_])], axis=1)
    wqkv = A(L0_attn_W_qkv)
    wo = _np.concatenate([A(L0_attn_W_out), A(L0_attn_b_out)[None]], axis=0)
    gw = _np.concatenate([A(L0_ffn_gate_w).T, A(L0_ffn_gate_b)[None]], axis=0)
    m1 = A(L0_ffn_mlp1_w).reshape(NE, HID, 2, D).transpose(0, 3, 2, 1).reshape(NE, D, 2 * HID)
    b1 = A(L0_ffn_mlp1_b).reshape(NE, HID, 2).transpose(0, 2, 1).reshape(NE, 2 * HID)
    m2 = A(L0_ffn_mlp2_w).reshape(NE, D, HC, P).transpose(0, 3, 2, 1).reshape(NE, P, HC * D)
    ns = A(L0_ffn_norm_scale)
    one = _np.zeros((3, P), f32)
    one[0, D1:D1 + 3] = 1
    one[1, D1 + 1] = 1
    tail = ns[P:D]
    sraw = _np.stack([ns[0:P], _np.concatenate([tail, tail]), _np.concatenate([tail, one[0, D1:]]),
                      _np.concatenate([tail, one[1, D1:]])], axis=1)
    r = _np.arange(P)
    c32 = _np.zeros((P, 275), f32)
    c32[:, 0:128] = _np.eye(P)
    c32[:, 128:256] = (r[:, None] // HD) == (r[None, :] // HD)
    c32[:, 256:272] = _np.arange(NE)
    c32[:, 272] = r
    c32[:, 273] = ROWS + 1 + r
    c16 = _np.zeros((P, 640), _np.float16)
    c16[:, 0:128] = _np.eye(P)
    c16[:, 128:256] = r[:, None] < r[None, :]
    c16[:, 256:384] = 1
    c16[:, 384:640] = _np.arange(256)
    pat = _np.zeros((1, 2 * HID), f32)
    pat[0, HID:] = 1

    def interpolation(n):
        pos = _np.clip((_np.arange(NTOK, dtype=f32) + f32(0.5)) * f32(n / NTOK) - f32(0.5), 0, n - 1)
        lo = _np.floor(pos).astype(_np.int32)
        hi = _np.minimum(lo + 1, n - 1)
        w = (pos - lo).astype(f32)
        m = _np.zeros((n, NTOK), f32)
        _np.add.at(m, (lo, _np.arange(NTOK)), 1 - w)
        _np.add.at(m, (hi, _np.arange(NTOK)), w)
        return m
    p1 = _np.tile(interpolation(64), (2, 1))
    m16 = interpolation(16)
    p2 = _np.zeros((P, 512), f32)
    for q in range(8):
        p2[16 * q:16 * q + 16, 256 * (q % 2):256 * (q % 2) + 256] = m16
    arrays = {"x0": x0, "x1": x1, "x2": x2, "idx": idx, "w0t": A(L0_tok_W0).T, "w1t": A(L0_tok_W1).T,
              "w2t": A(L0_tok_W2).T, "wft": wft, "bcol": bcol, "wq": wqkv[:, 0:D], "wk": wqkv[:, D:], "wo": wo,
              "gw": gw, "m1a": m1[:, 0:P], "m1b": m1[:, P:D], "b1": b1, "m2": m2, "b2": A(L0_ffn_mlp2_b),
              "sraw": sraw, "c32": c32, "c16": c16, "p1": p1, "p2": p2, "pat": pat}
    arrays = {k: _np.ascontiguousarray(v) for k, v in arrays.items()}
    nc = _bacc.Bacc("TRN2", target_bir_lowering=False, num_devices=1)
    aps = {k: nc.dram_tensor(f"in_{k}", v.shape, _mybir.dt.from_np(v.dtype), kind="ExternalInput").ap()
           for k, v in arrays.items()}
    out = nc.dram_tensor("out", (ROWS + P, D), F32, kind="ExternalOutput").ap()
    build(nc, out=out, **aps)
    got = _run(nc, [{f"in_{k}": v for k, v in arrays.items()}], core_ids=[0])
    return got.results[0]["out"][0:ROWS].reshape(NB, NTOK, D)
```

```python
import numpy as np
import concourse.bass as bass
from concourse import mybir
from contextlib import ExitStack

F32 = mybir.dt.float32
F16 = mybir.dt.float16
I32 = mybir.dt.int32
U32 = mybir.dt.uint32
ALU = mybir.AluOpType
ACT = mybir.ActivationFunctionType
AX = mybir.AxisListType

P = 128
NB, NTOK, D = 8, 256, 192
NT = NB * NTOK // P
ROWS = NB * NTOK
D1 = D - P
EMB, GP, CH = 64, 16, 3
HD = 16
NE, TOPK, HID = 16, 4, 384
QT = ROWS // P
TILES = ROWS * TOPK // P + NE - 1
STEPS = 80
RING = 8
AHEAD = 6
TAB = STEPS + RING
HC = HID // P
ROWT = D + D + 2 * NE
STAGES = 3
S1 = 2.0 ** 9
S2 = 2.0 ** 9
SA = 2.0 ** 9
LN_EPS, RMS_EPS, ATT_EPS = 1e-5, 1e-5, 1e-6
LIMIT, ALPHA = 7.0, 1.702
SIGMAX = float(1.0 / (1.0 + np.exp(-np.float64(LIMIT * ALPHA))))
MAGIC = 1597463007.0


def build(nc, x0, x1, x2, idx, w0t, w1t, w2t, wft, bcol, wq, wk, wo, gw, m1a, m1c, m2, b2, sraw,
          c32, c16, p1, p2, out):
    with ExitStack() as ctx:
        def sb(name, shape, dt=F32):
            return ctx.enter_context(nc.sbuf_tensor(name, shape, dt))

        def sem(name):
            return ctx.enter_context(nc.semaphore(name))

        t_dram = nc.dram_tensor("t_dram", [ROWS + P, ROWT // 2], F32, kind="Internal").ap()
        acc_odd = nc.dram_tensor("acc_odd", [ROWS + P, D], F32, kind="Internal").ap()

        W1s = sb("W1s", [P, NE, 4, 2 * HID], F16)
        W2s = sb("W2s", [P, NE, 2, HC * D], F16)
        C32 = sb("C32", [P, 128 + 128 + 16 + 3])
        C16 = sb("C16", [P, 128 * 3 + 256], F16)
        srow_raw = sb("srow_raw", [P, 3])
        srow = sb("srow", [P, 3])
        ident, bmask = C32[:, 0:128], C32[:, 128:256]
        iota16, pcol, pcol_pad = C32[:, 256:272], C32[:, 272:273], C32[:, 273:274]
        ident16, ustrict, ones16, iota256 = C16[:, 0:128], C16[:, 128:256], C16[:, 256:384], C16[:, 384:640]
        idx_sb = sb("idx_sb", [P, 42], I32)
        WF0 = sb("WF0", [P, D])
        WF1 = sb("WF1", [D1 + 1, D])
        BC = sb("BC", [P, 2])
        WA = sb("WA", [P, 8 * D])
        WQ = WA[:, 0:2 * D].rearrange("p (k n) -> p k n", k=2)
        WK = WA[:, 2 * D:6 * D].rearrange("p (k n) -> p k n", k=2)
        WO = WA[:, 6 * D:8 * D].rearrange("p (k n) -> p k n", k=2)
        GW = sb("GW", [P, 2, NE])
        GS = sb("GS", [P, 2, NE])
        B2 = sb("B2", [NE, D])
        lz = sb("lz", [P, 208])
        h_all = sb("h_all", [P, NT, D])

        RW = 12736
        R = sb("R", [P, RW])
        mark = [0]

        def carve(shape, dt=F32, parts=P):
            n = 1
            for k in shape:
                n *= k
            words = n if dt != F16 else n // 2
            a = mark[0]
            mark[0] += words
            assert mark[0] <= RW, mark[0]
            v = R[0:parts, a:a + words]
            if dt != F32:
                v = v.bitcast(dt)
            if len(shape) == 1:
                return v
            names = "abcde"[:len(shape)]
            return v.rearrange("p (" + " ".join(names) + ") -> p " + " ".join(names),
                               **{names[k]: shape[k] for k in range(len(shape))})

        hw = h_all[:, :, :].rearrange("p t n -> p (t n)")
        G = 2 * HID
        stA = [hw[:, 0:G], hw[:, G:2 * G], WA[:, 0:G]]
        stC = [hw[0:67, 2 * G:3 * G], hw[0:67, 3 * G:4 * G], WA[0:67, G:2 * G]]
        stD = [carve([HC * D]) for _ in range(STAGES)]
        G0w, G1w, G2w = carve([32 * 24]), carve([8 * 96]), carve([2 * 384])
        G0 = G0w.rearrange("p (k j b c) -> p k j b c", k=2, j=16, b=8)
        G1 = G1w.rearrange("p (j b f) -> p j b f", j=8, b=8)
        G2 = G2w.rearrange("p (j b f) -> p j b f", j=2, b=8)
        XT1 = carve([2, 8, 64], parts=96)
        x2w = mark[0]
        XT2 = carve([8, 8, 16], parts=96)
        X0T = R[0:48, x2w:x2w + 1024].rearrange("p (q n) -> p q n", q=2)
        o1 = carve([4, 64])
        o2 = carve([64])
        W0T = carve([64], parts=48)
        W1T = carve([2, 64], parts=96)
        W2T = carve([8, 64], parts=96)
        P1 = carve([256])
        P2 = carve([512])
        CT0 = carve([ROWS])
        CT1 = carve([ROWS], parts=D1 + 1)

        B2r = CT0[:, 0:768].rearrange("p (b n) -> p b n", b=8)
        B1r = CT0[:, 768:1536].rearrange("p (b n) -> p b n", b=8)
        B0r = G2w.rearrange("p (k b n) -> p k b n", k=2, b=8)

        mark[0] = 0
        rows = carve([2, 2, 2 * D], F16)
        rows32 = R[:, 0:4 * D].rearrange("p (s t n) -> p s t n", s=2, t=2)
        bst, mv, mv2 = carve([NT, 6]), carve([NT, 2]), carve([NT, 2])
        rs1, ve1 = carve([NT]), carve([NT])
        nw = carve([3, NT])
        vv, rr = carve([2, 2, 2]), carve([2, 2, 2])
        nw2 = carve([2, 3, 4])
        hn, hnT = carve([2, 2, D]), carve([2, 2, 256])
        ek, rk, phk = carve([2, D]), carve([2, D]), carve([2, 2, D])
        vx = carve([2, 2, 129 + 65])
        eq, rq, phq = carve([2, 256]), carve([2, 256]), carve([2, 2, 256])
        kvm = carve([2, 4, 128])
        dn = carve([2, 512])
        attT = carve([2, 2, 256])
        tp, tpT = carve([2, 2, D]), carve([2, 2, 256])
        g_all = carve([NT, NE])

        mark[0] = 4 * D
        comb, combs = carve([NT, NE]), carve([NT, NE])
        oh, ohw = carve([NT, TOPK, NE]), carve([NT, TOPK, NE])
        rank = carve([NT, NE])
        mx8 = carve([NT, 8])
        ix8 = carve([NT, 8], U32)
        ixf, ew, es = carve([NT, TOPK]), carve([NT, TOPK]), carve([NT])
        Mx = carve([NT, NE], F16)
        rkk, rkr, rkq, idv = carve([NT, TOPK]), carve([NT, TOPK]), carve([NT, TOPK]), carve([NT])
        rki = carve([2, NT, TOPK], I32)
        Aoh, Boh = carve([8, 256], F16), carve([8, 128], F16)
        lpad = carve([256])
        cnt_i, cnt, tt_e = carve([NE], I32), carve([4, NE]), carve([4])
        cT = carve([4, 512], parts=NE)
        mark[0] = 2 * NT * NE + 4 * D
        Ct, Cb = carve([2, 3, P], F16), carve([2, P], F16, parts=67)
        sg, lin, uu, av = (carve([2, HID]) for _ in range(4))
        ah, al = carve([2, HID], F16), carve([2, HID], F16)
        yv = carve([4, D])
        Li = sb("Li", [P, 257], I32)
        tab = sb("tab", [1, 2 * P], I32)
        ixr = sb("ixr", [P, RING], I32)
        Grw = carve([RING * ROWT // 2])
        Gr = Grw.bitcast(F16).rearrange("p (s n) -> p s n", s=RING)
        Gr32 = Grw.rearrange("p (s n) -> p s n", s=RING)

        bank = [ctx.enter_context(nc.psum_tensor(f"bank{k}", [P, 512], F32)) for k in range(8)]

        l1bank = [(bank[5], bank[6]), (bank[7], bank[4])]
        trs = [bank[0][:, 0:256].bitcast(F16), bank[7][:, 0:256].bitcast(F16)]

        s_c = sem("s_consts_loaded"); s_idx = sem("s_idx_loaded"); s_lw = sem("s_level_weights_loaded")
        s_aw = sem("s_attention_weights_loaded")
        s_st = [sem(f"s_stage_loaded{k}") for k in range(STAGES)]
        s_dup = sem("s_high_tails_doubled")
        s_sr = sem("s_scales_ready"); s_hi = sem("s_high_parts"); s_lo = sem("s_low_parts"); s_ah0 = sem("s_act_hold")
        s_g2 = sem("s_level2_gathered"); s_g1 = sem("s_level1_gathered"); s_g0 = [sem(f"s_level0_gathered{k}") for k in range(2)]
        s_by = sem("s_by_batch"); s_x = sem("s_level_matmul"); s_xe = sem("s_level_copied")
        s_ms = sem("s_constants_set")
        s_h = sem("s_h_matmul"); s_he = sem("s_h_copied")
        s_dv = sem("s_vector_chain")
        s_hn = sem("s_hn"); s_hnt = sem("s_hn_transposed"); s_hnte = sem("s_hnT_copied")
        s_kv = sem("s_kv"); s_q = sem("s_q"); s_ke = sem("s_k_parts"); s_qe = sem("s_q_parts")
        s_phk = sem("s_phi_k"); s_phq = sem("s_phi_q")
        s_stt = sem("s_state"); s_kvm = sem("s_state_masked"); s_nd = sem("s_num_den"); s_dn = sem("s_den_eps")
        s_att = sem("s_att"); s_o = sem("s_attention_out"); s_h2 = sem("s_h2")
        s_tp = sem("s_tp"); s_th = sem("s_high_rows"); s_tpt = sem("s_tp_transposed"); s_tpte = sem("s_tpT_copied")
        s_ga = sem("s_gate"); s_row = sem("s_rows_ready"); s_rowd = [sem(f"s_rows_stored{k}") for k in range(2)]
        s_z = sem("s_zero_rows"); s_zd = sem("s_zeros_stored")
        s_gs = sem("s_gate_weights_scaled")
        s_nx = sem("s_top_negated"); s_ex = sem("s_top_exp"); s_cb = sem("s_comb_ready"); s_cbd = sem("s_comb_stored")
        s_mr = sem("s_members"); s_rp = sem("s_rank"); s_oha = sem("s_onehot"); s_ohu = sem("s_onehot_used")
        s_ct = sem("s_comb_transposed"); s_cte = sem("s_combT_copied"); s_b2 = sem("s_bias2")
        s_base = sem("s_base"); s_based = sem("s_base_stored")
        s_tabt = sem("s_table_columns"); s_tabp = sem("s_table_row"); s_tab = sem("s_table_ready")
        s_ixc = sem("s_index_copied")
        s_gr = [sem(f"s_tile_gathered{k}") for k in range(RING)]
        s_tr = sem("s_tile_transposed"); s_tc = sem("s_tile_copied"); s_l1 = sem("s_hidden"); s_sg = sem("s_sigmoid")
        s_lin = sem("s_linear_clipped"); s_u = sem("s_gated"); s_a = sem("s_a"); s_at = sem("s_a_transposed"); s_ahi = sem("s_a_high"); s_alo = sem("s_a_low")
        s_l2 = sem("s_y"); s_y = sem("s_y_weighted"); s_sc = [sem(f"s_scattered{k}") for k in range(2)]
        s_hold = sem("s_hold"); s_clear = sem("s_accumulator_free"); s_fin = sem("s_final")

        block = ctx.enter_context(nc.Block())

        def wait(eng, s, v):
            if v > 0:
                eng.wait_ge(s, v)

        NCONST = 3 * 16

        @block.sync
        def _(sp):
            sp.dma_start(idx_sb[:, :], idx).then_inc(s_idx, 16)
            sp.dma_start(C32[:, :], c32).then_inc(s_c, 16)
            sp.dma_start(C16[:, :], c16).then_inc(s_c, 16)
            sp.dma_start(srow_raw[:, :], sraw).then_inc(s_c, 16)
            def load_expert(e, k):
                sp.dma_start(stA[k], m1a[e, :, :].rearrange("e p n -> (e p) n")).then_inc(s_st[k], 16)
                sp.dma_start(stC[k], m1c[e, :, :].rearrange("e p n -> (e p) n")).then_inc(s_st[k], 16)
                sp.dma_start(stD[k], m2[e, :, :].rearrange("e p n -> (e p) n")).then_inc(s_st[k], 16)
            for k in range(STAGES):
                load_expert(slice(k, k + 1), k)
            with sp.Fori(0, NE // STAGES - 1) as i:
                for k in range(STAGES):
                    sp.wait_ge(s_hi, i * STAGES + (k + 1))
                    sp.wait_ge(s_lo, i * STAGES + (k + 1))
                    load_expert(bass.ds(i * STAGES + (k + STAGES), 1), k)
            for e in range(NE // STAGES * STAGES, NE):
                sp.wait_ge(s_hi, e - STAGES + 1)
                sp.wait_ge(s_lo, e - STAGES + 1)
                load_expert(slice(e, e + 1), e % STAGES)
            sp.wait_ge(s_hi, NE)
            sp.wait_ge(s_lo, NE)
            for dst, src in ((WQ, wq), (WK, wk), (WO, wo), (GW, gw)):
                sp.dma_start(dst[:, 0, :], src[0:P, :]).then_inc(s_aw, 16)
                n = src.shape[0] - P
                sp.dma_start(dst[0:n, 1, :], src[P:P + n, :]).then_inc(s_aw, 16)
            sp.dma_start(B2[:, :], b2).then_inc(s_aw, 16)
            sp.dma_start(W1s[D1:P, :, 2, :], W1s[0:D1, :, 2, :]).then_inc(s_dup, 16)
            sp.wait_ge(s_z, 1)
            for t in range(NT + 1):
                sp.dma_start(acc_odd[t * P:(t + 1) * P, :], lz[:, 0:D]).then_inc(s_zd, 16)
            sp.dma_start(out[ROWS:ROWS + P, :], lz[:, 0:D]).then_inc(s_zd, 16)
            sp.dma_start(t_dram[ROWS:ROWS + P, :], lz[:, 0:ROWT // 2]).then_inc(s_zd, 16)
            tv = t_dram[0:ROWS, :].rearrange("(t p) n -> p t n", p=P)
            for b in range(NB):
                sp.wait_ge(s_row, b + 1)
                sp.dma_start(tv[:, 2 * b:2 * b + 2, 0:D], rows32[:, b % 2, :, :]).then_inc(s_rowd[b % 2], 16)
            sp.wait_ge(s_cb, 2)
            sp.dma_start(tv[:, :, D:D + NE], combs).then_inc(s_cbd, 16)
            ov = out[0:ROWS, :].rearrange("(t p) n -> p t n", p=P)
            for b in range(NB):
                sp.wait_ge(s_base, b + 1)
                sp.dma_start(ov[:, 2 * b:2 * b + 2, :], h_all[:, 2 * b:2 * b + 2, :]).then_inc(s_based, 16)

        @block.gpsimd
        def _(po):
            po.memset(lz[:, :], 0.0).then_inc(s_z, 1)
            po.wait_ge(s_z, 1)
            po.memset(CT1[D1:D1 + 1, :], 1.0).then_inc(s_ms, 1)
            po.wait_ge(s_ms, 1)
            po.wait_ge(s_idx, 16)

            def take(dst, src, col, s):
                po.indirect_dma_start(out=dst, out_offset=None, in_=src,
                                      in_offset=bass.IndirectOffsetOnAxis(ap=idx_sb[:, col:col + 1], axis=0)).then_inc(s, 16)
            for j in range(2):
                take(G2w[:, 384 * j:384 * (j + 1)], x2, 40 + j, s_g2)
            for j in range(8):
                take(G1w[:, 96 * j:96 * (j + 1)], x1, 32 + j, s_g1)
            for k in range(2):
                for j in range(16):
                    q = 16 * k + j
                    take(G0w[:, 24 * q:24 * (q + 1)], x0, q, s_g0[k])

            po.wait_ge(s_he, NB)
            po.memset(vx[:, :, :, :], 1.0).then_inc(s_ms, 1)
            po.wait_ge(s_ms, 2)
            po.memset(tpT[D1:D1 + 1, :, 1, :], 1.0).then_inc(s_ms, 1)
            po.wait_ge(s_ms, 3)
            po.memset(attT[D1:D1 + 1, :, 1, :], 1.0).then_inc(s_ms, 1)
            po.wait_ge(s_base, NB)
            po.memset(Cb[D1:67, :, :], 1.0).then_inc(s_ms, 1)
            po.wait_ge(s_ms, 5)

            po.wait_ge(s_tab, 1)
            po.wait_ge(s_rowd[0], 16 * NB // 2)
            po.wait_ge(s_rowd[1], 16 * NB // 2)
            po.wait_ge(s_cbd, 16)
            po.wait_ge(s_zd, 16 * (NT + 3))
            po.wait_ge(s_based, 16 * NB)

            def index(tile, slot, done):
                c = po.value_load(tab[0:1, tile], min_val=0, max_val=NE * QT)
                po.tensor_copy(ixr[:, slot:slot + 1], Li[:, bass.ds(c, 1)]).then_inc(s_ixc, 1)
                po.wait_ge(s_ixc, done)

            def gather(slot):
                po.indirect_dma_start(out=Gr32[:, slot, :], out_offset=None, in_=t_dram,
                                      in_offset=bass.IndirectOffsetOnAxis(ap=ixr[:, slot:slot + 1], axis=0)).then_inc(s_gr[slot], 16)
            for t in range(AHEAD):
                index(slice(t, t + 1), t, t + 1)
                gather(t)
            with po.Fori(0, STEPS // RING) as i:
                for u in range(RING):
                    po.wait_ge(s_y, i * RING + (u + 2))
                    po.sem_inc(s_hold, 1)
                    if u >= 2:
                        po.wait_ge(s_sc[u % 2], i * (RING // 2 * 16) + 16 * (u // 2))
                    po.sem_inc(s_clear, 1)
                    po.indirect_dma_start(out=(out, acc_odd)[u % 2],
                                          out_offset=bass.IndirectOffsetOnAxis(ap=ixr[:, u:u + 1], axis=0),
                                          in_=yv[:, u % 4, :], in_offset=None, compute_op=ALU.add).then_inc(s_sc[u % 2], 16)
                    v = (u + AHEAD) % RING
                    c = po.value_load(tab[0:1, bass.ds(i * RING + (u + AHEAD), 1)], min_val=0, max_val=NE * QT)
                    po.tensor_copy(ixr[:, v:v + 1], Li[:, bass.ds(c, 1)]).then_inc(s_ixc, 1)
                    po.wait_ge(s_ixc, i * RING + (u + 1 + AHEAD))
                    po.sem_inc(s_hold, 1)
                    gather(v)
                for k in range(2):
                    po.wait_ge(s_sc[k], i * (RING // 2 * 16) + RING // 2 * 16)
                    po.sem_inc(s_hold, 1)
            for k in range(RING):
                po.wait_ge(s_gr[k], 16 * (STEPS // RING + (1 if k < AHEAD else 0)))
            po.dma_start(out[0:ROWS, :], acc_odd[0:ROWS, :], accum_op=ALU.add, max_dma_last_dim=4096).then_inc(s_fin, 16)
            po.wait_ge(s_fin, 16)

        chain = {}

        def link(eng, ins):
            chain["n"] = chain.get("n", 0) + 1
            ins.then_inc(s_dv, 1)
            eng.wait_ge(s_dv, chain["n"])

        @block.vector
        def _(ve):
            ve.wait_ge(s_c, NCONST)
            ve.tensor_scalar(srow[:, :], srow_raw[:, :], S1, None, ALU.mult).then_inc(s_sr, 1)
            ve.wait_ge(s_sr, 1)

            def low_parts(e, k, n):
                ve.wait_ge(s_hi, n)
                ve.scalar_tensor_tensor(out=W1s[:, e, 1, :], in0=stA[k], scalar=srow[:, 0:1],
                                        in1=W1s[:, e, 0, :], op0=ALU.mult, op1=ALU.subtract)
                ve.scalar_tensor_tensor(out=W1s[0:67, e, 3, :], in0=stC[k], scalar=srow[0:67, 1:2],
                                        in1=W1s[0:67, e, 2, :], op0=ALU.mult, op1=ALU.subtract)
                ve.scalar_tensor_tensor(out=W2s[:, e, 1, :], in0=stD[k], scalar=S2,
                                        in1=W2s[:, e, 0, :], op0=ALU.mult, op1=ALU.subtract).then_inc(s_lo, 1)

            def low(e):
                low_parts(slice(e, e + 1), e % STAGES, e + 1)
            with ve.Fori(0, 2) as i:
                for k in range(STAGES):
                    low_parts(bass.ds(i * STAGES + k, 1), k, i * STAGES + (k + 1))
            ve.wait_ge(s_g2, 32)
            ve.tensor_copy(B2r.rearrange("p b (j f) -> p j b f", j=2), G2).then_inc(s_by, 1)
            ve.wait_ge(s_g1, 16 * 8)
            ve.tensor_copy(B1r.rearrange("p b (j f) -> p j b f", j=8), G1).then_inc(s_by, 1)
            low(6)
            for k in range(2):
                ve.wait_ge(s_x, 1 + k)
                ve.tensor_copy(XT2[:, :, 4 * k:4 * k + 4, :],
                               bank[k][0:96, :].rearrange("p (b h g) -> p h b g", b=4, h=8)).then_inc(s_xe, 1)
            low(7)
            ve.wait_ge(s_x, 3)
            ve.tensor_copy(o2, bank[2][:, 0:64]).then_inc(s_xe, 1)
            for k in range(2):
                ve.wait_ge(s_x, 4 + k)
                ve.tensor_copy(XT1[:, :, 4 * k:4 * k + 4, :],
                               bank[k][0:96, :].rearrange("p (b h g) -> p h b g", b=4, h=2)).then_inc(s_xe, 1)
            low(8)
            ve.wait_ge(s_x, 6)
            ve.tensor_copy(o1, bank[2][:, 0:256].rearrange("p (b e) -> p b e", b=4)).then_inc(s_xe, 1)
            low(9)
            for k in range(4):
                ve.wait_ge(s_x, 7 + k)
                ve.tensor_scalar(CT1[0:EMB, 512 * k:512 * k + 512], bank[3 + k % 2][0:EMB, :], BC[0:EMB, 1:2], None,
                                 ALU.add).then_inc(s_xe, 1)
            low(10)
            for k in range(4):
                ve.wait_ge(s_x, 11 + k)
                for j in range(2):
                    ins = ve.tensor_scalar(CT0[EMB:P, 512 * k + 256 * j:512 * k + 256 * (j + 1)],
                                           l1bank[k % 2][j][EMB:P, 0:256], BC[EMB:P, 0:1], None, ALU.add)
                ins.then_inc(s_xe, 1)
            CT0v = CT0.rearrange("p (b k t) -> p b k t", b=8, k=2)
            n = 14
            for k in range(2):
                ve.wait_ge(s_by, 1)
                ve.wait_ge(s_g0[k], 16 * 16)
                ve.tensor_copy(B0r[:, k].rearrange("p b (j c) -> p j b c", j=16), G0[:, k]).then_inc(s_by, 1)
                for q in range(2):
                    if k == 0 or q == 0:
                        low(11 + 2 * k + q)
                    ve.wait_ge(s_x, n + 1)
                    ve.tensor_copy(X0T[:, q, :], bank[q][0:48, :]).then_inc(s_xe, 1)
                    if k == 1:
                        low(14 + q)
                    ve.wait_ge(s_x, n + 2)
                    ve.tensor_scalar(CT0v[0:EMB, 4 * q:4 * q + 4, k, :],
                                     bank[2 + q][0:EMB, :].rearrange("p (b t) -> p b t", b=4), BC[0:EMB, 0:1], None,
                                     ALU.add).then_inc(s_xe, 1)
                    n += 2
            ve.wait_ge(s_aw, 16 * 9)
            ve.tensor_scalar(GS[:, 0, :], GW[:, 0, :], srow_raw[:, 0:1], None, ALU.mult)
            ve.tensor_scalar(GS[0:D1 + 1, 1, :], GW[0:D1 + 1, 1, :], srow_raw[0:D1 + 1, 1:2], None, ALU.mult).then_inc(s_gs, 1)

            def rsqrt(y, v, s0, s1, s2):
                link(ve, ve.tensor_scalar(y.bitcast(I32), v.bitcast(I32), -0.5, MAGIC, ALU.mult, ALU.add))
                for _ in range(3):
                    link(ve, ve.tensor_tensor(s0, y, y, ALU.mult))
                    link(ve, ve.tensor_tensor(s1, s0, v, ALU.mult))
                    link(ve, ve.tensor_scalar(s2, s1, -0.5, 1.5, ALU.mult, ALU.add))
                    link(ve, ve.tensor_tensor(y, y, s2, ALU.mult))

            for t in range(NT):
                ve.wait_ge(s_he, t // 2 + 1)
                ins = ve.bn_stats(bst[:, t, :], h_all[:, t, :])
            link(ve, ins)
            for t in range(NT):
                ins = ve.bn_aggr(mv[:, t, :], bst[:, t, :])
            link(ve, ins)
            link(ve, ve.tensor_scalar(ve1, mv[:, :, 1], LN_EPS, None, ALU.add))
            rsqrt(rs1, ve1, nw[:, 0, :], nw[:, 1, :], nw[:, 2, :])

            def normalise(b):
                p = b % 2
                wait(ve, s_hnt, b - 1)
                for j in range(2):
                    t = 2 * b + j
                    ins = ve.tensor_scalar(hn[:, p, j, :], h_all[:, t, :], mv[:, t, 0:1], rs1[:, t:t + 1],
                                           ALU.subtract, ALU.mult)
                ins.then_inc(s_hn, 1)

            def phi(b):
                p = b % 2
                ve.wait_ge(s_ke, b + 1)
                wait(ve, s_stt, b - 1)
                ve.scalar_tensor_tensor(out=phk[:, p, :, :], in0=ek, scalar=1.0, in1=rk,
                                        op0=ALU.min, op1=ALU.add).then_inc(s_phk, 1)
                ve.wait_ge(s_qe, b + 1)
                wait(ve, s_nd, b - 1)
                ve.scalar_tensor_tensor(out=phq[:, p, 0, :], in0=eq[:, 0, :], scalar=1.0, in1=rq[:, 0, :],
                                        op0=ALU.min, op1=ALU.add)
                ve.scalar_tensor_tensor(out=phq[0:D1, p, 1, :], in0=eq[0:D1, 1, :], scalar=1.0,
                                        in1=rq[0:D1, 1, :], op0=ALU.min, op1=ALU.add).then_inc(s_phq, 1)

            def mask_state(b):
                p = b % 2
                ve.wait_ge(s_stt, b + 1)
                wait(ve, s_nd, b - 1)
                ve.tensor_tensor(kvm[:, p, 0, :], bank[4][:, 0:128], bmask, ALU.mult)
                ve.scalar_tensor_tensor(out=kvm[:, p, 1, :], in0=bmask, scalar=bank[4][:, 128:129], in1=bmask,
                                        op0=ALU.mult, op1=ALU.add)
                ve.tensor_tensor(kvm[0:D1, p, 2, 0:D1], bank[4][0:D1, 256:256 + D1], bmask[0:D1, 0:D1], ALU.mult)
                ve.scalar_tensor_tensor(out=kvm[0:D1, p, 3, 0:D1], in0=bmask[0:D1, 0:D1],
                                        scalar=bank[4][0:D1, 320:321], in1=bmask[0:D1, 0:D1],
                                        op0=ALU.mult, op1=ALU.add).then_inc(s_kvm, 1)

            def divide(b):
                p = b % 2
                ve.wait_ge(s_dn, b + 1)
                ve.reciprocal(dn[:, p, 0:256], dn[:, p, 0:256])
                link(ve, ve.reciprocal(dn[0:D1, p, 256:512], dn[0:D1, p, 256:512]))
                wait(ve, s_o, b - 1)
                ve.tensor_tensor(attT[:, p, 0, :], bank[5][:, 0:256], dn[:, p, 0:256], ALU.mult)
                ve.tensor_tensor(attT[0:D1, p, 1, :], bank[5][0:D1, 256:512], dn[0:D1, p, 256:512],
                                 ALU.mult).then_inc(s_att, 1)

            def second_norm(b):
                p = b % 2
                h2 = h_all[:, 2 * b:2 * b + 2, :]
                ve.wait_ge(s_o, b + 1)
                link(ve, ve.tensor_tensor(h2, h2, bank[4][:, 0:2 * D].rearrange("p (t n) -> p t n", t=2), ALU.add))
                for j in range(2):
                    ins = ve.bn_stats(bst[:, 2 * b + j, :], h_all[:, 2 * b + j, :])
                ins.then_inc(s_h2, 1)
                ve.wait_ge(s_h2, b + 1)
                for j in range(2):
                    ins = ve.bn_aggr(mv2[:, 2 * b + j, :], bst[:, 2 * b + j, :])
                link(ve, ins)
                var = mv2[:, 2 * b:2 * b + 2, 1]
                link(ve, ve.tensor_scalar(vv[:, p, 0, :], var, LN_EPS, None, ALU.add))
                link(ve, ve.scalar_tensor_tensor(out=vv[:, p, 1, :], in0=vv[:, p, 0, :], scalar=RMS_EPS, in1=var,
                                                 op0=ALU.mult, op1=ALU.add))
                f = "p a t -> p (a t)"
                rsqrt(rr[:, p, :, :].rearrange(f), vv[:, p, :, :].rearrange(f), nw2[:, p, 0, :], nw2[:, p, 1, :],
                      nw2[:, p, 2, :])
                wait(ve, s_tpt, b - 1)
                wait(ve, s_th, b - 1)
                for j in range(2):
                    ins = ve.tensor_scalar(tp[:, p, j, :], h_all[:, 2 * b + j, :], mv2[:, 2 * b + j, 0:1],
                                           rr[:, p, 1, j:j + 1], ALU.subtract, ALU.mult)
                ins.then_inc(s_tp, 1)
                link(ve, ve.tensor_tensor(nw2[:, p, 0, 0:2], mv2[:, 2 * b:2 * b + 2, 0], rr[:, p, 0, :], ALU.mult))
                ve.tensor_scalar(nw2[:, p, 1, 0:2], nw2[:, p, 0, 0:2], -1.0, None, ALU.mult)
                link(ve, ve.tensor_scalar(nw2[:, p, 2, 0:2], rr[:, p, 0, :], 1.0, None, ALU.add))
                for j in range(2):
                    t = 2 * b + j
                    ve.tensor_scalar(h_all[:, t, :], h_all[:, t, :], nw2[:, p, 2, j:j + 1], nw2[:, p, 1, j:j + 1],
                                     ALU.mult, ALU.add)
                ve.wait_ge(s_th, b + 1)
                tt2 = tp[:, p, :, :]
                r2 = rows[:, p, :, :]
                ve.tensor_tensor(r2[:, :, D:D + D1], tt2[:, :, P:D], r2[:, :, P:D], ALU.subtract)
                ve.tensor_tensor(r2[:, :, D + D1:2 * D], tt2[:, :, 0:P], r2[:, :, 0:P], ALU.subtract).then_inc(s_row, 1)

            def gates(b):
                ve.wait_ge(s_ga, b + 1)
                ve.tensor_copy(g_all[:, 2 * b:2 * b + 2, :], bank[7][:, 0:32].rearrange("p (t e) -> p t e", t=2))\
                  .then_inc(s_gs, 1)

            for s in range(NB + 3):
                if s < NB:
                    normalise(s)
                if 0 <= s - 2 < NB:
                    second_norm(s - 2)
                if 0 <= s - 1 < NB:
                    mask_state(s - 1)
                if s < NB:
                    phi(s)
                if 0 <= s - 1 < NB:
                    divide(s - 1)
                if 0 <= s - 3 < NB:
                    gates(s - 3)

            ve.wait_ge(s_gs, NB + 1)
            for t in range(NT):
                ins = ve.max(mx8[:, t, :], g_all[:, t, :])
            link(ve, ins)
            for t in range(NT):
                ins = ve.max_index(ix8[:, t, :], mx8[:, t, :], g_all[:, t, :])
            top = mx8[:, :, 0:TOPK]
            ve.tensor_tensor(ew[:, :, :], top, mx8[:, :, 0:1].broadcast_to([P, NT, TOPK]), ALU.subtract).then_inc(s_nx, 1)
            link(ve, ins)
            link(ve, ve.tensor_copy(ixf[:, :, :], ix8[:, :, 0:TOPK]))
            full = [P, NT, TOPK, NE]
            link(ve, ve.tensor_tensor(oh, iota16.rearrange("p (a k e) -> p a k e", a=1, k=1).broadcast_to(full),
                                      ixf[:, :, :].rearrange("p t (k e) -> p t k e", e=1).broadcast_to(full), ALU.is_equal))
            with nc.allow_low_precision(reason="sums of zeros and one one are exact"):
                ve.tensor_reduce(Mx, oh.rearrange("p t k e -> p t e k"), AX.X, ALU.add).then_inc(s_mr, 1)
            ve.wait_ge(s_ex, 1)
            link(ve, ve.tensor_reduce(es, ew[:, :, :], AX.X, ALU.add))
            link(ve, ve.reciprocal(es, es))
            link(ve, ve.tensor_tensor(ew[:, :, :], ew[:, :, :],
                                      es.rearrange("p (t k) -> p t k", k=1).broadcast_to([P, NT, TOPK]), ALU.mult))
            link(ve, ve.tensor_tensor(ohw, oh, ew[:, :, :].rearrange("p t (k e) -> p t k e", e=1).broadcast_to(full), ALU.mult))
            ve.tensor_reduce(comb, ohw.rearrange("p t k e -> p t e k"), AX.X, ALU.add).then_inc(s_cb, 1)
            ve.wait_ge(s_cb, 1)
            ve.tensor_scalar(combs, comb, 1.0 / (SA * S2), None, ALU.mult).then_inc(s_cb, 1)
            ve.wait_ge(s_rp, 1)
            ve.wait_ge(s_cb, 1)
            link(ve, ve.tensor_copy(rank[:, :, :], bank[0][:, 0:NT * NE].rearrange("p (t e) -> p t e", t=NT)))
            link(ve, ve.tensor_tensor(ohw, oh, rank[:, :, :].rearrange("p t (k e) -> p t k e", k=1).broadcast_to(full), ALU.mult))
            link(ve, ve.tensor_reduce(rkk[:, :, :], ohw, AX.X, ALU.add))
            link(ve, ve.tensor_copy(rki[:, 0, :, :], rkk[:, :, :]))
            link(ve, ve.tensor_single_scalar(rki[:, 1, :, :], rki[:, 0, :, :], 7, ALU.logical_shift_right))
            link(ve, ve.tensor_copy(rkq[:, :, :], rki[:, 1, :, :]))
            link(ve, ve.scalar_tensor_tensor(out=rkr[:, :, :], in0=rkq[:, :, :], scalar=-128.0, in1=rkk[:, :, :],
                                             op0=ALU.mult, op1=ALU.add))
            link(ve, ve.scalar_tensor_tensor(out=rkq[:, :, :], in0=ixf[:, :, :], scalar=float(QT), in1=rkq[:, :, :],
                                             op0=ALU.mult, op1=ALU.add))
            for k in range(4):
                ve.wait_ge(s_ct, k + 1)
                ve.tensor_copy(cT[:, k, :], bank[3][0:NE, :]).then_inc(s_cte, 1)
            for t in range(NT):
                ins = ve.tensor_scalar(idv[:, t:t + 1], pcol, float(P * t + 1), None, ALU.add)
            link(ve, ins)
            for n in range(NT * TOPK):
                t, k = divmod(n, TOPK)
                wait(ve, s_ohu, n - 7)
                ve.tensor_scalar(Aoh[:, n % 8, :], iota256, rkq[:, t, k:k + 1], idv[:, t:t + 1], ALU.is_equal, ALU.mult)
                ve.tensor_scalar(Boh[:, n % 8, :], iota256[:, 0:128], rkr[:, t, k:k + 1], None,
                                 ALU.is_equal).then_inc(s_oha, 1)
            link(ve, ve.tensor_scalar(cnt[:, 0, :], bank[0][:, 256:256 + NE], 127.0, None, ALU.add))
            link(ve, ve.tensor_copy(cnt_i, cnt[:, 0, :]))
            link(ve, ve.tensor_single_scalar(cnt_i, cnt_i, 7, ALU.logical_shift_right))
            link(ve, ve.tensor_copy(cnt[:, 1, :], cnt_i))
            link(ve, ve.tensor_tensor_scan(cnt[:, 2, :], ones16[:, 0:NE], cnt[:, 1, :], 0.0, ALU.mult, ALU.add))
            link(ve, ve.tensor_scalar(cnt[:, 3, :], cnt[:, 2, :], pcol, None, ALU.is_le))
            link(ve, ve.tensor_reduce(tt_e[:, 0:1], cnt[:, 3, :], AX.X, ALU.add))
            link(ve, ve.tensor_tensor(cnt[:, 3, :], cnt[:, 3, :], cnt[:, 1, :], ALU.mult))
            link(ve, ve.tensor_reduce(tt_e[:, 1:2], cnt[:, 3, :], AX.X, ALU.add))
            link(ve, ve.tensor_tensor(tt_e[:, 1:2], pcol, tt_e[:, 1:2], ALU.subtract))
            link(ve, ve.scalar_tensor_tensor(out=tt_e[:, 2:3], in0=tt_e[:, 0:1], scalar=float(QT), in1=tt_e[:, 1:2],
                                             op0=ALU.mult, op1=ALU.add))
            ve.tensor_scalar(tt_e[:, 2:3], tt_e[:, 2:3], float(NE * QT), None, ALU.min)
            ve.tensor_scalar(tt_e[:, 3:4], tt_e[:, 0:1], float(NE - 1), None, ALU.min).then_inc(s_tabt, 1)
            ve.wait_ge(s_ohu, NT * TOPK)
            link(ve, ve.tensor_scalar(lpad, bank[1][:, 0:256], 0.0, pcol_pad, ALU.is_equal, ALU.mult))
            ve.scalar_tensor_tensor(out=Li[:, 0:256], in0=bank[1][:, 0:256], scalar=-1.0, in1=lpad,
                                    op0=ALU.add, op1=ALU.add)
            ve.tensor_scalar(Li[:, 256:257], pcol_pad, -1.0, None, ALU.add)
            ve.wait_ge(s_tabp, 1)
            ve.tensor_copy(tab[:, :], bank[2][0:1, 0:2 * P]).then_inc(s_tab, 1)
            for b in range(NB):
                ve.wait_ge(s_b2, b + 1)
                h2 = h_all[:, 2 * b:2 * b + 2, :]
                ve.tensor_tensor(h2, h2, bank[4 + b % 2][:, 0:2 * D].rearrange("p (t n) -> p t n", t=2), ALU.add)\
                  .then_inc(s_base, 1)

            def gated(p, n):
                ve.wait_ge(s_l1, n)
                ve.tensor_scalar(lin[:, p, :], bank[2 + 2 * p][:, 0:HID], (LIMIT + 1) * S1, (1 - LIMIT) * S1,
                                 ALU.min, ALU.max).then_inc(s_lin, 1)
                ve.wait_ge(s_sg, n)
                ve.wait_ge(s_lin, n)
                ve.scalar_tensor_tensor(out=uu[:, p, :], in0=bank[1 + 2 * p][:, 0:HID], scalar=LIMIT * S1,
                                        in1=lin[:, p, :], op0=ALU.min, op1=ALU.mult).then_inc(s_u, 1)

            def times_sigmoid(p, n):
                ve.wait_ge(s_u, n)
                ve.scalar_tensor_tensor(out=av[:, p, :], in0=sg[:, p, :], scalar=SIGMAX, in1=uu[:, p, :],
                                        op0=ALU.min, op1=ALU.mult).then_inc(s_a, 1)

            def low_half(p, n):
                ve.wait_ge(s_ahi, n)
                ve.scalar_tensor_tensor(out=al[:, p, :], in0=bank[6][:, 0:HID], scalar=SA / (S1 * S1),
                                        in1=ah[:, p, :], op0=ALU.mult, op1=ALU.subtract).then_inc(s_alo, 1)
            gated(0, 1)
            times_sigmoid(0, 1)
            gated(1, 2)
            low_half(0, 1)
            times_sigmoid(1, 2)
            with ve.Fori(0, STEPS // RING) as i:
                for u in range(RING):
                    gated(u % 2, i * RING + (u + 3))
                    low_half((u + 1) % 2, i * RING + (u + 2))
                    times_sigmoid(u % 2, i * RING + (u + 3))

        @block.scalar
        def _(ac):
            for dst, src in ((W2T, w2t.rearrange("(h p) e -> p h e", p=96)), (W1T, w1t.rearrange("(h p) e -> p h e", p=96)),
                             (W0T, w0t), (P1, p1), (P2, p2), (BC[:, :], bcol), (WF0[:, :], wft[0:P, :]),
                             (WF1[:, :], wft[P:D + 1, :])):
                ac.dma_start(dst, src).then_inc(s_lw, 16)
            ac.wait_ge(s_sr, 1)

            def high_parts(e, k):
                ac.activation(W1s[:, e, 0, :], stA[k], ACT.Copy, scale=srow[:, 0:1])
                ac.activation(W1s[0:67, e, 2, :], stC[k], ACT.Copy, scale=srow[0:67, 2:3])
                ac.activation(W2s[:, e, 0, :], stD[k], ACT.Copy, scale=S2).then_inc(s_hi, 1)
            with ac.Fori(0, NE // STAGES) as i:
                for k in range(STAGES):
                    ac.wait_ge(s_st[k], i * 48 + 48)
                    ac.sem_inc(s_ah0, 1)
                    high_parts(bass.ds(i * STAGES + k, 1), k)
            for e in range(NE // STAGES * STAGES, NE):
                ac.wait_ge(s_st[e % STAGES], 48 * (e // STAGES + 1))
                high_parts(slice(e, e + 1), e % STAGES)
            ac.wait_ge(s_lo, NE)
            for b in range(NB):
                ac.wait_ge(s_h, b + 1)
                ac.activation(h_all[:, 2 * b:2 * b + 2, :], bank[4 + b % 4][:, 0:2 * D].rearrange("p (t n) -> p t n", t=2),
                              ACT.Copy).then_inc(s_he, 1)
            ac.wait_ge(s_ms, 4)

            def copy_hnT(b):
                p = b % 2
                ac.wait_ge(s_hnt, b + 1)
                wait(ac, s_q, b - 1)
                ac.activation(hnT[:, p, 0, :], bank[0][:, 0:256], ACT.Copy)
                ac.activation(hnT[0:D1, p, 1, :], bank[0][0:D1, 256:512], ACT.Copy).then_inc(s_hnte, 1)

            def kv_parts(b):
                p = b % 2
                wait(ac, s_phk, b)
                wait(ac, s_stt, b - 1)
                for j in range(2):
                    ac.wait_ge(s_kv, 2 * b + j + 1)
                    ac.activation(ek[:, j, :], bank[1 + j][:, 0:D], ACT.Exp)
                    ac.activation(rk[:, j, :], bank[1 + j][:, 0:D], ACT.Relu)
                    ac.activation(vx[:, p, j, 0:P], bank[1 + j][:, D:D + P], ACT.Copy)
                    ins = ac.activation(vx[:, p, j, P + 1:D + 1], bank[1 + j][:, D + P:2 * D], ACT.Copy)
                ins.then_inc(s_ke, 1)

            def q_parts(b):
                p = b % 2
                ac.wait_ge(s_q, b + 1)
                wait(ac, s_phq, b)
                for f, dst in ((ACT.Exp, eq), (ACT.Relu, rq)):
                    ac.activation(dst[:, 0, :], bank[3][:, 0:256], f)
                    ins = ac.activation(dst[0:D1, 1, :], bank[3][0:D1, 256:512], f)
                ins.then_inc(s_qe, 1)

            def den(b):
                p = b % 2
                ac.wait_ge(s_nd, b + 1)
                wait(ac, s_att, b - 1)
                ac.activation(dn[:, p, 0:256], bank[6][:, 0:256], ACT.Copy, bias=ATT_EPS)
                ac.activation(dn[0:D1, p, 256:512], bank[6][0:D1, 256:512], ACT.Copy, bias=ATT_EPS).then_inc(s_dn, 1)

            def high_rows(b):
                p = b % 2
                ac.wait_ge(s_tp, b + 1)
                wait(ac, s_rowd[p], 16 * (b // 2))
                ac.activation(rows[:, p, :, 0:D], tp[:, p, :, :], ACT.Copy).then_inc(s_th, 1)

            def copy_tpT(b):
                p = b % 2
                ac.wait_ge(s_tpt, b + 1)
                wait(ac, s_ga, b - 1)
                ac.activation(tpT[:, p, 0, :], bank[0][:, 0:256], ACT.Copy)
                ac.activation(tpT[0:D1, p, 1, :], bank[0][0:D1, 256:512], ACT.Copy).then_inc(s_tpte, 1)

            for s in range(NB + 3):
                if s < NB:
                    copy_hnT(s)
                if 0 <= s - 2 < NB:
                    high_rows(s - 2)
                if s < NB:
                    kv_parts(s)
                    q_parts(s)
                if 0 <= s - 2 < NB:
                    copy_tpT(s - 2)
                if 0 <= s - 1 < NB:
                    den(s - 1)
            ac.wait_ge(s_nx, 1)
            ac.activation(ew[:, :, :], ew[:, :, :], ACT.Exp).then_inc(s_ex, 1)

            ac.wait_ge(s_ms, 5)
            ac.sem_inc(s_y, 1)
            ac.sem_inc(s_clear, 2)

            def copy_tile(p, n):
                ac.wait_ge(s_tr, n)
                ac.activation(Ct[:, p, :, :], trs[p][:, 0:384].rearrange("p (c t) -> p c t", c=3), ACT.Copy)
                ac.activation(Cb[0:D1, p, :], trs[p][0:D1, 128:256], ACT.Copy).then_inc(s_tc, 1)

            def sigmoid(p, n):
                ac.wait_ge(s_l1, n)
                ac.activation(sg[:, p, :], bank[1 + 2 * p][:, 0:HID], ACT.Sigmoid, scale=ALPHA / S1).then_inc(s_sg, 1)

            def high_half(p, n):
                ac.wait_ge(s_at, n)
                ac.activation(ah[:, p, :], bank[6][:, 0:HID], ACT.Copy, scale=SA / (S1 * S1)).then_inc(s_ahi, 1)
            copy_tile(0, 1)
            copy_tile(1, 2)
            sigmoid(0, 1)
            sigmoid(1, 2)
            high_half(0, 1)
            copy_tile(0, 3)
            with ac.Fori(0, STEPS // RING) as i:
                for u in range(RING):
                    e = ac.value_load(tab[0:1, bass.ds(i * RING + (P + u), 1)], min_val=0, max_val=NE - 1)
                    sigmoid(u % 2, i * RING + (u + 3))
                    high_half((u + 1) % 2, i * RING + (u + 2))
                    copy_tile((u + 1) % 2, i * RING + (u + 4))
                    ac.wait_ge(s_l2, i * RING + (u + 1))
                    ac.sem_inc(s_ah0, 1)
                    ac.wait_ge(s_clear, i * RING + (u + 1))
                    ac.sem_inc(s_ah0, 1)
                    ac.activation(yv[:, u % 4, :], bank[5][:, 0:D], ACT.Copy,
                                  scale=Gr32[:, u, bass.ds(e + D, 1)]).then_inc(s_y, 1)

        @block.tensor
        def _(pe):
            mm = pe.matmul
            pe.wait_ge(s_c, NCONST)
            pe.wait_ge(s_lw, 16 * 8)
            pe.wait_ge(s_by, 1)
            for k in range(2):
                for j in range(4):
                    ins = pe.transpose(bank[k][0:96, P * j:P * (j + 1)], B2r[:, 4 * k + j, :], ident)
                ins.then_inc(s_x, 1)
            pe.wait_ge(s_xe, 2)
            for h in range(8):
                ins = mm(bank[2][:, 0:64], XT2[:, h, :, :], W2T[:, h, :], start=h == 0, stop=h == 7)
            ins.then_inc(s_x, 1)
            pe.wait_ge(s_by, 2)
            for k in range(2):
                for j in range(4):
                    ins = pe.transpose(bank[k][0:96, P * j:P * (j + 1)], B1r[:, 4 * k + j, :], ident)
                ins.then_inc(s_x, 1)
            pe.wait_ge(s_xe, 5)
            for b in range(4):
                for h in range(2):
                    ins = mm(bank[2][:, 64 * b:64 * (b + 1)], XT1[:, h, 2 * b:2 * b + 2, :], W1T[:, h, :],
                             start=h == 0, stop=h == 1)
            ins.then_inc(s_x, 1)
            for k in range(4):
                if k >= 2:
                    pe.wait_ge(s_xe, 7 + k - 2)
                g = slice(32 * k, 32 * k + 32)
                mm(bank[3 + k % 2][0:EMB, :], o2[g, :], P2[g, :], start=True, stop=True).then_inc(s_x, 1)
            pe.wait_ge(s_xe, 10)
            for k in range(4):
                if k >= 2:
                    pe.wait_ge(s_xe, 11 + k - 2)
                for j in range(2):
                    g = slice(64 * j, 64 * j + 64)
                    ins = mm(l1bank[k % 2][j][EMB:P, 0:256], o1[g, k, :], P1[g, :], start=True, stop=True)
                ins.then_inc(s_x, 1)
            n = 14
            pe.wait_ge(s_xe, 10)
            for k in range(2):
                pe.wait_ge(s_by, 3 + k)
                for q in range(2):
                    pe.wait_ge(s_xe, n - 3 if k else 10)
                    for j in range(4):
                        ins = pe.transpose(bank[q][0:48, P * j:P * (j + 1)], B0r[:, k, 4 * q + j, :], ident)
                    ins.then_inc(s_x, 1)
                    pe.wait_ge(s_xe, n + 1)
                    mm(bank[2 + q][0:EMB, :], W0T, X0T[:, q, :], start=True, stop=True).then_inc(s_x, 1)
                    n += 2
            pe.wait_ge(s_xe, 22)
            for b in range(NB):
                wait(pe, s_he, b - 3)
                for j in range(2):
                    t = slice(P * (2 * b + j), P * (2 * b + j + 1))
                    o = bank[4 + b % 4][:, D * j:D * (j + 1)]
                    mm(o, CT0[:, t], WF0[:, :], start=True, stop=False)
                    ins = mm(o, CT1[:, t], WF1[:, :], start=False, stop=True)
                ins.then_inc(s_h, 1)

            pe.wait_ge(s_aw, 16 * 9)
            pe.wait_ge(s_he, NB)
            pe.wait_ge(s_ms, 4)

            def transposes(src, b, s):
                p = b % 2
                for j in range(2):
                    pe.transpose(bank[0][:, P * j:P * (j + 1)], src[:, p, j, 0:P], ident)
                    ins = pe.transpose(bank[0][0:D1, 256 + P * j:256 + P * (j + 1)], src[:, p, j, P:D], ident)
                ins.then_inc(s, 1)

            def kv(b):
                p = b % 2
                pe.wait_ge(s_hnte, b + 1)
                wait(pe, s_ke, b)
                for j in range(2):
                    t = slice(P * j, P * (j + 1))
                    mm(bank[1 + j][:, 0:2 * D], hnT[:, p, 0, t], WK[:, 0, :], start=True, stop=False)
                    mm(bank[1 + j][:, 0:2 * D], hnT[0:D1, p, 1, t], WK[0:D1, 1, :], start=False, stop=True).then_inc(s_kv, 1)

            def query(b):
                p = b % 2
                wait(pe, s_qe, b)
                mm(bank[3][:, 0:256], WQ[:, 0, 0:P], hnT[:, p, 0, :], start=True, stop=False)
                mm(bank[3][:, 0:256], WQ[0:D1, 1, 0:P], hnT[0:D1, p, 1, :], start=False, stop=True)
                mm(bank[3][0:D1, 256:512], WQ[:, 0, P:D], hnT[:, p, 0, :], start=True, stop=False)
                mm(bank[3][0:D1, 256:512], WQ[0:D1, 1, P:D], hnT[0:D1, p, 1, :], start=False, stop=True).then_inc(s_q, 1)

            def state(b):
                p = b % 2
                pe.wait_ge(s_phk, b + 1)
                wait(pe, s_h2, b)
                for j in range(2):
                    mm(bank[4][:, 0:129], phk[:, p, j, 0:P], vx[:, p, j, 0:129], start=j == 0, stop=j == 1)
                for j in range(2):
                    ins = mm(bank[4][0:D1, 256:321], phk[:, p, j, P:D], vx[:, p, j, 129:194], start=j == 0, stop=j == 1)
                ins.then_inc(s_stt, 1)

            def num_den(b):
                p = b % 2
                pe.wait_ge(s_kvm, b + 1)
                pe.wait_ge(s_phq, b + 1)
                wait(pe, s_att, b)
                for k in range(2):
                    mm(bank[5 + k][:, 0:256], kvm[:, p, k, :], phq[:, p, 0, :], start=True, stop=True)
                    ins = mm(bank[5 + k][0:D1, 256:512], kvm[0:D1, p, 2 + k, 0:D1], phq[0:D1, p, 1, :], start=True, stop=True)
                ins.then_inc(s_nd, 1)

            def project(b):
                p = b % 2
                pe.wait_ge(s_att, b + 1)
                for j in range(2):
                    t = slice(P * j, P * (j + 1))
                    o = bank[4][:, D * j:D * (j + 1)]
                    mm(o, attT[:, p, 0, t], WO[:, 0, :], start=True, stop=False)
                    ins = mm(o, attT[0:D1 + 1, p, 1, t], WO[0:D1 + 1, 1, :], start=False, stop=True)
                ins.then_inc(s_o, 1)

            def gate(b):
                p = b % 2
                pe.wait_ge(s_tpte, b + 1)
                pe.wait_ge(s_gs, b + 1)
                for j in range(2):
                    t = slice(P * j, P * (j + 1))
                    o = bank[7][:, NE * j:NE * (j + 1)]
                    mm(o, tpT[:, p, 0, t], GS[:, 0, :], start=True, stop=False)
                    ins = mm(o, tpT[0:D1 + 1, p, 1, t], GS[0:D1 + 1, 1, :], start=False, stop=True)
                ins.then_inc(s_ga, 1)

            for s in range(NB + 3):
                if s < NB:
                    wait(pe, s_tpte, s - 2)
                    pe.wait_ge(s_hn, s + 1)
                    transposes(hn, s, s_hnt)
                    kv(s)
                if 0 <= s - 1 < NB:
                    state(s - 1)
                if s < NB:
                    query(s)
                if 0 <= s - 2 < NB:
                    pe.wait_ge(s_tp, s - 1)
                    pe.wait_ge(s_hnte, min(s + 1, NB))
                    transposes(tp, s - 2, s_tpt)
                if 0 <= s - 1 < NB:
                    num_den(s - 1)
                if 0 <= s - 2 < NB:
                    gate(s - 2)
                if 0 <= s - 1 < NB:
                    project(s - 1)

            pe.wait_ge(s_mr, 1)
            R0 = bank[0][:, 0:NT * NE]
            mm(R0, ustrict, Mx.rearrange("p t e -> p (t e)"), start=True, stop=False)
            for j in range(NT - 1):
                mm(bank[0][:, NE * (j + 1):NE * NT].rearrange("p (t e) -> p t e", e=NE), ones16,
                   Mx[:, j:j + 1, :].broadcast_to([P, NT - 1 - j, NE]), start=False, stop=j == NT - 2)
            for j in range(NT):
                ins = mm(bank[0][:, 256:256 + NE], ones16, Mx[:, j, :], start=j == 0, stop=j == NT - 1)
            ins.then_inc(s_rp, 1)
            pe.wait_ge(s_cb, 1)
            for k in range(4):
                wait(pe, s_cte, k)
                for j in range(4):
                    ins = pe.transpose(bank[3][0:NE, P * j:P * (j + 1)], comb[:, 4 * k + j, :], ident)
                ins.then_inc(s_ct, 1)
            for n in range(NT * TOPK):
                pe.wait_ge(s_oha, n + 1)
                ins = mm(bank[1][:, 0:256], Boh[:, n % 8, :], Aoh[:, n % 8, :], start=n == 0, stop=n == NT * TOPK - 1)
                ins.then_inc(s_ohu, 1)
            pe.wait_ge(s_tabt, 1)
            for k in range(2):
                ins = mm(bank[2][0:1, P * k:P * (k + 1)], tt_e[:, 2 + k:3 + k], ident, start=True, stop=True)
            ins.then_inc(s_tabp, 1)
            for b in range(NB):
                pe.wait_ge(s_cte, b // 2 + 1)
                wait(pe, s_base, b - 1)
                for j in range(2):
                    t = 2 * b + j
                    ins = mm(bank[4 + b % 2][:, D * j:D * (j + 1)], cT[:, t // 4, P * (t % 4):P * (t % 4 + 1)],
                             B2[:, :], start=True, stop=True)
                ins.then_inc(s_b2, 1)

            pe.wait_ge(s_dup, 16)
            pe.wait_ge(s_tab, 1)
            pe.wait_ge(s_base, NB)

            def tile_transposes(slot, p, n):
                pe.wait_ge(s_gr[slot], n)
                for c in range(3):
                    ins = pe.transpose(trs[p][:, P * c:P * (c + 1)], Gr[:, slot, P * c:P * (c + 1)], ident16)
                ins.then_inc(s_tr, 1)

            def hidden(p, e):
                for m in range(2):
                    o = bank[1 + m + 2 * p][:, 0:HID]
                    c = slice(HID * m, HID * (m + 1))
                    mm(o, Ct[:, p, 0, :], W1s[:, e, 0, c], start=True, stop=False)
                    mm(o, Ct[:, p, 2, :], W1s[:, e, 0, c], start=False, stop=False)
                    mm(o, Ct[:, p, 0, :], W1s[:, e, 1, c], start=False, stop=False)
                    mm(o, Ct[:, p, 1, :], W1s[:, e, 2, c], start=False, stop=False)
                    ins = mm(o, Cb[0:67, p, :], W1s[0:67, e, 3, c], start=False, stop=True)
                ins.then_inc(s_l1, 1)

            def hidden_transposes(p):
                for m in range(HC):
                    ins = pe.transpose(bank[6][:, P * m:P * (m + 1)], av[:, p, P * m:P * (m + 1)], ident)
                ins.then_inc(s_at, 1)

            def down(p, e):
                k = 0
                for m in range(HC):
                    for a, w in ((ah, 0), (al, 0), (ah, 1)):
                        ins = mm(bank[5][:, 0:D], a[:, p, P * m:P * (m + 1)], W2s[:, e, w, D * m:D * (m + 1)],
                                 start=k == 0, stop=k == 3 * HC - 1)
                        k += 1
                ins.then_inc(s_l2, 1)

            def expert(at):
                return bass.ds(pe.value_load(tab[0:1, at], min_val=0, max_val=NE - 1), 1)
            tile_transposes(0, 0, 16)
            tile_transposes(1, 1, 16)
            for t in range(2):
                pe.wait_ge(s_tc, t + 1)
                hidden(t, expert(slice(P + t, P + t + 1)))
            pe.wait_ge(s_a, 1)
            hidden_transposes(0)
            tile_transposes(2, 0, 16)
            with pe.Fori(0, STEPS // RING) as i:
                for u in range(RING):
                    e2 = expert(bass.ds(i * RING + (P + u + 2), 1))
                    pe.wait_ge(s_tc, i * RING + (u + 3))
                    pe.sem_inc(s_hold, 1)
                    pe.wait_ge(s_u, i * RING + (u + 1))
                    pe.sem_inc(s_hold, 1)
                    hidden(u % 2, e2)
                    pe.wait_ge(s_a, i * RING + (u + 2))
                    pe.sem_inc(s_hold, 1)
                    pe.wait_ge(s_alo, i * RING + (u + 1))
                    hidden_transposes((u + 1) % 2)
                    v = (u + 3) % RING
                    tile_transposes(v, (u + 1) % 2, i * 16 + (16 if u + 3 < RING else 32))
                    e0 = expert(bass.ds(i * RING + (P + u), 1))
                    pe.wait_ge(s_y, i * RING + (u + 1))
                    down(u % 2, e0)



def kernel(x, L0_tok_W0, L0_tok_b0, L0_tok_W1, L0_tok_b1, L0_tok_W2, L0_tok_b2, L0_tok_Wf, L0_tok_bf,
           L0_tok_idx0, L0_tok_idx1, L0_tok_idx2, L0_attn_W_qkv, L0_attn_W_out, L0_attn_b_out, L0_ffn_norm_scale,
           L0_ffn_gate_w, L0_ffn_gate_b, L0_ffn_mlp1_w, L0_ffn_mlp1_b, L0_ffn_mlp2_w, L0_ffn_mlp2_b):
    import numpy as _np
    import concourse.bacc as _bacc
    from concourse import mybir as _mybir
    from concourse.bass_utils import run_bass_kernel_spmd as _run
    f32 = _np.float32
    A = _np.asarray
    x = A(x)
    x0 = x.transpose(2, 3, 0, 1).reshape(4096, 24)
    x1 = x.reshape(8, 3, 32, 2, 32, 2).transpose(2, 4, 0, 3, 5, 1).reshape(1024, 96)
    x2 = x.reshape(8, 3, 16, 4, 16, 4).transpose(2, 4, 0, 3, 5, 1).reshape(256, 384)
    i0 = A(L0_tok_idx0).reshape(2, 128, 16).transpose(1, 0, 2).reshape(128, 32)
    i1 = A(L0_tok_idx1).reshape(64, 2, 8).transpose(1, 0, 2).reshape(128, 8)
    i2 = A(L0_tok_idx2).reshape(16, 8, 2).transpose(1, 0, 2).reshape(128, 2)
    idx = _np.concatenate([i0, i1, i2], axis=1)
    wft = _np.concatenate([A(L0_tok_Wf).T, A(L0_tok_bf)[None]], axis=0)
    b0, b1_, b2_ = A(L0_tok_b0), A(L0_tok_b1), A(L0_tok_b2)
    bcol = _np.stack([_np.concatenate([b0, b1_]), _np.concatenate([b2_, b2_])], axis=1)
    wqkv = A(L0_attn_W_qkv)
    wo = _np.concatenate([A(L0_attn_W_out), A(L0_attn_b_out)[None]], axis=0)
    gw = _np.concatenate([A(L0_ffn_gate_w).T, A(L0_ffn_gate_b)[None]], axis=0)
    m1 = A(L0_ffn_mlp1_w).reshape(NE, HID, 2, D).transpose(0, 3, 2, 1).reshape(NE, D, 2 * HID)
    b1 = A(L0_ffn_mlp1_b).reshape(NE, HID, 2).transpose(0, 2, 1).reshape(NE, 2 * HID)
    m2 = A(L0_ffn_mlp2_w).reshape(NE, D, HC, P).transpose(0, 3, 2, 1).reshape(NE, P, HC * D)
    ns = A(L0_ffn_norm_scale)
    one = _np.zeros((3, P), f32)
    one[0, D1:D1 + 3] = 1
    one[1, D1 + 1] = 1
    tail = ns[P:D]
    sraw = _np.stack([ns[0:P], _np.concatenate([tail, one[0, D1:]]),
                      _np.concatenate([tail, one[1, D1:]])], axis=1)
    r = _np.arange(P)
    c32 = _np.zeros((P, 275), f32)
    c32[:, 0:128] = _np.eye(P)
    c32[:, 128:256] = (r[:, None] // HD) == (r[None, :] // HD)
    c32[:, 256:272] = _np.arange(NE)
    c32[:, 272] = r
    c32[:, 273] = ROWS + 1 + r
    c16 = _np.zeros((P, 640), _np.float16)
    c16[:, 0:128] = _np.eye(P)
    c16[:, 128:256] = r[:, None] < r[None, :]
    c16[:, 256:384] = 1
    c16[:, 384:640] = _np.arange(256)
    pat = _np.zeros((NE, 1, 2 * HID), f32)
    pat[:, 0, HID:] = 1
    m1c = _np.concatenate([m1[:, P:D], b1[:, None], b1[:, None], pat], axis=1)

    def interpolation(n):
        pos = _np.clip((_np.arange(NTOK, dtype=f32) + f32(0.5)) * f32(n / NTOK) - f32(0.5), 0, n - 1)
        lo = _np.floor(pos).astype(_np.int32)
        hi = _np.minimum(lo + 1, n - 1)
        w = (pos - lo).astype(f32)
        m = _np.zeros((n, NTOK), f32)
        _np.add.at(m, (lo, _np.arange(NTOK)), 1 - w)
        _np.add.at(m, (hi, _np.arange(NTOK)), w)
        return m
    p1 = _np.tile(interpolation(64), (2, 1))
    m16 = interpolation(16)
    p2 = _np.zeros((P, 512), f32)
    for q in range(8):
        p2[16 * q:16 * q + 16, 256 * (q % 2):256 * (q % 2) + 256] = m16
    arrays = {"x0": x0, "x1": x1, "x2": x2, "idx": idx, "w0t": A(L0_tok_W0).T, "w1t": A(L0_tok_W1).T,
              "w2t": A(L0_tok_W2).T, "wft": wft, "bcol": bcol, "wq": wqkv[:, 0:D], "wk": wqkv[:, D:], "wo": wo,
              "gw": gw, "m1a": m1[:, 0:P], "m1c": m1c, "m2": m2, "b2": A(L0_ffn_mlp2_b),
              "sraw": sraw, "c32": c32, "c16": c16, "p1": p1, "p2": p2}
    arrays = {k: _np.ascontiguousarray(v) for k, v in arrays.items()}
    nc = _bacc.Bacc("TRN2", target_bir_lowering=False, num_devices=1)
    aps = {k: nc.dram_tensor(f"in_{k}", v.shape, _mybir.dt.from_np(v.dtype), kind="ExternalInput").ap()
           for k, v in arrays.items()}
    out = nc.dram_tensor("out", (ROWS + P, D), F32, kind="ExternalOutput").ap()
    build(nc, out=out, **aps)
    got = _run(nc, [{f"in_{k}": v for k, v in arrays.items()}], core_ids=[0])
    return got.results[0]["out"][0:ROWS].reshape(NB, NTOK, D)
```

```python
import numpy as np
import concourse.bass as bass
from concourse import mybir
from contextlib import ExitStack

F32 = mybir.dt.float32
F16 = mybir.dt.float16
I32 = mybir.dt.int32
U32 = mybir.dt.uint32
ALU = mybir.AluOpType
ACT = mybir.ActivationFunctionType
AX = mybir.AxisListType

P = 128
NB, NTOK, D = 8, 256, 192
NT = NB * NTOK // P
ROWS = NB * NTOK
D1 = D - P
EMB, GP, CH = 64, 16, 3
HD = 16
NH, NH0 = D // HD, P // HD
NDW = D + NH
NE, TOPK, HID = 16, 4, 384
QT = ROWS // P
TILES = ROWS * TOPK // P + NE - 1
STEPS = 80
RING = 8
AHEAD = 6
TAB = STEPS + RING
HC = HID // P
ROWT = D + D + 2 * NE
STAGES = 3
S1 = 2.0 ** 9
S2 = 2.0 ** 9
SA = 2.0 ** 9
LN_EPS, RMS_EPS, ATT_EPS = 1e-5, 1e-5, 1e-6
LIMIT, ALPHA = 7.0, 1.702
SIGMAX = float(1.0 / (1.0 + np.exp(-np.float64(LIMIT * ALPHA))))
MAGIC = 1597463007.0


def build(nc, x0, x1, x2, idx, w0t, w1t, w2t, wft, bcol, wq, wk, wo, gw, m1a, m1c, m2, b2, sraw,
          c32, c16, p1, p2, out):
    with ExitStack() as ctx:
        def sb(name, shape, dt=F32):
            return ctx.enter_context(nc.sbuf_tensor(name, shape, dt))

        def sem(name):
            return ctx.enter_context(nc.semaphore(name))

        t_dram = nc.dram_tensor("t_dram", [ROWS + P, ROWT // 2], F32, kind="Internal").ap()
        acc_odd = nc.dram_tensor("acc_odd", [ROWS + P, D], F32, kind="Internal").ap()

        W1s = sb("W1s", [P, NE, 4, 2 * HID], F16)
        W2s = sb("W2s", [P, NE, 2, HC * D], F16)
        C32 = sb("C32", [P, 128 + 128 + 16 + 2 + NT])
        C16 = sb("C16", [P, 128 * 3 + 256], F16)
        srow_raw = sb("srow_raw", [P, 3])
        srow = sb("srow", [P, 3])
        ident, bmask = C32[:, 0:128], C32[:, 128:256]
        iota16, pcol, pcol_pad, idv = C32[:, 256:272], C32[:, 272:273], C32[:, 273:274], C32[:, 274:274 + NT]
        ident16, ustrict, ones16, iota256 = C16[:, 0:128], C16[:, 128:256], C16[:, 256:384], C16[:, 384:640]
        idx_sb = sb("idx_sb", [P, 42], I32)
        WF0 = sb("WF0", [P, D])
        WF1 = sb("WF1", [D1 + 1, D])
        BC = sb("BC", [P, 2])
        WA = sb("WA", [P, 8 * D])
        WQ = WA[:, 0:2 * D].rearrange("p (k n) -> p k n", k=2)
        WK = WA[:, 2 * D:6 * D].rearrange("p (k n) -> p k n", k=2)
        WO = WA[:, 6 * D:8 * D].rearrange("p (k n) -> p k n", k=2)
        GW = sb("GW", [P, 2, NE])
        GS = sb("GS", [P, 2, NE])
        B2 = sb("B2", [NE, D])
        lz = sb("lz", [P, 208])
        h_all = sb("h_all", [P, NT, D])

        RW = 12736
        R = sb("R", [P, RW])
        mark = [0]

        def carve(shape, dt=F32, parts=P):
            n = 1
            for k in shape:
                n *= k
            words = n if dt != F16 else n // 2
            a = mark[0]
            mark[0] += words
            assert mark[0] <= RW, mark[0]
            v = R[0:parts, a:a + words]
            if dt != F32:
                v = v.bitcast(dt)
            if len(shape) == 1:
                return v
            names = "abcde"[:len(shape)]
            return v.rearrange("p (" + " ".join(names) + ") -> p " + " ".join(names),
                               **{names[k]: shape[k] for k in range(len(shape))})

        hw = h_all[:, :, :].rearrange("p t n -> p (t n)")
        G = 2 * HID
        stA = [hw[:, 0:G], hw[:, G:2 * G], WA[:, 0:G]]
        stC = [hw[0:67, 2 * G:3 * G], hw[0:67, 3 * G:4 * G], WA[0:67, G:2 * G]]
        stD = [carve([HC * D]) for _ in range(STAGES)]
        G0w, G1w, G2w = carve([32 * 24]), carve([8 * 96]), carve([2 * 384])
        G0 = G0w.rearrange("p (k j b c) -> p k j b c", k=2, j=16, b=8)
        G1 = G1w.rearrange("p (j b f) -> p j b f", j=8, b=8)
        G2 = G2w.rearrange("p (j b f) -> p j b f", j=2, b=8)
        XT1 = carve([2, 8, 64], parts=96)
        x2w = mark[0]
        XT2 = carve([8, 8, 16], parts=96)
        X0T = R[0:48, x2w:x2w + 1024].rearrange("p (q n) -> p q n", q=2)
        o1 = carve([4, 64])
        o2 = carve([64])
        W0T = carve([64], parts=48)
        W1T = carve([2, 64], parts=96)
        W2T = carve([8, 64], parts=96)
        P1 = carve([256])
        P2 = carve([512])
        CT0 = carve([ROWS])
        CT1 = carve([ROWS], parts=D1 + 1)

        B2r = CT0[:, 0:768].rearrange("p (b n) -> p b n", b=8)
        B1r = CT0[:, 768:1536].rearrange("p (b n) -> p b n", b=8)
        B0r = G2w.rearrange("p (k b n) -> p k b n", k=2, b=8)

        mark[0] = 0
        rows = carve([2, 2, 2 * D], F16)
        rows32 = R[:, 0:4 * D].rearrange("p (s t n) -> p s t n", s=2, t=2)
        bst, mv, mv2 = carve([NT, 6]), carve([NT, 2]), carve([NT, 2])
        rs1, ve1 = carve([NT]), carve([NT])
        nw = carve([3, NT])
        vv, rr = carve([2, 2, 2]), carve([2, 2, 2])
        nw2 = carve([2, 3, 4])
        hn, hnT = carve([2, 2, D]), carve([2, 2, 256])
        ek, rk, phk = carve([2, D]), carve([2, D]), carve([2, 2, D])
        vx = carve([2, 2, 129 + 65])
        eq, rq, phq = carve([2, 256]), carve([2, 256]), carve([2, 2, 256])
        kvm = carve([2, 2, P + NH0])
        att, zz = carve([2, 2, D]), carve([2, NH])
        attT = carve([2, 2, 256])
        tp, tpT = carve([2, 2, D]), carve([2, 2, 256])
        g_all = carve([NT, NE])

        mark[0] = 4 * D
        comb, combs = carve([NT, NE]), carve([NT, NE])
        oh, ohw = carve([NT, TOPK, NE]), carve([NT, TOPK, NE])
        rank = carve([NT, NE])
        mx8 = carve([NT, 8])
        ix8 = carve([NT, 8], U32)
        ixf, ew, es = carve([NT, TOPK]), carve([NT, TOPK]), carve([NT])
        Mx = carve([NT, NE], F16)
        rkk, rkr, rkq = carve([NT, TOPK]), carve([NT, TOPK]), carve([NT, TOPK])
        rki = carve([2, NT, TOPK], I32)
        Aoh, Boh = carve([8, 256], F16), carve([8, 128], F16)
        lpad = carve([256])
        cnt_i, cnt, tt_e = carve([NE], I32), carve([4, NE]), carve([4])
        cT = carve([4, 512], parts=NE)
        mark[0] = 2 * NT * NE + 4 * D
        Ct, Cb = carve([2, 3, P], F16), carve([2, P], F16, parts=67)
        sg, lin, uu, av = (carve([2, HID]) for _ in range(4))
        ah, al = carve([2, HID], F16), carve([2, HID], F16)
        yv = carve([4, D])
        Li = sb("Li", [P, 257], I32)
        tab = sb("tab", [1, 2 * P], I32)
        ixr = sb("ixr", [P, RING], I32)
        Grw = carve([RING * ROWT // 2])
        Gr = Grw.bitcast(F16).rearrange("p (s n) -> p s n", s=RING)
        Gr32 = Grw.rearrange("p (s n) -> p s n", s=RING)

        bank = [ctx.enter_context(nc.psum_tensor(f"bank{k}", [P, 512], F32)) for k in range(8)]

        l1bank = [(bank[5], bank[6]), (bank[7], bank[4])]
        trs = [bank[0][:, 0:256].bitcast(F16), bank[7][:, 0:256].bitcast(F16)]

        s_c = sem("s_consts_loaded"); s_idx = sem("s_idx_loaded"); s_lw = sem("s_level_weights_loaded")
        s_aw = sem("s_attention_weights_loaded")
        s_st = [sem(f"s_stage_loaded{k}") for k in range(STAGES)]
        s_dup = sem("s_high_tails_doubled")
        s_sr = sem("s_scales_ready"); s_hi = sem("s_high_parts"); s_lo = sem("s_low_parts"); s_ah0 = sem("s_act_hold")
        s_g2 = sem("s_level2_gathered"); s_g1 = sem("s_level1_gathered"); s_g0 = [sem(f"s_level0_gathered{k}") for k in range(2)]
        s_by = sem("s_by_batch"); s_x = sem("s_level_matmul"); s_xe = sem("s_level_copied")
        s_ms = sem("s_constants_set")
        s_h = sem("s_h_matmul"); s_he = sem("s_h_copied")
        s_dv = sem("s_vector_chain")
        s_hn = sem("s_hn"); s_hnt = sem("s_hn_transposed"); s_hnte = sem("s_hnT_copied")
        s_kv = sem("s_kv"); s_q = sem("s_q"); s_ke = sem("s_k_parts"); s_qe = sem("s_q_parts")
        s_phk = sem("s_phi_k"); s_phq = sem("s_phi_q")
        s_stt = sem("s_state"); s_kvm = sem("s_state_masked"); s_nd = sem("s_num_den"); s_atr = sem("s_att_rows"); s_att_t = sem("s_att_transposed")
        s_att = sem("s_attT_copied"); s_o = sem("s_attention_out"); s_h2 = sem("s_h2")
        s_tp = sem("s_tp"); s_th = sem("s_high_rows"); s_tpt = sem("s_tp_transposed"); s_tpte = sem("s_tpT_copied")
        s_ga = sem("s_gate"); s_row = sem("s_rows_ready"); s_rowd = [sem(f"s_rows_stored{k}") for k in range(2)]
        s_z = sem("s_zero_rows"); s_zd = sem("s_zeros_stored")
        s_mv = sem("s_second_statistics"); s_rr = sem("s_second_roots"); s_po = sem("s_gpsimd_chain")
        s_gs = sem("s_gate_weights_scaled")
        s_nx = sem("s_top_negated"); s_ex = sem("s_top_exp"); s_cb = sem("s_comb_ready"); s_cbd = sem("s_comb_stored")
        s_mr = sem("s_members"); s_rp = sem("s_rank"); s_oha = sem("s_onehot"); s_ohu = sem("s_onehot_used")
        s_ct = sem("s_comb_transposed"); s_cte = sem("s_combT_copied"); s_b2 = sem("s_bias2")
        s_base = sem("s_base"); s_based = sem("s_base_stored")
        s_tabt = sem("s_table_columns"); s_tabp = sem("s_table_row"); s_tab = sem("s_table_ready")
        s_ixc = sem("s_index_copied")
        s_gr = [sem(f"s_tile_gathered{k}") for k in range(RING)]
        s_tr = sem("s_tile_transposed"); s_tc = sem("s_tile_copied"); s_l1 = sem("s_hidden"); s_sg = sem("s_sigmoid")
        s_lin = sem("s_linear_clipped"); s_u = sem("s_gated"); s_a = sem("s_a"); s_at = sem("s_a_transposed"); s_ahi = sem("s_a_high"); s_alo = sem("s_a_low")
        s_l2 = sem("s_y"); s_y = sem("s_y_weighted"); s_sc = [sem(f"s_scattered{k}") for k in range(2)]
        s_hold = sem("s_hold"); s_clear = sem("s_accumulator_free"); s_fin = sem("s_final")

        block = ctx.enter_context(nc.Block())

        def wait(eng, s, v):
            if v > 0:
                eng.wait_ge(s, v)

        NCONST = 3 * 16

        @block.sync
        def _(sp):
            sp.dma_start(idx_sb[:, :], idx).then_inc(s_idx, 16)
            sp.dma_start(C32[:, :], c32).then_inc(s_c, 16)
            sp.dma_start(C16[:, :], c16).then_inc(s_c, 16)
            sp.dma_start(srow_raw[:, :], sraw).then_inc(s_c, 16)
            def load_expert(e, k):
                sp.dma_start(stA[k], m1a[e, :, :].rearrange("e p n -> (e p) n")).then_inc(s_st[k], 16)
                sp.dma_start(stC[k], m1c[e, :, :].rearrange("e p n -> (e p) n")).then_inc(s_st[k], 16)
                sp.dma_start(stD[k], m2[e, :, :].rearrange("e p n -> (e p) n")).then_inc(s_st[k], 16)
            for k in range(STAGES):
                load_expert(slice(k, k + 1), k)
            with sp.Fori(0, NE // STAGES - 1) as i:
                for k in range(STAGES):
                    sp.wait_ge(s_hi, i * STAGES + (k + 1))
                    sp.wait_ge(s_lo, i * STAGES + (k + 1))
                    load_expert(bass.ds(i * STAGES + (k + STAGES), 1), k)
            for e in range(NE // STAGES * STAGES, NE):
                sp.wait_ge(s_hi, e - STAGES + 1)
                sp.wait_ge(s_lo, e - STAGES + 1)
                load_expert(slice(e, e + 1), e % STAGES)
            sp.wait_ge(s_hi, NE)
            sp.wait_ge(s_lo, NE)
            for dst, src in ((WQ, wq), (WK, wk), (WO, wo), (GW, gw)):
                sp.dma_start(dst[:, 0, :], src[0:P, :]).then_inc(s_aw, 16)
                n = src.shape[0] - P
                sp.dma_start(dst[0:n, 1, :], src[P:P + n, :]).then_inc(s_aw, 16)
            sp.dma_start(B2[:, :], b2).then_inc(s_aw, 16)
            sp.dma_start(W1s[D1:P, :, 2, :], W1s[0:D1, :, 2, :]).then_inc(s_dup, 16)
            sp.wait_ge(s_z, 1)
            for t in range(NT + 1):
                sp.dma_start(acc_odd[t * P:(t + 1) * P, :], lz[:, 0:D]).then_inc(s_zd, 16)
            sp.dma_start(out[ROWS:ROWS + P, :], lz[:, 0:D]).then_inc(s_zd, 16)
            sp.dma_start(t_dram[ROWS:ROWS + P, :], lz[:, 0:ROWT // 2]).then_inc(s_zd, 16)
            tv = t_dram[0:ROWS, :].rearrange("(t p) n -> p t n", p=P)
            for b in range(NB):
                sp.wait_ge(s_row, b + 1)
                sp.dma_start(tv[:, 2 * b:2 * b + 2, 0:D], rows32[:, b % 2, :, :]).then_inc(s_rowd[b % 2], 16)
            sp.wait_ge(s_cb, 2)
            sp.dma_start(tv[:, :, D:D + NE], combs).then_inc(s_cbd, 16)
            ov = out[0:ROWS, :].rearrange("(t p) n -> p t n", p=P)
            for b in range(NB):
                sp.wait_ge(s_base, b + 1)
                sp.dma_start(ov[:, 2 * b:2 * b + 2, :], h_all[:, 2 * b:2 * b + 2, :]).then_inc(s_based, 16)

        @block.gpsimd
        def _(po):
            po.memset(lz[:, :], 0.0).then_inc(s_z, 1)
            po.wait_ge(s_z, 1)
            po.memset(CT1[D1:D1 + 1, :], 1.0).then_inc(s_ms, 1)
            po.wait_ge(s_ms, 1)
            po.wait_ge(s_idx, 16)

            def take(dst, src, col, s):
                po.indirect_dma_start(out=dst, out_offset=None, in_=src,
                                      in_offset=bass.IndirectOffsetOnAxis(ap=idx_sb[:, col:col + 1], axis=0)).then_inc(s, 16)
            for j in range(2):
                take(G2w[:, 384 * j:384 * (j + 1)], x2, 40 + j, s_g2)
            for j in range(8):
                take(G1w[:, 96 * j:96 * (j + 1)], x1, 32 + j, s_g1)
            for k in range(2):
                for j in range(16):
                    q = 16 * k + j
                    take(G0w[:, 24 * q:24 * (q + 1)], x0, q, s_g0[k])

            po.wait_ge(s_he, NB)
            po.memset(vx[:, :, :, :], 1.0).then_inc(s_ms, 1)
            po.wait_ge(s_ms, 2)
            po.memset(tpT[D1:D1 + 1, :, 1, :], 1.0).then_inc(s_ms, 1)
            po.wait_ge(s_ms, 3)
            po.memset(attT[D1:D1 + 1, :, 1, :], 1.0).then_inc(s_ms, 1)
            links = 0
            for b in range(NB):
                p = b % 2
                po.wait_ge(s_mv, b + 1)
                wait(po, s_row, b - 1)
                var, mean = mv2[:, 2 * b:2 * b + 2, 1], mv2[:, 2 * b:2 * b + 2, 0]
                f = "p a t -> p (a t)"
                y, v = rr[:, p, :, :].rearrange(f), vv[:, p, :, :].rearrange(f)
                s0, s1, s2 = nw2[:, p, 0, :], nw2[:, p, 1, :], nw2[:, p, 2, :]

                def then(ins):
                    nonlocal links
                    links += 1
                    ins.then_inc(s_po, 1)
                    po.wait_ge(s_po, links)
                then(po.tensor_scalar(vv[:, p, 0, :], var, LN_EPS, None, ALU.add))
                then(po.tensor_scalar(s0[:, 0:2], vv[:, p, 0, :], RMS_EPS, None, ALU.mult))
                then(po.tensor_tensor(vv[:, p, 1, :], s0[:, 0:2], var, ALU.add))
                then(po.tensor_scalar(y.bitcast(I32), v.bitcast(I32), -0.5, MAGIC, ALU.mult, ALU.add))
                for _ in range(3):
                    then(po.tensor_tensor(s0, y, y, ALU.mult))
                    then(po.tensor_tensor(s1, s0, v, ALU.mult))
                    then(po.tensor_scalar(s2, s1, -0.5, 1.5, ALU.mult, ALU.add))
                    then(po.tensor_tensor(y, y, s2, ALU.mult))
                then(po.tensor_tensor(s0[:, 0:2], mean, rr[:, p, 0, :], ALU.mult))
                po.tensor_scalar(s1[:, 0:2], s0[:, 0:2], -1.0, None, ALU.mult)
                po.tensor_scalar(s2[:, 0:2], rr[:, p, 0, :], 1.0, None, ALU.add).then_inc(s_rr, 1)

            po.wait_ge(s_tab, 1)
            po.wait_ge(s_base, NB)
            po.memset(Cb[D1:67, :, :], 1.0).then_inc(s_ms, 1)
            po.wait_ge(s_ms, 5)

            po.wait_ge(s_rowd[0], 16 * NB // 2)
            po.wait_ge(s_rowd[1], 16 * NB // 2)
            po.wait_ge(s_cbd, 16)
            po.wait_ge(s_zd, 16 * (NT + 3))

            def index(tile, slot, done):
                c = po.value_load(tab[0:1, tile], min_val=0, max_val=NE * QT)
                po.tensor_copy(ixr[:, slot:slot + 1], Li[:, bass.ds(c, 1)]).then_inc(s_ixc, 1)
                po.wait_ge(s_ixc, done)

            def gather(slot):
                po.indirect_dma_start(out=Gr32[:, slot, :], out_offset=None, in_=t_dram,
                                      in_offset=bass.IndirectOffsetOnAxis(ap=ixr[:, slot:slot + 1], axis=0)).then_inc(s_gr[slot], 16)
            for t in range(AHEAD):
                index(slice(t, t + 1), t, t + 1)
                gather(t)
            po.wait_ge(s_based, 16 * NB)
            with po.Fori(0, STEPS // RING) as i:
                for u in range(RING):
                    po.wait_ge(s_y, i * RING + (u + 2))
                    po.sem_inc(s_hold, 1)
                    if u >= 2:
                        po.wait_ge(s_sc[u % 2], i * (RING // 2 * 16) + 16 * (u // 2))
                    po.sem_inc(s_clear, 1)
                    po.indirect_dma_start(out=(out, acc_odd)[u % 2],
                                          out_offset=bass.IndirectOffsetOnAxis(ap=ixr[:, u:u + 1], axis=0),
                                          in_=yv[:, u % 4, :], in_offset=None, compute_op=ALU.add).then_inc(s_sc[u % 2], 16)
                    v = (u + AHEAD) % RING
                    c = po.value_load(tab[0:1, bass.ds(i * RING + (u + AHEAD), 1)], min_val=0, max_val=NE * QT)
                    po.tensor_copy(ixr[:, v:v + 1], Li[:, bass.ds(c, 1)]).then_inc(s_ixc, 1)
                    po.wait_ge(s_ixc, i * RING + (u + 1 + AHEAD))
                    po.sem_inc(s_hold, 1)
                    gather(v)
                for k in range(2):
                    po.wait_ge(s_sc[k], i * (RING // 2 * 16) + RING // 2 * 16)
                    po.sem_inc(s_hold, 1)
            for k in range(RING):
                po.wait_ge(s_gr[k], 16 * (STEPS // RING + (1 if k < AHEAD else 0)))
            po.dma_start(out[0:ROWS, :], acc_odd[0:ROWS, :], accum_op=ALU.add, max_dma_last_dim=4096).then_inc(s_fin, 16)
            po.wait_ge(s_fin, 16)

        chain = {}

        def link(eng, ins):
            chain["n"] = chain.get("n", 0) + 1
            ins.then_inc(s_dv, 1)
            eng.wait_ge(s_dv, chain["n"])

        @block.vector
        def _(ve):
            ve.wait_ge(s_c, NCONST)
            ve.tensor_scalar(srow[:, :], srow_raw[:, :], S1, None, ALU.mult).then_inc(s_sr, 1)
            ve.wait_ge(s_sr, 1)

            def low_parts(e, k, n):
                ve.wait_ge(s_hi, n)
                ve.scalar_tensor_tensor(out=W1s[:, e, 1, :], in0=stA[k], scalar=srow[:, 0:1],
                                        in1=W1s[:, e, 0, :], op0=ALU.mult, op1=ALU.subtract)
                ve.scalar_tensor_tensor(out=W1s[0:67, e, 3, :], in0=stC[k], scalar=srow[0:67, 1:2],
                                        in1=W1s[0:67, e, 2, :], op0=ALU.mult, op1=ALU.subtract)
                ve.scalar_tensor_tensor(out=W2s[:, e, 1, :], in0=stD[k], scalar=S2,
                                        in1=W2s[:, e, 0, :], op0=ALU.mult, op1=ALU.subtract).then_inc(s_lo, 1)

            def low(e):
                low_parts(slice(e, e + 1), e % STAGES, e + 1)
            with ve.Fori(0, 2) as i:
                for k in range(STAGES):
                    low_parts(bass.ds(i * STAGES + k, 1), k, i * STAGES + (k + 1))
            ve.wait_ge(s_g2, 32)
            ve.tensor_copy(B2r.rearrange("p b (j f) -> p j b f", j=2), G2).then_inc(s_by, 1)
            ve.wait_ge(s_g1, 16 * 8)
            ve.tensor_copy(B1r.rearrange("p b (j f) -> p j b f", j=8), G1).then_inc(s_by, 1)
            low(6)
            for k in range(2):
                ve.wait_ge(s_x, 1 + k)
                ve.tensor_copy(XT2[:, :, 4 * k:4 * k + 4, :],
                               bank[k][0:96, :].rearrange("p (b h g) -> p h b g", b=4, h=8)).then_inc(s_xe, 1)
            low(7)
            ve.wait_ge(s_x, 3)
            ve.tensor_copy(o2, bank[2][:, 0:64]).then_inc(s_xe, 1)
            for k in range(2):
                ve.wait_ge(s_x, 4 + k)
                ve.tensor_copy(XT1[:, :, 4 * k:4 * k + 4, :],
                               bank[k][0:96, :].rearrange("p (b h g) -> p h b g", b=4, h=2)).then_inc(s_xe, 1)
            low(8)
            ve.wait_ge(s_x, 6)
            ve.tensor_copy(o1, bank[2][:, 0:256].rearrange("p (b e) -> p b e", b=4)).then_inc(s_xe, 1)
            low(9)
            for k in range(4):
                ve.wait_ge(s_x, 7 + k)
                ve.tensor_scalar(CT1[0:EMB, 512 * k:512 * k + 512], bank[3 + k % 2][0:EMB, :], BC[0:EMB, 1:2], None,
                                 ALU.add).then_inc(s_xe, 1)
            low(10)
            for k in range(4):
                ve.wait_ge(s_x, 11 + k)
                for j in range(2):
                    ins = ve.tensor_scalar(CT0[EMB:P, 512 * k + 256 * j:512 * k + 256 * (j + 1)],
                                           l1bank[k % 2][j][EMB:P, 0:256], BC[EMB:P, 0:1], None, ALU.add)
                ins.then_inc(s_xe, 1)
            CT0v = CT0.rearrange("p (b k t) -> p b k t", b=8, k=2)
            n = 14
            for k in range(2):
                ve.wait_ge(s_by, 1)
                ve.wait_ge(s_g0[k], 16 * 16)
                ve.tensor_copy(B0r[:, k].rearrange("p b (j c) -> p j b c", j=16), G0[:, k]).then_inc(s_by, 1)
                for q in range(2):
                    if k == 0 or q == 0:
                        low(11 + 2 * k + q)
                    ve.wait_ge(s_x, n + 1)
                    ve.tensor_copy(X0T[:, q, :], bank[q][0:48, :]).then_inc(s_xe, 1)
                    if k == 1:
                        low(14 + q)
                    ve.wait_ge(s_x, n + 2)
                    ve.tensor_scalar(CT0v[0:EMB, 4 * q:4 * q + 4, k, :],
                                     bank[2 + q][0:EMB, :].rearrange("p (b t) -> p b t", b=4), BC[0:EMB, 0:1], None,
                                     ALU.add).then_inc(s_xe, 1)
                    n += 2
            ve.wait_ge(s_aw, 16 * 9)
            ve.tensor_scalar(GS[:, 0, :], GW[:, 0, :], srow_raw[:, 0:1], None, ALU.mult)
            ve.tensor_scalar(GS[0:D1 + 1, 1, :], GW[0:D1 + 1, 1, :], srow_raw[0:D1 + 1, 1:2], None, ALU.mult).then_inc(s_gs, 1)

            def rsqrt(y, v, s0, s1, s2):
                link(ve, ve.tensor_scalar(y.bitcast(I32), v.bitcast(I32), -0.5, MAGIC, ALU.mult, ALU.add))
                for _ in range(3):
                    link(ve, ve.tensor_tensor(s0, y, y, ALU.mult))
                    link(ve, ve.tensor_tensor(s1, s0, v, ALU.mult))
                    link(ve, ve.tensor_scalar(s2, s1, -0.5, 1.5, ALU.mult, ALU.add))
                    link(ve, ve.tensor_tensor(y, y, s2, ALU.mult))

            for t in range(NT):
                ve.wait_ge(s_he, t // 2 + 1)
                ins = ve.bn_stats(bst[:, t, :], h_all[:, t, :])
            link(ve, ins)
            for t in range(NT):
                ins = ve.bn_aggr(mv[:, t, :], bst[:, t, :])
            link(ve, ins)
            link(ve, ve.tensor_scalar(ve1, mv[:, :, 1], LN_EPS, None, ALU.add))
            rsqrt(rs1, ve1, nw[:, 0, :], nw[:, 1, :], nw[:, 2, :])

            def normalise(b):
                p = b % 2
                wait(ve, s_hnt, b - 1)
                for j in range(2):
                    t = 2 * b + j
                    ins = ve.tensor_scalar(hn[:, p, j, :], h_all[:, t, :], mv[:, t, 0:1], rs1[:, t:t + 1],
                                           ALU.subtract, ALU.mult)
                ins.then_inc(s_hn, 1)

            def phi_k(b):
                p = b % 2
                ve.wait_ge(s_ke, b + 1)
                wait(ve, s_stt, b - 1)
                ve.scalar_tensor_tensor(out=phk[:, p, :, :], in0=ek, scalar=1.0, in1=rk,
                                        op0=ALU.min, op1=ALU.add).then_inc(s_phk, 1)

            def phi_q(b):
                p = b % 2
                ve.wait_ge(s_qe, b + 1)
                wait(ve, s_nd, b - 1)
                ve.scalar_tensor_tensor(out=phq[:, p, 0, :], in0=eq[:, 0, :], scalar=1.0, in1=rq[:, 0, :],
                                        op0=ALU.min, op1=ALU.add)
                ve.scalar_tensor_tensor(out=phq[0:D1, p, 1, :], in0=eq[0:D1, 1, :], scalar=1.0,
                                        in1=rq[0:D1, 1, :], op0=ALU.min, op1=ALU.add).then_inc(s_phq, 1)

            def mask_state(b):
                p = b % 2
                head = bmask.rearrange("p (h d) -> p h d", d=HD)[:, :, 0]
                n1 = NH - NH0
                ve.wait_ge(s_stt, b + 1)
                wait(ve, s_nd, b - 1)
                ve.tensor_tensor(kvm[:, p, 0, 0:P], bank[4][:, 0:P], bmask, ALU.mult)
                ve.scalar_tensor_tensor(out=kvm[:, p, 0, P:P + NH0], in0=head, scalar=bank[4][:, P:P + 1], in1=head,
                                        op0=ALU.mult, op1=ALU.add)
                ve.tensor_tensor(kvm[0:D1, p, 1, n1:n1 + D1], bank[4][0:D1, 256:256 + D1], bmask[0:D1, 0:D1], ALU.mult)
                ve.scalar_tensor_tensor(out=kvm[0:D1, p, 1, 0:n1], in0=head[0:D1, 0:n1],
                                        scalar=bank[4][0:D1, 256 + D1:257 + D1], in1=head[0:D1, 0:n1],
                                        op0=ALU.mult, op1=ALU.add).then_inc(s_kvm, 1)

            def divide(b):
                p = b % 2
                nd = bank[5][:, 0:2 * NDW].rearrange("p (t n) -> p t n", t=2)
                ve.wait_ge(s_nd, b + 1)
                link(ve, ve.tensor_scalar(zz, nd[:, :, P:P + NH], ATT_EPS, None, ALU.add))
                link(ve, ve.reciprocal(zz, zz))
                wait(ve, s_att_t, b - 1)
                for d, c, h, m in ((0, 0, 0, NH0), (P, P + NH, NH0, NH - NH0)):
                    for j in range(2):
                        ins = ve.tensor_tensor(att[:, p, j, d:d + HD * m].rearrange("p (h d) -> p h d", d=HD),
                                               nd[:, j, c:c + HD * m].rearrange("p (h d) -> p h d", d=HD),
                                               zz[:, j, h:h + m].rearrange("p (h d) -> p h d", d=1)
                                               .broadcast_to([P, m, HD]), ALU.mult)
                ins.then_inc(s_atr, 1)

            def second_statistics(b):
                h2 = h_all[:, 2 * b:2 * b + 2, :]
                ve.wait_ge(s_o, b + 1)
                link(ve, ve.tensor_tensor(h2, h2, bank[4][:, 0:2 * D].rearrange("p (t n) -> p t n", t=2), ALU.add))
                for j in range(2):
                    ins = ve.bn_stats(bst[:, 2 * b + j, :], h_all[:, 2 * b + j, :])
                ins.then_inc(s_h2, 1)
                ve.wait_ge(s_h2, b + 1)
                for j in range(2):
                    ins = ve.bn_aggr(mv2[:, 2 * b + j, :], bst[:, 2 * b + j, :])
                ins.then_inc(s_mv, 1)

            def second_norm(b):
                p = b % 2
                ve.wait_ge(s_rr, b + 1)
                wait(ve, s_tpt, b - 1)
                wait(ve, s_th, b - 1)
                for j in range(2):
                    ins = ve.tensor_scalar(tp[:, p, j, :], h_all[:, 2 * b + j, :], mv2[:, 2 * b + j, 0:1],
                                           rr[:, p, 1, j:j + 1], ALU.subtract, ALU.mult)
                ins.then_inc(s_tp, 1)
                for j in range(2):
                    t = 2 * b + j
                    ve.tensor_scalar(h_all[:, t, :], h_all[:, t, :], nw2[:, p, 2, j:j + 1], nw2[:, p, 1, j:j + 1],
                                     ALU.mult, ALU.add)
                ve.wait_ge(s_th, b + 1)
                tt2 = tp[:, p, :, :]
                r2 = rows[:, p, :, :]
                ve.tensor_tensor(r2[:, :, D:D + D1], tt2[:, :, P:D], r2[:, :, P:D], ALU.subtract)
                ve.tensor_tensor(r2[:, :, D + D1:2 * D], tt2[:, :, 0:P], r2[:, :, 0:P], ALU.subtract).then_inc(s_row, 1)

            def gates(b):
                ve.wait_ge(s_ga, b + 1)
                ve.tensor_copy(g_all[:, 2 * b:2 * b + 2, :], bank[7][:, 0:32].rearrange("p (t e) -> p t e", t=2))\
                  .then_inc(s_gs, 1)

            normalise(0)
            normalise(1)
            phi_k(0)
            for s in range(NB + 3):
                if 0 <= s - 1 < NB:
                    mask_state(s - 1)
                if s < NB:
                    phi_q(s)
                if 0 <= s - 1 < NB:
                    divide(s - 1)
                if 0 <= s - 2 < NB:
                    second_norm(s - 2)
                if 0 <= s - 3 < NB:
                    gates(s - 3)
                if 0 <= s - 1 < NB:
                    second_statistics(s - 1)
                if s + 1 < NB:
                    phi_k(s + 1)
                if s + 2 < NB:
                    normalise(s + 2)

            ve.wait_ge(s_gs, NB + 1)
            for t in range(NT):
                ins = ve.max(mx8[:, t, :], g_all[:, t, :])
            link(ve, ins)
            for t in range(NT):
                ins = ve.max_index(ix8[:, t, :], mx8[:, t, :], g_all[:, t, :])
            top = mx8[:, :, 0:TOPK]
            ve.tensor_tensor(ew[:, :, :], top, mx8[:, :, 0:1].broadcast_to([P, NT, TOPK]), ALU.subtract).then_inc(s_nx, 1)
            link(ve, ins)
            link(ve, ve.tensor_copy(ixf[:, :, :], ix8[:, :, 0:TOPK]))
            full = [P, NT, TOPK, NE]
            link(ve, ve.tensor_tensor(oh, iota16.rearrange("p (a k e) -> p a k e", a=1, k=1).broadcast_to(full),
                                      ixf[:, :, :].rearrange("p t (k e) -> p t k e", e=1).broadcast_to(full), ALU.is_equal))
            with nc.allow_low_precision(reason="sums of zeros and one one are exact"):
                ve.tensor_reduce(Mx, oh.rearrange("p t k e -> p t e k"), AX.X, ALU.add).then_inc(s_mr, 1)
            ve.wait_ge(s_ex, 1)
            link(ve, ve.tensor_reduce(es, ew[:, :, :], AX.X, ALU.add))
            link(ve, ve.reciprocal(es, es))
            link(ve, ve.tensor_tensor(ew[:, :, :], ew[:, :, :],
                                      es.rearrange("p (t k) -> p t k", k=1).broadcast_to([P, NT, TOPK]), ALU.mult))
            link(ve, ve.tensor_tensor(ohw, oh, ew[:, :, :].rearrange("p t (k e) -> p t k e", e=1).broadcast_to(full), ALU.mult))
            ve.tensor_reduce(comb, ohw.rearrange("p t k e -> p t e k"), AX.X, ALU.add).then_inc(s_cb, 1)
            ve.wait_ge(s_cb, 1)
            ve.tensor_scalar(combs, comb, 1.0 / (SA * S2), None, ALU.mult).then_inc(s_cb, 1)
            ve.wait_ge(s_rp, 1)
            ve.wait_ge(s_cb, 1)
            link(ve, ve.tensor_copy(rank[:, :, :], bank[0][:, 0:NT * NE].rearrange("p (t e) -> p t e", t=NT)))
            link(ve, ve.tensor_tensor(ohw, oh, rank[:, :, :].rearrange("p t (k e) -> p t k e", k=1).broadcast_to(full), ALU.mult))
            link(ve, ve.tensor_reduce(rkk[:, :, :], ohw, AX.X, ALU.add))
            link(ve, ve.tensor_copy(rki[:, 0, :, :], rkk[:, :, :]))
            link(ve, ve.tensor_single_scalar(rki[:, 1, :, :], rki[:, 0, :, :], 7, ALU.logical_shift_right))
            link(ve, ve.tensor_copy(rkq[:, :, :], rki[:, 1, :, :]))
            link(ve, ve.scalar_tensor_tensor(out=rkr[:, :, :], in0=rkq[:, :, :], scalar=-128.0, in1=rkk[:, :, :],
                                             op0=ALU.mult, op1=ALU.add))
            link(ve, ve.scalar_tensor_tensor(out=rkq[:, :, :], in0=ixf[:, :, :], scalar=float(QT), in1=rkq[:, :, :],
                                             op0=ALU.mult, op1=ALU.add))
            def onehots(first, last):
                for n in range(first, last):
                    t, k = divmod(n, TOPK)
                    wait(ve, s_ohu, n - 7)
                    ve.tensor_scalar(Aoh[:, n % 8, :], iota256, rkq[:, t, k:k + 1], idv[:, t:t + 1], ALU.is_equal, ALU.mult)
                    ve.tensor_scalar(Boh[:, n % 8, :], iota256[:, 0:128], rkr[:, t, k:k + 1], None,
                                     ALU.is_equal).then_inc(s_oha, 1)

            def after(ins, first):
                ins.then_inc(s_dv, 1)
                chain["n"] += 1
                onehots(first, first + 4)
                ve.wait_ge(s_dv, chain["n"])
            after(ve.tensor_scalar(cnt[:, 0, :], bank[0][:, 256:256 + NE], 127.0, None, ALU.add), 0)
            after(ve.tensor_copy(cnt_i, cnt[:, 0, :]), 4)
            after(ve.tensor_single_scalar(cnt_i, cnt_i, 7, ALU.logical_shift_right), 8)
            after(ve.tensor_copy(cnt[:, 1, :], cnt_i), 12)
            after(ve.tensor_tensor_scan(cnt[:, 2, :], ones16[:, 0:NE], cnt[:, 1, :], 0.0, ALU.mult, ALU.add), 16)
            after(ve.tensor_scalar(cnt[:, 3, :], cnt[:, 2, :], pcol, None, ALU.is_le), 20)
            after(ve.tensor_reduce(tt_e[:, 0:1], cnt[:, 3, :], AX.X, ALU.add), 24)
            after(ve.tensor_tensor(cnt[:, 3, :], cnt[:, 3, :], cnt[:, 1, :], ALU.mult), 28)
            after(ve.tensor_reduce(tt_e[:, 1:2], cnt[:, 3, :], AX.X, ALU.add), 32)
            after(ve.tensor_tensor(tt_e[:, 1:2], pcol, tt_e[:, 1:2], ALU.subtract), 36)
            after(ve.scalar_tensor_tensor(out=tt_e[:, 2:3], in0=tt_e[:, 0:1], scalar=float(QT), in1=tt_e[:, 1:2],
                                          op0=ALU.mult, op1=ALU.add), 40)
            ve.tensor_scalar(tt_e[:, 2:3], tt_e[:, 2:3], float(NE * QT), None, ALU.min)
            ve.tensor_scalar(tt_e[:, 3:4], tt_e[:, 0:1], float(NE - 1), None, ALU.min).then_inc(s_tabt, 1)
            onehots(44, NT * TOPK - 8)
            ve.wait_ge(s_tabp, 1)
            ve.tensor_copy(tab[:, :], bank[2][0:1, 0:2 * P]).then_inc(s_dv, 1)
            chain["n"] += 1
            onehots(NT * TOPK - 8, NT * TOPK)
            ve.wait_ge(s_ohu, NT * TOPK)
            link(ve, ve.tensor_scalar(lpad, bank[1][:, 0:256], 0.0, pcol_pad, ALU.is_equal, ALU.mult))
            ve.scalar_tensor_tensor(out=Li[:, 0:256], in0=bank[1][:, 0:256], scalar=-1.0, in1=lpad,
                                    op0=ALU.add, op1=ALU.add)
            ve.wait_ge(s_dv, chain["n"])
            ve.tensor_scalar(Li[:, 256:257], pcol_pad, -1.0, None, ALU.add).then_inc(s_tab, 1)

            def gated(p, n):
                ve.wait_ge(s_l1, n)
                ve.tensor_scalar(lin[:, p, :], bank[2 + 2 * p][:, 0:HID], (LIMIT + 1) * S1, (1 - LIMIT) * S1,
                                 ALU.min, ALU.max).then_inc(s_lin, 1)
                ve.wait_ge(s_sg, n)
                ve.wait_ge(s_lin, n)
                ve.scalar_tensor_tensor(out=uu[:, p, :], in0=bank[1 + 2 * p][:, 0:HID], scalar=LIMIT * S1,
                                        in1=lin[:, p, :], op0=ALU.min, op1=ALU.mult).then_inc(s_u, 1)

            def times_sigmoid(p, n):
                ve.wait_ge(s_u, n)
                ve.scalar_tensor_tensor(out=av[:, p, :], in0=sg[:, p, :], scalar=SIGMAX, in1=uu[:, p, :],
                                        op0=ALU.min, op1=ALU.mult).then_inc(s_a, 1)

            def low_half(p, n):
                ve.wait_ge(s_ahi, n)
                ve.scalar_tensor_tensor(out=al[:, p, :], in0=bank[6][:, 0:HID], scalar=SA / (S1 * S1),
                                        in1=ah[:, p, :], op0=ALU.mult, op1=ALU.subtract).then_inc(s_alo, 1)
            gated(0, 1)
            times_sigmoid(0, 1)
            gated(1, 2)
            low_half(0, 1)
            times_sigmoid(1, 2)
            with ve.Fori(0, STEPS // RING) as i:
                for u in range(RING):
                    gated(u % 2, i * RING + (u + 3))
                    low_half((u + 1) % 2, i * RING + (u + 2))
                    times_sigmoid(u % 2, i * RING + (u + 3))

        @block.scalar
        def _(ac):
            for dst, src in ((W2T, w2t.rearrange("(h p) e -> p h e", p=96)), (W1T, w1t.rearrange("(h p) e -> p h e", p=96)),
                             (W0T, w0t), (P1, p1), (P2, p2), (BC[:, :], bcol), (WF0[:, :], wft[0:P, :]),
                             (WF1[:, :], wft[P:D + 1, :])):
                ac.dma_start(dst, src).then_inc(s_lw, 16)
            ac.wait_ge(s_sr, 1)

            def high_parts(e, k):
                ac.activation(W1s[:, e, 0, :], stA[k], ACT.Copy, scale=srow[:, 0:1])
                ac.activation(W1s[0:67, e, 2, :], stC[k], ACT.Copy, scale=srow[0:67, 2:3])
                ac.activation(W2s[:, e, 0, :], stD[k], ACT.Copy, scale=S2).then_inc(s_hi, 1)
            with ac.Fori(0, NE // STAGES) as i:
                for k in range(STAGES):
                    ac.wait_ge(s_st[k], i * 48 + 48)
                    ac.sem_inc(s_ah0, 1)
                    high_parts(bass.ds(i * STAGES + k, 1), k)
            for e in range(NE // STAGES * STAGES, NE):
                ac.wait_ge(s_st[e % STAGES], 48 * (e // STAGES + 1))
                high_parts(slice(e, e + 1), e % STAGES)
            ac.wait_ge(s_lo, NE)
            for b in range(NB):
                ac.wait_ge(s_h, b + 1)
                ac.activation(h_all[:, 2 * b:2 * b + 2, :], bank[4 + b % 4][:, 0:2 * D].rearrange("p (t n) -> p t n", t=2),
                              ACT.Copy).then_inc(s_he, 1)
            ac.wait_ge(s_ms, 4)

            def copy_hnT(b):
                p = b % 2
                ac.wait_ge(s_hnt, b + 1)
                wait(ac, s_q, b - 1)
                ac.activation(hnT[:, p, 0, :], bank[0][:, 0:256], ACT.Copy)
                ac.activation(hnT[0:D1, p, 1, :], bank[0][0:D1, 256:512], ACT.Copy).then_inc(s_hnte, 1)

            def kv_parts(b):
                p = b % 2
                wait(ac, s_phk, b)
                wait(ac, s_stt, b - 1)
                for j in range(2):
                    ac.wait_ge(s_kv, 2 * b + j + 1)
                    ac.activation(ek[:, j, :], bank[1 + j][:, 0:D], ACT.Exp)
                    ac.activation(rk[:, j, :], bank[1 + j][:, 0:D], ACT.Relu)
                    ac.activation(vx[:, p, j, 0:P], bank[1 + j][:, D:D + P], ACT.Copy)
                    ins = ac.activation(vx[:, p, j, P + 1:D + 1], bank[1 + j][:, D + P:2 * D], ACT.Copy)
                ins.then_inc(s_ke, 1)

            def q_parts(b):
                p = b % 2
                ac.wait_ge(s_q, b + 1)
                wait(ac, s_phq, b)
                for f, dst in ((ACT.Exp, eq), (ACT.Relu, rq)):
                    ac.activation(dst[:, 0, :], bank[3][:, 0:256], f)
                    ins = ac.activation(dst[0:D1, 1, :], bank[3][0:D1, 256:512], f)
                ins.then_inc(s_qe, 1)

            def copy_attT(b):
                p = b % 2
                ac.wait_ge(s_att_t, b + 1)
                wait(ac, s_o, b - 1)
                ac.activation(attT[:, p, 0, :], bank[6][:, 0:256], ACT.Copy)
                ac.activation(attT[0:D1, p, 1, :], bank[6][0:D1, 256:512], ACT.Copy).then_inc(s_att, 1)

            def high_rows(b):
                p = b % 2
                ac.wait_ge(s_tp, b + 1)
                wait(ac, s_rowd[p], 16 * (b // 2))
                ac.activation(rows[:, p, :, 0:D], tp[:, p, :, :], ACT.Copy).then_inc(s_th, 1)

            def copy_tpT(b):
                p = b % 2
                ac.wait_ge(s_tpt, b + 1)
                wait(ac, s_ga, b - 1)
                ac.activation(tpT[:, p, 0, :], bank[0][:, 0:256], ACT.Copy)
                ac.activation(tpT[0:D1, p, 1, :], bank[0][0:D1, 256:512], ACT.Copy).then_inc(s_tpte, 1)

            copy_hnT(0)
            kv_parts(0)
            for s in range(NB + 2):
                if s < NB:
                    q_parts(s)
                if s + 1 < NB:
                    copy_hnT(s + 1)
                if 0 <= s - 1 < NB:
                    copy_attT(s - 1)
                if 0 <= s - 2 < NB:
                    high_rows(s - 2)
                if s + 1 < NB:
                    kv_parts(s + 1)
                if 0 <= s - 2 < NB:
                    copy_tpT(s - 2)
            ac.wait_ge(s_nx, 1)
            ac.activation(ew[:, :, :], ew[:, :, :], ACT.Exp).then_inc(s_ex, 1)
            for k in range(4):
                ac.wait_ge(s_ct, k + 1)
                ac.activation(cT[:, k, :], bank[3][0:NE, :], ACT.Copy).then_inc(s_cte, 1)
            for b in range(NB):
                ac.wait_ge(s_b2, b + 1)
                ac.activation(h_all[:, 2 * b:2 * b + 2, :],
                              bank[4 + b % 2][:, 0:2 * D].rearrange("p (t n) -> p t n", t=2), ACT.Copy).then_inc(s_base, 1)

            ac.wait_ge(s_ms, 5)
            ac.sem_inc(s_y, 1)
            ac.sem_inc(s_clear, 2)

            def copy_tile(p, n):
                ac.wait_ge(s_tr, n)
                ac.activation(Ct[:, p, :, :], trs[p][:, 0:384].rearrange("p (c t) -> p c t", c=3), ACT.Copy)
                ac.activation(Cb[0:D1, p, :], trs[p][0:D1, 128:256], ACT.Copy).then_inc(s_tc, 1)

            def sigmoid(p, n):
                ac.wait_ge(s_l1, n)
                ac.activation(sg[:, p, :], bank[1 + 2 * p][:, 0:HID], ACT.Sigmoid, scale=ALPHA / S1).then_inc(s_sg, 1)

            def high_half(p, n):
                ac.wait_ge(s_at, n)
                ac.activation(ah[:, p, :], bank[6][:, 0:HID], ACT.Copy, scale=SA / (S1 * S1)).then_inc(s_ahi, 1)
            copy_tile(0, 1)
            copy_tile(1, 2)
            sigmoid(0, 1)
            sigmoid(1, 2)
            high_half(0, 1)
            copy_tile(0, 3)
            with ac.Fori(0, STEPS // RING) as i:
                for u in range(RING):
                    e = ac.value_load(tab[0:1, bass.ds(i * RING + (P + u), 1)], min_val=0, max_val=NE - 1)
                    sigmoid(u % 2, i * RING + (u + 3))
                    high_half((u + 1) % 2, i * RING + (u + 2))
                    copy_tile((u + 1) % 2, i * RING + (u + 4))
                    ac.wait_ge(s_l2, i * RING + (u + 1))
                    ac.sem_inc(s_ah0, 1)
                    ac.wait_ge(s_clear, i * RING + (u + 1))
                    ac.sem_inc(s_ah0, 1)
                    ac.activation(yv[:, u % 4, :], bank[5][:, 0:D], ACT.Copy,
                                  scale=Gr32[:, u, bass.ds(e + D, 1)]).then_inc(s_y, 1)

        @block.tensor
        def _(pe):
            mm = pe.matmul
            pe.wait_ge(s_c, NCONST)
            pe.wait_ge(s_lw, 16 * 8)
            pe.wait_ge(s_by, 1)
            for k in range(2):
                for j in range(4):
                    ins = pe.transpose(bank[k][0:96, P * j:P * (j + 1)], B2r[:, 4 * k + j, :], ident)
                ins.then_inc(s_x, 1)
            pe.wait_ge(s_xe, 2)
            for h in range(8):
                ins = mm(bank[2][:, 0:64], XT2[:, h, :, :], W2T[:, h, :], start=h == 0, stop=h == 7)
            ins.then_inc(s_x, 1)
            pe.wait_ge(s_by, 2)
            for k in range(2):
                for j in range(4):
                    ins = pe.transpose(bank[k][0:96, P * j:P * (j + 1)], B1r[:, 4 * k + j, :], ident)
                ins.then_inc(s_x, 1)
            pe.wait_ge(s_xe, 5)
            for b in range(4):
                for h in range(2):
                    ins = mm(bank[2][:, 64 * b:64 * (b + 1)], XT1[:, h, 2 * b:2 * b + 2, :], W1T[:, h, :],
                             start=h == 0, stop=h == 1)
            ins.then_inc(s_x, 1)
            for k in range(4):
                if k >= 2:
                    pe.wait_ge(s_xe, 7 + k - 2)
                g = slice(32 * k, 32 * k + 32)
                mm(bank[3 + k % 2][0:EMB, :], o2[g, :], P2[g, :], start=True, stop=True).then_inc(s_x, 1)
            pe.wait_ge(s_xe, 10)
            for k in range(4):
                if k >= 2:
                    pe.wait_ge(s_xe, 11 + k - 2)
                for j in range(2):
                    g = slice(64 * j, 64 * j + 64)
                    ins = mm(l1bank[k % 2][j][EMB:P, 0:256], o1[g, k, :], P1[g, :], start=True, stop=True)
                ins.then_inc(s_x, 1)
            n = 14
            pe.wait_ge(s_xe, 10)
            for k in range(2):
                pe.wait_ge(s_by, 3 + k)
                for q in range(2):
                    pe.wait_ge(s_xe, n - 3 if k else 10)
                    for j in range(4):
                        ins = pe.transpose(bank[q][0:48, P * j:P * (j + 1)], B0r[:, k, 4 * q + j, :], ident)
                    ins.then_inc(s_x, 1)
                    pe.wait_ge(s_xe, n + 1)
                    mm(bank[2 + q][0:EMB, :], W0T, X0T[:, q, :], start=True, stop=True).then_inc(s_x, 1)
                    n += 2
            pe.wait_ge(s_xe, 22)
            for b in range(NB):
                wait(pe, s_he, b - 3)
                for j in range(2):
                    t = slice(P * (2 * b + j), P * (2 * b + j + 1))
                    o = bank[4 + b % 4][:, D * j:D * (j + 1)]
                    mm(o, CT0[:, t], WF0[:, :], start=True, stop=False)
                    ins = mm(o, CT1[:, t], WF1[:, :], start=False, stop=True)
                ins.then_inc(s_h, 1)

            pe.wait_ge(s_aw, 16 * 9)
            pe.wait_ge(s_he, NB)
            pe.wait_ge(s_ms, 4)

            def transposes(src, b, s):
                p = b % 2
                for j in range(2):
                    pe.transpose(bank[0][:, P * j:P * (j + 1)], src[:, p, j, 0:P], ident)
                    ins = pe.transpose(bank[0][0:D1, 256 + P * j:256 + P * (j + 1)], src[:, p, j, P:D], ident)
                ins.then_inc(s, 1)

            def kv(b, j):
                p = b % 2
                pe.wait_ge(s_hnte, b + 1)
                wait(pe, s_ke, b)
                t = slice(P * j, P * (j + 1))
                mm(bank[1 + j][:, 0:2 * D], hnT[:, p, 0, t], WK[:, 0, :], start=True, stop=False)
                mm(bank[1 + j][:, 0:2 * D], hnT[0:D1, p, 1, t], WK[0:D1, 1, :], start=False, stop=True).then_inc(s_kv, 1)

            def query(b):
                p = b % 2
                wait(pe, s_qe, b)
                mm(bank[3][:, 0:256], WQ[:, 0, 0:P], hnT[:, p, 0, :], start=True, stop=False)
                mm(bank[3][:, 0:256], WQ[0:D1, 1, 0:P], hnT[0:D1, p, 1, :], start=False, stop=True)
                mm(bank[3][0:D1, 256:512], WQ[:, 0, P:D], hnT[:, p, 0, :], start=True, stop=False)
                mm(bank[3][0:D1, 256:512], WQ[0:D1, 1, P:D], hnT[0:D1, p, 1, :], start=False, stop=True).then_inc(s_q, 1)

            def state(b):
                p = b % 2
                pe.wait_ge(s_phk, b + 1)
                wait(pe, s_h2, b)
                for j in range(2):
                    mm(bank[4][:, 0:129], phk[:, p, j, 0:P], vx[:, p, j, 0:129], start=j == 0, stop=j == 1)
                for j in range(2):
                    ins = mm(bank[4][0:D1, 256:321], phk[:, p, j, P:D], vx[:, p, j, 129:194], start=j == 0, stop=j == 1)
                ins.then_inc(s_stt, 1)

            def num_den(b):
                p = b % 2
                pe.wait_ge(s_kvm, b + 1)
                pe.wait_ge(s_phq, b + 1)
                wait(pe, s_atr, b)
                for j in range(2):
                    t = slice(P * j, P * (j + 1))
                    o = NDW * j
                    m = P + NH0
                    mm(bank[5][:, o:o + m], phq[:, p, 0, t], kvm[:, p, 0, :], start=True, stop=True)
                    ins = mm(bank[5][:, o + m:o + NDW], phq[0:D1, p, 1, t], kvm[0:D1, p, 1, 0:NDW - m],
                             start=True, stop=True)
                ins.then_inc(s_nd, 1)

            def att_transposes(b):
                p = b % 2
                pe.wait_ge(s_atr, b + 1)
                wait(pe, s_att, b)
                for j in range(2):
                    pe.transpose(bank[6][:, P * j:P * (j + 1)], att[:, p, j, 0:P], ident)
                    ins = pe.transpose(bank[6][0:D1, 256 + P * j:256 + P * (j + 1)], att[:, p, j, P:D], ident)
                ins.then_inc(s_att_t, 1)

            def project(b):
                p = b % 2
                pe.wait_ge(s_att, b + 1)
                for j in range(2):
                    t = slice(P * j, P * (j + 1))
                    o = bank[4][:, D * j:D * (j + 1)]
                    mm(o, attT[:, p, 0, t], WO[:, 0, :], start=True, stop=False)
                    ins = mm(o, attT[0:D1 + 1, p, 1, t], WO[0:D1 + 1, 1, :], start=False, stop=True)
                ins.then_inc(s_o, 1)

            def gate(b):
                p = b % 2
                pe.wait_ge(s_tpte, b + 1)
                pe.wait_ge(s_gs, b + 1)
                for j in range(2):
                    t = slice(P * j, P * (j + 1))
                    o = bank[7][:, NE * j:NE * (j + 1)]
                    mm(o, tpT[:, p, 0, t], GS[:, 0, :], start=True, stop=False)
                    ins = mm(o, tpT[0:D1 + 1, p, 1, t], GS[0:D1 + 1, 1, :], start=False, stop=True)
                ins.then_inc(s_ga, 1)

            def keys(b):
                wait(pe, s_tpte, b - 3)
                pe.wait_ge(s_hn, b + 1)
                transposes(hn, b, s_hnt)
                kv(b, 0)
            keys(0)
            kv(0, 1)
            for s in range(NB + 3):
                if 0 <= s - 1 < NB:
                    state(s - 1)
                if s < NB:
                    query(s)
                if 0 <= s - 1 < NB:
                    num_den(s - 1)
                if s + 1 < NB:
                    keys(s + 1)
                if 0 <= s - 3 < NB:
                    gate(s - 3)
                if 0 <= s - 1 < NB:
                    att_transposes(s - 1)
                if s + 1 < NB:
                    kv(s + 1, 1)
                if 0 <= s - 1 < NB:
                    project(s - 1)
                if 0 <= s - 2 < NB:
                    pe.wait_ge(s_tp, s - 1)
                    pe.wait_ge(s_hnte, min(s + 2, NB))
                    transposes(tp, s - 2, s_tpt)

            pe.wait_ge(s_mr, 1)
            R0 = bank[0][:, 0:NT * NE]
            mm(R0, ustrict, Mx.rearrange("p t e -> p (t e)"), start=True, stop=False)
            for j in range(NT - 1):
                mm(bank[0][:, NE * (j + 1):NE * NT].rearrange("p (t e) -> p t e", e=NE), ones16,
                   Mx[:, j:j + 1, :].broadcast_to([P, NT - 1 - j, NE]), start=False, stop=j == NT - 2)
            for j in range(NT):
                ins = mm(bank[0][:, 256:256 + NE], ones16, Mx[:, j, :], start=j == 0, stop=j == NT - 1)
            ins.then_inc(s_rp, 1)
            pe.wait_ge(s_cb, 1)
            for k in range(4):
                wait(pe, s_cte, k)
                for j in range(4):
                    ins = pe.transpose(bank[3][0:NE, P * j:P * (j + 1)], comb[:, 4 * k + j, :], ident)
                ins.then_inc(s_ct, 1)
            def base(b):
                pe.wait_ge(s_cte, b // 2 + 1)
                pe.wait_ge(s_row, NB)
                wait(pe, s_base, b - 1)
                for j in range(2):
                    t = 2 * b + j
                    o = bank[4 + b % 2][:, D * j:D * (j + 1)]
                    mm(o, ident, h_all[:, t, :], start=True, stop=False)
                    ins = mm(o, cT[:, t // 4, P * (t % 4):P * (t % 4 + 1)], B2[:, :], start=False, stop=True)
                ins.then_inc(s_b2, 1)
            for n in range(NT * TOPK):
                if n % (NT * TOPK // NB) == 4:
                    base(n * NB // (NT * TOPK))
                if n == NT * TOPK - 12:
                    pe.wait_ge(s_tabt, 1)
                    for k in range(2):
                        ins = mm(bank[2][0:1, P * k:P * (k + 1)], tt_e[:, 2 + k:3 + k], ident, start=True, stop=True)
                    ins.then_inc(s_tabp, 1)
                pe.wait_ge(s_oha, n + 1)
                ins = mm(bank[1][:, 0:256], Boh[:, n % 8, :], Aoh[:, n % 8, :], start=n == 0, stop=n == NT * TOPK - 1)
                ins.then_inc(s_ohu, 1)
            pe.wait_ge(s_dup, 16)
            pe.wait_ge(s_tab, 1)
            pe.wait_ge(s_base, NB)

            def tile_transposes(slot, p, n):
                pe.wait_ge(s_gr[slot], n)
                for c in range(3):
                    ins = pe.transpose(trs[p][:, P * c:P * (c + 1)], Gr[:, slot, P * c:P * (c + 1)], ident16)
                ins.then_inc(s_tr, 1)

            def hidden(p, e):
                for m in range(2):
                    o = bank[1 + m + 2 * p][:, 0:HID]
                    c = slice(HID * m, HID * (m + 1))
                    mm(o, Ct[:, p, 0, :], W1s[:, e, 0, c], start=True, stop=False)
                    mm(o, Ct[:, p, 2, :], W1s[:, e, 0, c], start=False, stop=False)
                    mm(o, Ct[:, p, 0, :], W1s[:, e, 1, c], start=False, stop=False)
                    mm(o, Ct[:, p, 1, :], W1s[:, e, 2, c], start=False, stop=False)
                    ins = mm(o, Cb[0:67, p, :], W1s[0:67, e, 3, c], start=False, stop=True)
                ins.then_inc(s_l1, 1)

            def hidden_transposes(p):
                for m in range(HC):
                    ins = pe.transpose(bank[6][:, P * m:P * (m + 1)], av[:, p, P * m:P * (m + 1)], ident)
                ins.then_inc(s_at, 1)

            def down(p, e):
                k = 0
                for m in range(HC):
                    for a, w in ((ah, 0), (al, 0), (ah, 1)):
                        ins = mm(bank[5][:, 0:D], a[:, p, P * m:P * (m + 1)], W2s[:, e, w, D * m:D * (m + 1)],
                                 start=k == 0, stop=k == 3 * HC - 1)
                        k += 1
                ins.then_inc(s_l2, 1)

            def expert(at):
                return bass.ds(pe.value_load(tab[0:1, at], min_val=0, max_val=NE - 1), 1)
            tile_transposes(0, 0, 16)
            tile_transposes(1, 1, 16)
            for t in range(2):
                pe.wait_ge(s_tc, t + 1)
                hidden(t, expert(slice(P + t, P + t + 1)))
            pe.wait_ge(s_a, 1)
            hidden_transposes(0)
            tile_transposes(2, 0, 16)
            with pe.Fori(0, STEPS // RING) as i:
                for u in range(RING):
                    e2 = expert(bass.ds(i * RING + (P + u + 2), 1))
                    pe.wait_ge(s_tc, i * RING + (u + 3))
                    pe.sem_inc(s_hold, 1)
                    pe.wait_ge(s_u, i * RING + (u + 1))
                    pe.sem_inc(s_hold, 1)
                    hidden(u % 2, e2)
                    pe.wait_ge(s_a, i * RING + (u + 2))
                    pe.sem_inc(s_hold, 1)
                    pe.wait_ge(s_alo, i * RING + (u + 1))
                    hidden_transposes((u + 1) % 2)
                    v = (u + 3) % RING
                    tile_transposes(v, (u + 1) % 2, i * 16 + (16 if u + 3 < RING else 32))
                    e0 = expert(bass.ds(i * RING + (P + u), 1))
                    pe.wait_ge(s_y, i * RING + (u + 1))
                    down(u % 2, e0)



def kernel(x, L0_tok_W0, L0_tok_b0, L0_tok_W1, L0_tok_b1, L0_tok_W2, L0_tok_b2, L0_tok_Wf, L0_tok_bf,
           L0_tok_idx0, L0_tok_idx1, L0_tok_idx2, L0_attn_W_qkv, L0_attn_W_out, L0_attn_b_out, L0_ffn_norm_scale,
           L0_ffn_gate_w, L0_ffn_gate_b, L0_ffn_mlp1_w, L0_ffn_mlp1_b, L0_ffn_mlp2_w, L0_ffn_mlp2_b):
    import numpy as _np
    import concourse.bacc as _bacc
    from concourse import mybir as _mybir
    from concourse.bass_utils import run_bass_kernel_spmd as _run
    f32 = _np.float32
    A = _np.asarray
    x = A(x)
    x0 = x.transpose(2, 3, 0, 1).reshape(4096, 24)
    x1 = x.reshape(8, 3, 32, 2, 32, 2).transpose(2, 4, 0, 3, 5, 1).reshape(1024, 96)
    x2 = x.reshape(8, 3, 16, 4, 16, 4).transpose(2, 4, 0, 3, 5, 1).reshape(256, 384)
    i0 = A(L0_tok_idx0).reshape(2, 128, 16).transpose(1, 0, 2).reshape(128, 32)
    i1 = A(L0_tok_idx1).reshape(64, 2, 8).transpose(1, 0, 2).reshape(128, 8)
    i2 = A(L0_tok_idx2).reshape(16, 8, 2).transpose(1, 0, 2).reshape(128, 2)
    idx = _np.concatenate([i0, i1, i2], axis=1)
    wft = _np.concatenate([A(L0_tok_Wf).T, A(L0_tok_bf)[None]], axis=0)
    b0, b1_, b2_ = A(L0_tok_b0), A(L0_tok_b1), A(L0_tok_b2)
    bcol = _np.stack([_np.concatenate([b0, b1_]), _np.concatenate([b2_, b2_])], axis=1)
    wqkv = A(L0_attn_W_qkv)
    wo = _np.concatenate([A(L0_attn_W_out), A(L0_attn_b_out)[None]], axis=0)
    gw = _np.concatenate([A(L0_ffn_gate_w).T, A(L0_ffn_gate_b)[None]], axis=0)
    m1 = A(L0_ffn_mlp1_w).reshape(NE, HID, 2, D).transpose(0, 3, 2, 1).reshape(NE, D, 2 * HID)
    b1 = A(L0_ffn_mlp1_b).reshape(NE, HID, 2).transpose(0, 2, 1).reshape(NE, 2 * HID)
    m2 = A(L0_ffn_mlp2_w).reshape(NE, D, HC, P).transpose(0, 3, 2, 1).reshape(NE, P, HC * D)
    ns = A(L0_ffn_norm_scale)
    one = _np.zeros((3, P), f32)
    one[0, D1:D1 + 3] = 1
    one[1, D1 + 1] = 1
    tail = ns[P:D]
    sraw = _np.stack([ns[0:P], _np.concatenate([tail, one[0, D1:]]),
                      _np.concatenate([tail, one[1, D1:]])], axis=1)
    r = _np.arange(P)
    c32 = _np.zeros((P, 274 + NT), f32)
    c32[:, 0:128] = _np.eye(P)
    c32[:, 128:256] = (r[:, None] // HD) == (r[None, :] // HD)
    c32[:, 256:272] = _np.arange(NE)
    c32[:, 272] = r
    c32[:, 273] = ROWS + 1 + r
    c32[:, 274:] = r[:, None] + P * _np.arange(NT) + 1
    c16 = _np.zeros((P, 640), _np.float16)
    c16[:, 0:128] = _np.eye(P)
    c16[:, 128:256] = r[:, None] < r[None, :]
    c16[:, 256:384] = 1
    c16[:, 384:640] = _np.arange(256)
    pat = _np.zeros((NE, 1, 2 * HID), f32)
    pat[:, 0, HID:] = 1
    m1c = _np.concatenate([m1[:, P:D], b1[:, None], b1[:, None], pat], axis=1)

    def interpolation(n):
        pos = _np.clip((_np.arange(NTOK, dtype=f32) + f32(0.5)) * f32(n / NTOK) - f32(0.5), 0, n - 1)
        lo = _np.floor(pos).astype(_np.int32)
        hi = _np.minimum(lo + 1, n - 1)
        w = (pos - lo).astype(f32)
        m = _np.zeros((n, NTOK), f32)
        _np.add.at(m, (lo, _np.arange(NTOK)), 1 - w)
        _np.add.at(m, (hi, _np.arange(NTOK)), w)
        return m
    p1 = _np.tile(interpolation(64), (2, 1))
    m16 = interpolation(16)
    p2 = _np.zeros((P, 512), f32)
    for q in range(8):
        p2[16 * q:16 * q + 16, 256 * (q % 2):256 * (q % 2) + 256] = m16
    arrays = {"x0": x0, "x1": x1, "x2": x2, "idx": idx, "w0t": A(L0_tok_W0).T, "w1t": A(L0_tok_W1).T,
              "w2t": A(L0_tok_W2).T, "wft": wft, "bcol": bcol, "wq": wqkv[:, 0:D], "wk": wqkv[:, D:], "wo": wo,
              "gw": gw, "m1a": m1[:, 0:P], "m1c": m1c, "m2": m2, "b2": A(L0_ffn_mlp2_b),
              "sraw": sraw, "c32": c32, "c16": c16, "p1": p1, "p2": p2}
    arrays = {k: _np.ascontiguousarray(v) for k, v in arrays.items()}
    nc = _bacc.Bacc("TRN2", target_bir_lowering=False, num_devices=1)
    aps = {k: nc.dram_tensor(f"in_{k}", v.shape, _mybir.dt.from_np(v.dtype), kind="ExternalInput").ap()
           for k, v in arrays.items()}
    out = nc.dram_tensor("out", (ROWS + P, D), F32, kind="ExternalOutput").ap()
    build(nc, out=out, **aps)
    got = _run(nc, [{f"in_{k}": v for k, v in arrays.items()}], core_ids=[0])
    return got.results[0]["out"][0:ROWS].reshape(NB, NTOK, D)
```
